# Optimizing a Trainium2 kernel written in Bass

```python
import numpy as np
import jax
import jax.numpy as jnp

def _softmax(x, axis=-1):
    return jax.nn.softmax(x, axis=axis)

def _gelu(x):
    return jax.nn.gelu(x, approximate=True)

def _silu(x):
    return jax.nn.silu(x)

def _sigmoid(x):
    return jax.nn.sigmoid(x)

def _layernorm(x, axis=-1, eps=1e-05):
    m = jnp.mean(x, axis=axis, keepdims=True)
    v = jnp.var(x, axis=axis, keepdims=True)
    return (x - m) / jnp.sqrt(v + eps)

def _scatter_add(tgt, idx, src, axis=0):
    return tgt.at[idx].add(src)

def _segment_sum(src, seg, n):
    return jax.ops.segment_sum(src, seg, n)
kernel_name = 'mk_adaln_d1_jaxref_r4_faec64'

def setup_inputs(seed: int=0):
    np.random.seed(seed)
    _w = jnp.asarray

    def _L0_attn_setup():
        import jax, jax.numpy as jnp
        import numpy as np
        Q_H, KV_H, DIM = (32, 8, 1024)
        HEAD_DIM = DIM // Q_H
        FACTOR = Q_H // KV_H
        BS, SL = (2, 512)
        key = jax.random.key(seed)
        ks = jax.random.split(key, 9)
        s_in = 1.0 / np.sqrt(DIM)
        x = jax.random.normal(ks[0], (BS, SL, DIM), dtype=jnp.float32)
        wq_w = jax.random.uniform(ks[1], (DIM, Q_H * HEAD_DIM), jnp.float32, -s_in, s_in)
        wq_b = jax.random.uniform(ks[2], (Q_H * HEAD_DIM,), jnp.float32, -s_in, s_in)
        wk_w = jax.random.uniform(ks[3], (DIM, KV_H * HEAD_DIM), jnp.float32, -s_in, s_in)
        wk_b = jax.random.uniform(ks[4], (KV_H * HEAD_DIM,), jnp.float32, -s_in, s_in)
        wv_w = jax.random.uniform(ks[5], (DIM, KV_H * HEAD_DIM), jnp.float32, -s_in, s_in)
        wv_b = jax.random.uniform(ks[6], (KV_H * HEAD_DIM,), jnp.float32, -s_in, s_in)
        wo_w = jax.random.uniform(ks[7], (DIM, DIM), jnp.float32, -s_in, s_in)
        wo_b = jax.random.uniform(ks[8], (DIM,), jnp.float32, -s_in, s_in)
        return {'x': x, 'wq_w': wq_w, 'wq_b': wq_b, 'wk_w': wk_w, 'wk_b': wk_b, 'wv_w': wv_w, 'wv_b': wv_b, 'wo_w': wo_w, 'wo_b': wo_b}
    _L0_attn_in = _L0_attn_setup()

    def _L0_ffn_setup():
        import jax, jax.numpy as jnp
        import numpy as np
        LORA_SCALE = 16.0 / jnp.sqrt(16.0)
        TOP_K = 2
        key = jax.random.key(seed)
        k1, k2, k3, k4 = jax.random.split(key, 4)
        B_, S, D, O, E, R = (4, 512, 1024, 1024, 4, 16)
        x = jax.random.normal(k1, (B_, S, D), dtype=jnp.float32)
        router_w = jax.random.normal(k2, (E, D), dtype=jnp.float32) * 0.02
        A = jax.random.normal(k3, (E, R, D), dtype=jnp.float32) * 0.02
        B = jax.random.normal(k4, (O,), dtype=jnp.float32)
        B = jax.random.normal(k4, (E, O, R), dtype=jnp.float32) * 0.02
        return {'x': x, 'router_w': router_w, 'A': A, 'B': B}
    _L0_ffn_in = _L0_ffn_setup()
    _L0_c = _w((lambda *s: np.random.randn(*s).astype(np.float32) * 0.05)(4, 1024))
    _L0_wmod = _w((lambda *s: np.random.randn(*s).astype(np.float32) * 0.05)(1024, 6 * 1024) * 1024 ** (-0.5))
    _d = {'L0_attn_x': _L0_attn_in['x'], 'L0_attn_wq_w': _L0_attn_in['wq_w'], 'L0_attn_wq_b': _L0_attn_in['wq_b'], 'L0_attn_wk_w': _L0_attn_in['wk_w'], 'L0_attn_wk_b': _L0_attn_in['wk_b'], 'L0_attn_wv_w': _L0_attn_in['wv_w'], 'L0_attn_wv_b': _L0_attn_in['wv_b'], 'L0_attn_wo_w': _L0_attn_in['wo_w'], 'L0_attn_wo_b': _L0_attn_in['wo_b'], 'L0_ffn_router_w': _L0_ffn_in['router_w'], 'L0_ffn_A': _L0_ffn_in['A'], 'L0_ffn_B': _L0_ffn_in['B'], 'L0_c': _L0_c, 'L0_wmod': _L0_wmod}
    _x0 = _d['L0_attn_x']
    _d['L0_attn_x'] = jax.random.normal(jax.random.fold_in(jax.random.key(seed), 1), (4, 1024, 1024), dtype=_x0.dtype)
    del _x0
    return _d

def reference(L0_attn_x, L0_attn_wq_w, L0_attn_wq_b, L0_attn_wk_w, L0_attn_wk_b, L0_attn_wv_w, L0_attn_wv_b, L0_attn_wo_w, L0_attn_wo_b, L0_ffn_router_w, L0_ffn_A, L0_ffn_B, L0_c, L0_wmod):

    def _L0_attn_ref(x, wq_w, wq_b, wk_w, wk_b, wv_w, wv_b, wo_w, wo_b):
        import jax, jax.numpy as jnp
        import numpy as np
        Q_H, KV_H, DIM = (32, 8, 1024)
        HEAD_DIM = DIM // Q_H
        FACTOR = Q_H // KV_H
        BS, SL = (2, 512)
        bs, sl, _ = x.shape
        q = (x @ wq_w + wq_b).reshape(bs, sl, Q_H, HEAD_DIM)
        k = (x @ wk_w + wk_b).reshape(bs, sl, KV_H, HEAD_DIM)
        v = (x @ wv_w + wv_b).reshape(bs, sl, KV_H, HEAD_DIM)
        qg = q.reshape(bs, sl, KV_H, FACTOR, HEAD_DIM)
        scale = 1.0 / jnp.sqrt(jnp.asarray(HEAD_DIM, x.dtype))
        attn = jnp.einsum('bqhfd,bkhd->bhfqk', qg, k) * scale
        att = jax.nn.softmax(attn, axis=-1)
        a = jnp.einsum('bhfqk,bkhd->bqhfd', att, v)
        a = a.reshape(bs, sl, DIM)
        return a @ wo_w + wo_b

    def _L0_ffn_ref(x, router_w, A, B):
        import jax, jax.numpy as jnp
        import numpy as np
        LORA_SCALE = 16.0 / jnp.sqrt(16.0)
        TOP_K = 2
        D = x.shape[-1]
        flat = x.reshape(-1, D)
        logits = flat @ router_w.T
        topk_vals, topk_idx = jax.lax.top_k(logits, TOP_K)
        sparse = jnp.full_like(logits, -jnp.inf)
        rows = jnp.arange(logits.shape[0])[:, None]
        sparse = sparse.at[rows, topk_idx].set(topk_vals)
        gates = jax.nn.softmax(sparse, axis=-1)
        mid = jnp.einsum('tf,erf->ter', flat, A)
        all_deltas = jnp.einsum('ter,eor->teo', mid, B) * LORA_SCALE
        delta = jnp.einsum('te,teo->to', gates, all_deltas)
        return delta.reshape(*x.shape[:-1], -1)
    x = L0_attn_x
    mod = (_silu(L0_c) @ L0_wmod).reshape(L0_c.shape[0], 6, 1, -1)
    sa, ca, ga, sb, cb, gb = (mod[:, 0], mod[:, 1], mod[:, 2], mod[:, 3], mod[:, 4], mod[:, 5])
    ga = (2 * (ga >= 0) - 1) * jnp.maximum(jnp.abs(ga), 0.25)
    gb = (2 * (gb >= 0) - 1) * jnp.maximum(jnp.abs(gb), 0.25)
    h = _layernorm(x, axis=-1) * (1 + ca) + sa
    x = x + ga * _L0_attn_ref(h, L0_attn_wq_w, L0_attn_wq_b, L0_attn_wk_w, L0_attn_wk_b, L0_attn_wv_w, L0_attn_wv_b, L0_attn_wo_w, L0_attn_wo_b)
    h = _layernorm(x, axis=-1) * (1 + cb) + sb
    x = x + gb * _L0_ffn_ref(h, L0_ffn_router_w, L0_ffn_A, L0_ffn_B)
    return x

_drawn_inputs = setup_inputs


def setup_inputs(seed=0):
    import zlib

    import numpy as np

    out = dict(_drawn_inputs(seed))
    spreads = {}
    factors = {'L0_attn_wq_w': 8.0,
     'L0_attn_wq_b': 8.0,
     'L0_attn_wk_w': 8.0,
     'L0_attn_wk_b': 64.0,
     'L0_attn_wv_w': 8.0,
     'L0_attn_wv_b': 8.0,
     'L0_attn_wo_w': 8.0,
     'L0_attn_wo_b': 64.0,
     'L0_ffn_router_w': 8.0,
     'L0_ffn_A': 7.579,
     'L0_ffn_B': 7.582}
    for name, (base, spread) in spreads.items():
        noise = np.random.default_rng([zlib.crc32(name.encode()), seed]).standard_normal(out[name].shape)
        drawn = base * np.exp(spread * noise) if base else spread * noise
        out[name] = jnp.asarray(drawn.astype(out[name].dtype))
    for name, factor in factors.items():
        out[name] = (out[name] * factor).astype(out[name].dtype)
    return out
```

```python
from contextlib import ExitStack

import concourse.bass as bass
from concourse import mybir

ALU = mybir.AluOpType
ACT = mybir.ActivationFunctionType
F32 = mybir.dt.float32
F32R = mybir.dt.float32r
BF16 = mybir.dt.bfloat16
AX_X = mybir.AxisListType.X

P = 128
EPS = 1e-5
GATE_FLOOR = 0.25


def is_int(i, value):
    return isinstance(i, int) and i == value


def adaln_block(nc, x, w_q, w_k, w_v, w_o, b_q, b_k, b_v, b_o, lora_in, lora_out, c_t, w_mod, ident_in, earlier_in, out):
    NTOK, D = x.shape
    NB = c_t.shape[2]
    S = NTOK // NB
    KT = D // P
    NKV = w_k.shape[1]
    HD = 32
    REP = D // NKV
    G = NKV // HD
    E = 4
    R = lora_out.shape[0] // E
    BLK = 512
    NBLK = NTOK // BLK
    KVT = NKV // P
    assert S == 2 * BLK and REP * HD == P and KT == 8 and NBLK == 8 and G == 8

    NIT = NB * G
    q_hi_d = nc.dram_tensor("q_hi_d", (NIT, P, S), F32, kind="Internal").ap()
    q_lo_d = nc.dram_tensor("q_lo_d", (NIT, P, S), F32, kind="Internal").ap()
    k_hi_d = nc.dram_tensor("k_hi_d", (NIT * HD, S), F32, kind="Internal").ap()
    k_lo_d = nc.dram_tensor("k_lo_d", (NIT * HD, S), F32, kind="Internal").ap()
    v_d = nc.dram_tensor("v_d", (NIT, P, S // P, HD), F32, kind="Internal").ap()
    att_d = nc.dram_tensor("att_d", (NIT, P, S), F32, kind="Internal").ap()
    mod_raw_d = nc.dram_tensor("mod_raw_d", (4, NB, D), F32, kind="Internal").ap()
    mod_gate_d = nc.dram_tensor("mod_gate_d", (4, NB, D), F32, kind="Internal").ap()

    with ExitStack() as whole:
        def keep(name, shape, dt):
            return whole.enter_context(nc.sbuf_tensor(name, shape, dt))

        ident = keep("ident", [P, P], F32)
        project(nc, x, w_q, w_k, w_v, b_q, b_k, b_v, c_t, w_mod, ident_in, ident,
                q_hi_d, q_lo_d, k_hi_d, k_lo_d, v_d, mod_raw_d, mod_gate_d)
        wo_hi = keep("wo_hi", [P, KT, D], F32R)
        wo_lo = keep("wo_lo", [P, KT, D], F32R)
        attend(nc, w_o, ident, wo_hi, wo_lo, q_hi_d, q_lo_d, k_hi_d, k_lo_d, v_d, att_d)
        finish(nc, x, b_o, lora_in, lora_out, earlier_in, ident, wo_hi, wo_lo, att_d, mod_raw_d, mod_gate_d, out)


def project(nc, x, w_q, w_k, w_v, b_q, b_k, b_v, c_t, w_mod, ident_in, ident,
            q_hi_d, q_lo_d, k_hi_d, k_lo_d, v_d, mod_raw_d, mod_gate_d):
    NTOK, D = x.shape
    NB = c_t.shape[2]
    KT = D // P
    NKV = w_k.shape[1]
    KVT = NKV // P
    HD = 32
    G = NKV // HD
    NW = D + 2 * NKV
    BLK = 512
    HALF = 256
    HT = HALF // P
    QG, KG, VG = KT, KVT, BLK // P
    NG = QG + KG + VG
    QK = QG + KG
    SLOTS = 4
    MOD_CHUNKS = 2 * KT
    W_CHUNKS = 2 * KT
    OBANKS = 4
    NBLK = NTOK // BLK

    PREPARE = {-1: [("fetch", 0)], 0: [("stats", 0)], 1: [("norm", 0)], 2: [("turn", 0, 0), ("turn", 0, 1)],
               3: [("turn", 0, 2), ("turn", 0, 3)], 4: [("turn", 0, 4), ("turn", 0, 5)],
               5: [("turn", 0, 6), ("turn", 0, 7), ("fetch", 1)], 7: [("stats", 1)], 8: [("norm", 1)],
               9: [("turn", 1, 0), ("turn", 1, 1)], 10: [("turn", 1, 2), ("turn", 1, 3)],
               11: [("turn", 1, 4), ("turn", 1, 5)], 12: [("turn", 1, 6), ("turn", 1, 7)]}
    MODULATE = {-1: [("rows", 0)], 3: [("mod", 0), ("rows", 1)], 11: [("mod", 1)]}
    FIRST = [ev for hf in range(2) for ev in
             [("fetch", hf), ("stats", hf), ("norm", hf)] + [("turn", hf, kt) for kt in range(KT)]]

    def events(prepare, modulate):
        seen = []
        for g in range(-1, NG):
            if g >= 0:
                seen.append(("group", g))
            if modulate:
                seen += MODULATE.get(g, [])
            if prepare:
                seen += PREPARE.get(g, [])
        return seen

    def blocks(eng, do):
        do(0, 0, 0, events(True, True), 0)
        with eng.Fori(0, NBLK // 2 - 1) as n:
            do(n * 2 + 1, n, 1, events(True, False), None)
            do(n * 2 + 2, n + 1, 0, events(True, True), n + 1)
        do(NBLK - 1, NB - 1, 1, events(False, False), None)

    with ExitStack() as ctx:
        def sb(name, shape, dt):
            return ctx.enter_context(nc.sbuf_tensor(name, shape, dt))

        def sem(name):
            return ctx.enter_context(nc.semaphore(name))

        w_hi = sb("w_hi", [P, KT, NW], F32R)
        w_lo = sb("w_lo", [P, KT, NW], F32R)
        h_hi = sb("h_hi", [P, 2, KT, BLK], F32R)
        h_lo = sb("h_lo", [P, 2, KT, BLK], F32R)
        xn = sb("xn", [P, HT, D], F32)
        stage = sb("stage", [P, SLOTS, D], F32)
        h_f = sb("h_f", [P, 2, HALF], F32)
        o_f = sb("o_f", [P, 2, BLK], F32)
        o_hi = sb("o_hi", [P, 2, BLK], F32R)
        o_lo = sb("o_lo", [P, 2, BLK], F32R)
        v_f = sb("v_f", [P, 2, NKV], F32)
        cs = sb("cs", [P, KT, NB], F32)
        ce = sb("ce", [P, KT, NB], F32)
        cr = sb("cr", [P, KT, NB], F32)
        c_rep = sb("c_rep", [P, KT, 32], F32)
        shift = sb("shift", [P, KT, NB], F32)
        scale1 = sb("scale1", [P, KT, NB], F32)
        bias_qk = sb("bias_qk", [P, QK], F32)
        bias_v = sb("bias_v", [P, NKV], F32)
        stats = sb("stats", [P, HT, 2, 6], F32)
        mv = sb("mv", [P, HT, 2], F32)
        std = sb("std", [P, HT], F32)
        rstd = sb("rstd", [P, HT], F32)
        eps = sb("eps", [P, 1], F32)
        mrow = sb("mrow", [P, HALF], F32)
        mmax = sb("mmax", [P, HALF], F32)
        mmin = sb("mmin", [P, HALF], F32)
        mgate = sb("mgate", [P, HALF], F32)

        t_ps = ctx.enter_context(nc.psum_tensor("t_ps", [P, 2, 512], F32))
        o_ps = ctx.enter_context(nc.psum_tensor("o_ps", [P, OBANKS, 512], F32))
        m_ps = ctx.enter_context(nc.psum_tensor("m_ps", [P, 512], F32))

        small_in = sem("small_in")
        stage_in = [sem(f"stage_in{s}") for s in range(SLOTS)]
        stage_used = sem("stage_used")
        w_hi_done = sem("w_hi_done")
        w_lo_done = sem("w_lo_done")
        c_exp = sem("c_exp")
        c_step = sem("c_step")
        c_done = sem("c_done")
        x_in = sem("x_in")
        stats_done = sem("stats_done")
        std_done = sem("std_done")
        xn_ready = sem("xn_ready")
        waited = sem("waited")
        ln_step = sem("ln_step")
        turned = sem("turned")
        h_ready = sem("h_ready")
        h_hi_done = sem("h_hi_done")
        h_lo_done = sem("h_lo_done")
        o_ready = sem("o_ready")
        o_taken = sem("o_taken")
        o_hi_done = sem("o_hi_done")
        o_lo_done = sem("o_lo_done")
        qk_out = [sem(f"qk_out{s}") for s in range(2)]
        v_out = [sem(f"v_out{s}") for s in range(2)]
        row_ready = sem("row_ready")
        row_step = sem("row_step")
        row_out = sem("row_out")

        w_mod_t = w_mod.rearrange("(k p) n -> p k n", p=P)
        x_half = x.rearrange("(h t p) d -> h p t d", p=P, t=HT)

        with nc.Block() as block:

            @block.sync
            def _(sp):
                def fetch(half):
                    sp.wait_ge(turned, half * KT)
                    sp.dma_start(xn[:, :, :], x[bass.ds(half * HALF, HALF), :].rearrange("(t p) d -> p t d", p=P))\
                      .then_inc(x_in, 16)

                sp.dma_start(cs[:, :, :], c_t).then_inc(small_in, 16)
                sp.dma_start(ident[:, :], ident_in).then_inc(small_in, 16)
                sp.dma_start(bias_qk[:, 0:QG], b_q).then_inc(small_in, 16)
                sp.dma_start(bias_qk[:, QG:QK], b_k).then_inc(small_in, 16)
                sp.dma_start(bias_v[:, :], b_v.partition_broadcast(P)).then_inc(small_in, 16)
                fetch(0)
                for ch in range(MOD_CHUNKS):
                    if ch >= SLOTS:
                        sp.wait_ge(stage_used, ch - SLOTS + 1)
                    sp.dma_start(stage[:, ch % SLOTS, :].rearrange("p (k n) -> p k n", k=KT),
                                 w_mod_t[:, :, ch * P:(ch + 1) * P]).then_inc(stage_in[ch % SLOTS], 16)
                for ch in range(W_CHUNKS):
                    slot = ch % SLOTS
                    if ch < SLOTS:
                        sp.wait_ge(stage_used, MOD_CHUNKS - SLOTS + ch + 1)
                    else:
                        if ch == SLOTS:
                            fetch(1)
                        sp.wait_ge(w_lo_done, ch - SLOTS + 1)
                    rows = slice((ch // 2) * P, (ch // 2 + 1) * P)
                    if ch % 2 == 0:
                        sp.dma_start(stage[:, slot, :], w_q[rows, :]).then_inc(stage_in[slot], 16)
                    else:
                        sp.dma_start(stage[:, slot, 0:NKV], w_k[rows, :]).then_inc(stage_in[slot], 16)
                        sp.dma_start(stage[:, slot, NKV:2 * NKV], w_v[rows, :]).then_inc(stage_in[slot], 16)
                sp.wait_ge(w_lo_done, W_CHUNKS)

                def do(i, b, par, evs, vec):
                    cols = slice(par * BLK, (par + 1) * BLK)
                    for ev in evs:
                        if ev[0] == "fetch":
                            fetch(i * 2 + (2 + ev[1]))
                        elif ev[0] == "group" and ev[1] < QK:
                            g = ev[1]
                            if g < QG:
                                dst_hi = q_hi_d.rearrange("i p s -> (i p) s")
                                dst_lo = q_lo_d.rearrange("i p s -> (i p) s")
                                rows = bass.ds(b * (G * P) + g * P, P)
                            else:
                                dst_hi, dst_lo = k_hi_d, k_lo_d
                                rows = bass.ds(b * (G * HD) + (g - QG) * P, P)
                            sp.wait_ge(o_hi_done, i * QK + (g + 1))
                            sp.dma_start(dst_hi[rows, cols], o_hi[:, g % 2, :].bitcast(F32)).then_inc(qk_out[g % 2], 16)
                            sp.wait_ge(o_lo_done, i * QK + (g + 1))
                            sp.dma_start(dst_lo[rows, cols], o_lo[:, g % 2, :].bitcast(F32)).then_inc(qk_out[g % 2], 16)
                        elif ev[0] == "group":
                            v = ev[1] - QK
                            sp.wait_ge(o_taken, i * NG + (ev[1] + 1))
                            dst = v_d.rearrange("i p t c -> t p i c")[par * VG + v][:, bass.ds(b * G, G), :]
                            sp.dma_start(dst, v_f[:, v % 2, :].rearrange("p (i c) -> p i c", c=HD))\
                              .then_inc(v_out[v % 2], 16)
                        elif ev[0] == "rows":
                            sp.wait_ge(stage_used, vec * (2 * SLOTS) + (MOD_CHUNKS + ev[1] * SLOTS))
                            for s in range(SLOTS):
                                sp.dma_start(stage[:, s, :],
                                             w_mod_t[:, ev[1] * SLOTS + s, bass.ds(vec * D + 2 * D, D)])\
                                  .then_inc(stage_in[s], 16)
                        elif ev == ("mod", 1):
                            sp.wait_ge(row_ready, vec + 1)
                            for j in range(4):
                                src = slice(32 * j, 32 * j + 25, 8)
                                for d, t in ((mod_raw_d, mrow), (mod_gate_d, mgate)):
                                    dst = d.rearrange("v b n -> (v b) n")[bass.ds(vec * NB, NB),
                                                                          j * HALF:(j + 1) * HALF]
                                    sp.dma_start(dst, t[src, :]).then_inc(row_out, 16)

                blocks(sp, do)
                for s in range(2):
                    sp.wait_ge(qk_out[s], 32 * NBLK * QK // 2)
                    sp.wait_ge(v_out[s], 16 * NBLK * VG // 2)
                sp.wait_ge(row_out, 16 * 8 * NB)

            @block.scalar
            def _(act):
                act.wait_ge(small_in, 80)
                nc.scalar.activation(ce[:, :, :], cs[:, :, :], ACT.Exp, scale=-1.0).then_inc(c_exp, 1)
                count = [0] * SLOTS

                def weights():
                    for ch in range(W_CHUNKS):
                        slot, kt = ch % SLOTS, ch // 2
                        count[slot] += 16 if ch % 2 == 0 else 32
                        act.wait_ge(stage_in[slot], 16 * MOD_CHUNKS // SLOTS + count[slot])
                        cols = slice(0, D) if ch % 2 == 0 else slice(D, NW)
                        nc.scalar.copy(w_hi[:, kt, cols], stage[:, slot, 0:cols.stop - cols.start])\
                          .then_inc(w_hi_done, 1)

                def do(i, b, par, evs, vec):
                    for ev in evs:
                        if ev[0] == "stats":
                            half = i * 2 + (2 + ev[1])
                            act.wait_ge(stats_done, half + 1)
                            nc.scalar.activation(std[:, :], mv[:, :, 1], ACT.Sqrt, bias=eps[:, 0:1])\
                              .then_inc(std_done, 1)
                        elif ev[0] == "turn":
                            hf, kt = ev[1:]
                            tile = i * (2 * KT) + ((2 + hf) * KT + kt)
                            if kt == 0 and hf == 0 and not is_int(i, -1):
                                act.wait_ge(o_ready, i * NG)
                            act.wait_ge(h_ready, tile + 1)
                            nc.scalar.copy(h_hi[:, 1 - par, kt, hf * HALF:(hf + 1) * HALF], h_f[:, kt % 2, :])\
                              .then_inc(h_hi_done, 1)
                        elif ev[0] == "group" and ev[1] < QK:
                            g = ev[1]
                            act.wait_ge(o_taken, i * NG + (g + 1))
                            act.wait_ge(qk_out[g % 2], i * (32 * QK // 2) + 32 * (g // 2))
                            nc.scalar.copy(o_hi[:, g % 2, :], o_f[:, g % 2, :]).then_inc(o_hi_done, 1)

                do(-1, -1, 1, FIRST, None)
                weights()
                blocks(act, do)

            @block.gpsimd
            def _(pool):
                def weights():
                    for ch in range(W_CHUNKS):
                        slot, kt = ch % SLOTS, ch // 2
                        cols = slice(0, D) if ch % 2 == 0 else slice(D, NW)
                        pool.wait_ge(w_hi_done, ch + 1)
                        nc.gpsimd.tensor_tensor(w_lo[:, kt, cols], stage[:, slot, 0:cols.stop - cols.start],
                                                w_hi[:, kt, cols].bitcast(F32), ALU.subtract).then_inc(w_lo_done, 1)

                def do(i, b, par, evs, vec):
                    for ev in evs:
                        if ev[0] == "turn":
                            hf, kt = ev[1:]
                            tile = i * (2 * KT) + ((2 + hf) * KT + kt)
                            cols = slice(hf * HALF, (hf + 1) * HALF)
                            pool.wait_ge(h_hi_done, tile + 1)
                            nc.gpsimd.tensor_tensor(h_lo[:, 1 - par, kt, cols], h_f[:, kt % 2, :],
                                                    h_hi[:, 1 - par, kt, cols].bitcast(F32), ALU.subtract)\
                              .then_inc(h_lo_done, 1)
                        elif ev[0] == "group" and ev[1] < QK:
                            g = ev[1]
                            pool.wait_ge(o_hi_done, i * QK + (g + 1))
                            nc.gpsimd.tensor_tensor(o_lo[:, g % 2, :], o_f[:, g % 2, :],
                                                    o_hi[:, g % 2, :].bitcast(F32), ALU.subtract)\
                              .then_inc(o_lo_done, 1)

                do(-1, -1, 1, FIRST, None)
                weights()
                blocks(pool, do)

            @block.vector
            def _(dve):
                nc.vector.memset(eps[:, :], EPS)
                dve.wait_ge(c_exp, 1)
                nc.vector.tensor_scalar(cr[:, :, :], ce[:, :, :], 1.0, None, ALU.add).then_inc(c_step, 1)
                dve.wait_ge(c_step, 1)
                nc.vector.reciprocal(ce[:, :, :], cr[:, :, :]).then_inc(c_step, 1)
                dve.wait_ge(c_step, 2)
                nc.vector.tensor_tensor(cr[:, :, :], cs[:, :, :], ce[:, :, :], ALU.mult).then_inc(c_step, 1)
                dve.wait_ge(c_step, 3)
                nc.vector.tensor_copy(c_rep[:, :, :].rearrange("p k (b r) -> p k b r", b=NB),
                                      cr[:, :, :].unsqueeze(3).broadcast_to([P, KT, NB, 8])).then_inc(c_done, 1)

                def do(i, b, par, evs, vec):
                    for ev in evs:
                        if ev[0] == "stats":
                            half = i * 2 + (2 + ev[1])
                            dve.wait_ge(x_in, half * 16 + 16)
                            for t in range(HT):
                                for c in range(2):
                                    last = nc.vector.bn_stats(stats[:, t, c, :], xn[:, t, c * 512:(c + 1) * 512])
                            last.then_inc(ln_step, 1)
                            dve.wait_ge(ln_step, half * 2 + 1)
                            dve.sem_inc(waited, 1)
                            for t in range(HT):
                                last = nc.vector.bn_aggr(mv[:, t, :], stats[:, t, :, :].rearrange("p c s -> p (c s)"))
                            last.then_inc(stats_done, 1)
                        elif ev[0] == "norm":
                            half = i * 2 + (2 + ev[1])
                            dve.wait_ge(std_done, half + 1)
                            nc.vector.reciprocal(rstd[:, :], std[:, :]).then_inc(ln_step, 1)
                            dve.wait_ge(ln_step, half * 2 + 2)
                            for t in range(HT):
                                last = nc.vector.tensor_scalar(xn[:, t, :], xn[:, t, :], mv[:, t, 0:1],
                                                               rstd[:, t:t + 1], ALU.subtract, ALU.mult)
                            last.then_inc(xn_ready, 1)
                        elif ev[0] == "turn":
                            hf, kt = ev[1:]
                            tile = i * (2 * KT) + ((2 + hf) * KT + kt)
                            if is_int(i, -1) and hf == 0 and kt == 0:
                                dve.wait_ge(stage_used, MOD_CHUNKS)
                                m = m_ps[:, 0:2 * KT * NB].rearrange("p (v k b) -> p v k b", v=2, k=KT)
                                nc.vector.tensor_copy(shift[:, :, :], m[:, 0])
                                nc.vector.tensor_scalar(scale1[:, :, :], m[:, 1], 1.0, None, ALU.add)\
                                  .then_inc(c_step, 1)
                                dve.wait_ge(c_step, 4)
                            dve.wait_ge(turned, tile + 1)
                            if not (is_int(i, -1) and hf == 0 and kt < 2):
                                dve.wait_ge(h_lo_done, tile - 1)
                            at = b + par
                            nc.vector.tensor_scalar(h_f[:, kt % 2, :], t_ps[:, kt % 2, 0:HALF],
                                                    scale1[:, kt, bass.ds(at, 1)], shift[:, kt, bass.ds(at, 1)],
                                                    ALU.mult, ALU.add).then_inc(h_ready, 1)
                        elif ev[0] == "group":
                            g = ev[1]
                            dve.wait_ge(o_ready, i * NG + (g + 1))
                            bank = (par * NG + g) % OBANKS
                            if g < QK:
                                if not (is_int(i, 0) and g < 2):
                                    dve.wait_ge(o_lo_done, i * QK + (g - 1))
                                nc.vector.tensor_scalar(o_f[:, g % 2, :], o_ps[:, bank, :], bias_qk[:, g:g + 1],
                                                        None, ALU.add).then_inc(o_taken, 1)
                            else:
                                v = g - QK
                                dve.wait_ge(v_out[v % 2], i * (16 * VG // 2) + 16 * (v // 2))
                                nc.vector.tensor_tensor(v_f[:, v % 2, :], o_ps[:, bank, 0:NKV], bias_v[:, :],
                                                        ALU.add).then_inc(o_taken, 1)
                        elif ev == ("mod", 1):
                            dve.wait_ge(stage_used, vec * (2 * SLOTS) + (MOD_CHUNKS + 2 * SLOTS))
                            dve.wait_ge(row_out, vec * (16 * 8))
                            nc.vector.tensor_copy(mrow[:, :], m_ps[:, 0:HALF]).then_inc(row_step, 1)
                            dve.wait_ge(row_step, vec * 3 + 1)
                            nc.vector.tensor_scalar(mmax[:, :], mrow[:, :], GATE_FLOOR, None, ALU.max)
                            nc.vector.tensor_scalar(mmin[:, :], mrow[:, :], -GATE_FLOOR, None, ALU.min)\
                              .then_inc(row_step, 1)
                            dve.wait_ge(row_step, vec * 3 + 2)
                            nc.vector.scalar_tensor_tensor(mmax[:, :], mrow[:, :], 0.0, mmax[:, :], ALU.is_ge, ALU.mult)
                            nc.vector.scalar_tensor_tensor(mmin[:, :], mrow[:, :], 0.0, mmin[:, :], ALU.is_lt, ALU.mult)\
                              .then_inc(row_step, 1)
                            dve.wait_ge(row_step, vec * 3 + 3)
                            nc.vector.tensor_tensor(mgate[:, :], mmax[:, :], mmin[:, :], ALU.add).then_inc(row_ready, 1)

                do(-1, -1, 1, FIRST, None)
                blocks(dve, do)

            @block.tensor
            def _(pe):
                pe.wait_ge(c_done, 1)
                for ch in range(MOD_CHUNKS):
                    pe.wait_ge(stage_in[ch % SLOTS], 16 * (ch // SLOTS + 1))
                    w = stage[:, ch % SLOTS, :].rearrange("p (k n) -> p k n", k=KT)
                    for kt in range(KT):
                        last = nc.tensor.matmul(m_ps[:, ch * NB:(ch + 1) * NB], w[:, kt, :], cr[:, kt, :],
                                                start=(kt == 0), stop=(kt == KT - 1))
                    last.then_inc(stage_used, 1)

                def do(i, b, par, evs, vec):
                    for ev in evs:
                        if ev[0] == "turn":
                            hf, kt = ev[1:]
                            half = i * 2 + (2 + hf)
                            tile = i * (2 * KT) + ((2 + hf) * KT + kt)
                            pe.wait_ge(xn_ready, half + 1)
                            if not (is_int(i, -1) and hf == 0 and kt < 2):
                                pe.wait_ge(h_ready, tile - 1)
                            for t in range(HT):
                                last = nc.tensor.transpose(t_ps[:, kt % 2, t * P:(t + 1) * P],
                                                           xn[:, t, kt * P:(kt + 1) * P], ident[:, :])
                            last.then_inc(turned, 1)
                        elif ev[0] == "group":
                            g = ev[1]
                            if g == 0:
                                pe.wait_ge(h_lo_done, i * (2 * KT) + 2 * KT)
                            if not (is_int(i, 0) and g < OBANKS):
                                pe.wait_ge(o_taken, i * NG + (g - OBANKS + 1))
                            bank = (par * NG + g) % OBANKS
                            for kt in range(KT):
                                for n, (h, w) in enumerate(((h_hi, w_hi), (h_hi, w_lo), (h_lo, w_hi))):
                                    begin, end = kt == 0 and n == 0, kt == KT - 1 and n == 2
                                    if g < QK:
                                        last = nc.tensor.matmul(o_ps[:, bank, :], w[:, kt, g * P:(g + 1) * P],
                                                                h[:, par, kt, :], start=begin, stop=end)
                                    else:
                                        v = g - QK
                                        last = nc.tensor.matmul(o_ps[:, bank, 0:NKV],
                                                                h[:, par, kt, v * P:(v + 1) * P],
                                                                w[:, kt, D + NKV:NW], start=begin, stop=end)
                            last.then_inc(o_ready, 1)
                        elif ev[0] == "mod":
                            part = ev[1]
                            if part == 0 and not (is_int(vec, 0)):
                                pe.wait_ge(row_ready, vec)
                            for s in range(SLOTS):
                                pe.wait_ge(stage_in[s], vec * 32 + (stage_base[s] + 16 * (part + 1)))
                                for j in range(4):
                                    last = nc.tensor.matmul(m_ps[32 * j:32 * j + 32, 0:HALF],
                                                            c_rep[:, part * SLOTS + s, :],
                                                            stage[:, s, j * HALF:(j + 1) * HALF],
                                                            start=(part == 0 and s == 0),
                                                            stop=(part == 1 and s == SLOTS - 1))
                                last.then_inc(stage_used, 1)

                stage_base = [16 * MOD_CHUNKS // SLOTS + sum(16 if ch % 2 == 0 else 32 for ch in range(W_CHUNKS)
                                                             if ch % SLOTS == s) for s in range(SLOTS)]

                do(-1, -1, 1, FIRST, None)
                pe.wait_ge(w_lo_done, W_CHUNKS)
                blocks(pe, do)


def attend(nc, w_o, ident, wo_hi, wo_lo, q_hi_d, q_lo_d, k_hi_d, k_lo_d, v_d, att_d):
    NIT, _, S = q_hi_d.shape
    HD = 32
    REP = P // HD
    KT = w_o.shape[0] // P
    D = w_o.shape[1]
    SCALE = float(HD) ** -0.5
    QW = 512
    NQW = S // QW
    NKT = S // P
    STEPS = NQW * NKT
    TILES = STEPS * REP
    STACK = 3 * HD
    ROWS = STACK + 3
    PT = 4

    LATE = 3
    ring = []
    for j in range(REP):
        for t in range(NKT):
            if j and t == LATE:
                ring.append(("m", j - 1))
            ring.append(("s", j, t))
    ring.append(("m", REP - 1))
    NRING = len(ring)
    PLAN = {s: [] for s in range(STEPS)}
    per_step = [3, 3, 3, 3, 3, 4, 3, 3, 3, 3, 4]
    at = 0
    for s, n in enumerate(per_step):
        PLAN[s + 3] = list(range(at, at + n))
        at += n
    assert at == NRING - 1
    PLAN[STEPS - 1] = [NRING - 1]

    with ExitStack() as ctx:
        def sb(name, shape, dt):
            return ctx.enter_context(nc.sbuf_tensor(name, shape, dt))

        def ps(name, shape):
            return ctx.enter_context(nc.psum_tensor(name, shape, F32))

        def sem(name):
            return ctx.enter_context(nc.semaphore(name))

        q_st = sb("q_st", [ROWS, 2, REP, S], F32R)
        k_st = sb("k_st", [ROWS, 2, S], F32R)
        v_sb = sb("v_sb", [P, 2, NKT, HD], F32)
        p_t = sb("p_t", [P, PT, REP, QW], F32)
        ones = sb("ones", [P, HD], F32)
        ident_b = sb("ident_b", [P, P], BF16)
        mx = sb("mx", [P, 2, NKT], F32)
        rest1 = sb("rest1", [P, NKT], F32)
        rest2 = sb("rest2", [P, NKT], F32)
        m_parts = sb("m_parts", [P, 2, NKT, P], BF16)
        num_sb = sb("num_sb", [P, QW], F32)
        den_sb = sb("den_sb", [P, QW], F32)
        rden = sb("rden", [P, QW], F32)
        a_sb = sb("a_sb", [P, 2, QW], F32)
        wo_st = sb("wo_st", [P, 2, D], F32)

        st_ps = ps("st_ps", [P, 2, QW])
        s_ps = ps("s_ps", [P, 2, S])
        num_ps = ps("num_ps", [P, QW])
        den_ps = ps("den_ps", [P, QW])

        qk_in = [sem(f"qk_in{u}") for u in range(2)]
        v_in = [sem(f"v_in{u}") for u in range(2)]
        wo_in = [sem(f"wo_in{u}") for u in range(2)]
        wo_hi_done = sem("wo_hi_done")
        wo_lo_done = sem("wo_lo_done")
        consts = sem("consts")
        s_ready = sem("s_ready")
        max_done = sem("max_done")
        m_step = sem("m_step")
        m_made = sem("m_made")
        m_ready = sem("m_ready")
        m_put = sem("m_put")
        st_ready = sem("st_ready")
        exp_done = sem("exp_done")
        pv_done = sem("pv_done")
        num_taken = sem("num_taken")
        den_taken = sem("den_taken")
        rden_done = sem("rden_done")
        a_ready = sem("a_ready")
        a_out = [sem(f"a_out{u}") for u in range(2)]

        def iterations(eng, do):
            do(0, 0, True, True)
            do(1, 1, False, True)
            with eng.Fori(1, NIT // 2 - 1) as n:
                do(n * 2, 0, False, True)
                do(n * 2 + 1, 1, False, True)
            do(NIT - 2, 0, False, True)
            do(NIT - 1, 1, False, False)

        def s_count(r):
            return sum(e[0] == "s" for e in ring[:r])

        def m_count(r):
            return sum(e[0] == "m" for e in ring[:r])

        NS, NM = s_count(NRING), m_count(NRING)

        with nc.Block() as block:

            @block.sync
            def _(sp):
                def load_qk(it, u):
                    for row, src in ((0, q_hi_d), (1, q_lo_d), (2, q_hi_d)):
                        sp.dma_start(q_st[row * HD:(row + 1) * HD, u, :, :].bitcast(F32),
                                     src.rearrange("i (j d) s -> (i j) d s", d=HD)[bass.ds(it * REP, REP)]
                                     .rearrange("j d s -> d j s")).then_inc(qk_in[u], 16)
                    for row, src in ((0, k_hi_d), (1, k_hi_d), (2, k_lo_d)):
                        sp.dma_start(k_st[row * HD:(row + 1) * HD, u, :].bitcast(F32), src[bass.ds(it * HD, HD), :])\
                          .then_inc(qk_in[u], 16)

                def load_v(it, u):
                    sp.dma_start(v_sb[:, u, :, :], v_d.rearrange("i p t c -> (i p) t c")[bass.ds(it * P, P)])\
                      .then_inc(v_in[u], 16)

                def store(half, par, it):
                    sp.wait_ge(a_ready, half + 1)
                    sp.dma_start(att_d.rearrange("i p s -> (i p) s")[bass.ds(it * P, P), par * QW:(par + 1) * QW],
                                 a_sb[:, par, :]).then_inc(a_out[par], 16)

                load_qk(0, 0)
                load_v(0, 0)
                load_qk(1, 1)

                def do(it, u, first, more):
                    if not first:
                        store(it * 2 - 1, 1, it - 1)
                    if more:
                        if not first:
                            sp.wait_ge(pv_done, it * STEPS)
                        load_v(it + 1, 1 - u)
                    store(it * 2, 0, it)
                    if more and not is_int(it, NIT - 2):
                        sp.wait_ge(st_ready, it * TILES + TILES)
                        load_qk(it + 2, u)

                iterations(sp, do)
                store(2 * NIT - 1, 1, NIT - 1)
                for u in range(2):
                    sp.wait_ge(a_out[u], 16 * NIT)

            @block.gpsimd
            def _(pool):
                nc.gpsimd.memset(ones[:, :], 1.0)
                nc.gpsimd.memset(m_parts[:, :, :, :], 0.0)
                nc.gpsimd.tensor_copy(ident_b[:, :], ident[:, :]).then_inc(consts, 1)
                def split(n):
                    for u in range(2):
                        if not is_int(n, 0):
                            pool.wait_ge(wo_lo_done, n * 2)
                        pool.dma_start(wo_st[:, u, :], w_o[bass.ds(n * (2 * P) + u * P, P), :]).then_inc(wo_in[u], 16)
                    for u in range(2):
                        pool.wait_ge(wo_in[u], n * 16 + 16)
                        hi = wo_hi[:, bass.ds(n * 2 + u, 1), :].rearrange("p k n -> p (k n)")
                        lo = wo_lo[:, bass.ds(n * 2 + u, 1), :].rearrange("p k n -> p (k n)")
                        nc.gpsimd.tensor_copy(hi, wo_st[:, u, :]).then_inc(wo_hi_done, 1)
                        pool.wait_ge(wo_hi_done, n * 2 + (u + 1))
                        nc.gpsimd.tensor_tensor(lo, wo_st[:, u, :], hi.bitcast(F32), ALU.subtract)\
                          .then_inc(wo_lo_done, 1)

                split(0)
                with pool.Fori(1, KT // 2) as n:
                    split(n)

            @block.scalar
            def _(act):
                def put(it, u, r):
                    j = ring[r][1]
                    if j == 0 and not is_int(it, 0) and not is_int(it, 1):
                        act.wait_ge(st_ready, it * TILES - TILES)
                    act.wait_ge(m_ready, it * NM + (j + 1))
                    nc.scalar.copy(q_st[STACK:ROWS, u, j, :], s_ps[STACK:ROWS, r % 2, :]).then_inc(m_put, 1)

                for r in range(NRING):
                    if ring[r][0] == "m":
                        put(0, 0, r)

                def take_num(half):
                    act.wait_ge(pv_done, half * NKT + NKT)
                    if not is_int(half, 0):
                        act.wait_ge(a_ready, half)
                    nc.scalar.copy(num_sb[:, :], num_ps[:, :]).then_inc(num_taken, 1)

                def do(it, u, first, more):
                    for s in range(STEPS):
                        if s % NKT == 1 and not (first and s == 1):
                            take_num(it * 2 + (s // NKT - 1))
                        if not (first and s < PT):
                            act.wait_ge(pv_done, it * STEPS + (s - PT + 1))
                        for j in range(REP):
                            tile = it * TILES + (s * REP + j)
                            act.wait_ge(st_ready, tile + 1)
                            nc.scalar.activation(p_t[:, s % PT, j, :], st_ps[:, j % 2, :], ACT.Exp, scale=SCALE)\
                              .then_inc(exp_done, 1)
                        if more:
                            for r in PLAN[s]:
                                if ring[r][0] == "m":
                                    put(it + 1, 1 - u, r)

                iterations(act, do)
                take_num(2 * NIT - 1)

            @block.vector
            def _(dve):
                nc.vector.memset(k_st[STACK:ROWS, :, :].bitcast(F32), 1.0).then_inc(consts, 1)
                dve.wait_ge(consts, 2)

                def entry(it, u, r):
                    if ring[r][0] != "s":
                        return
                    j, t = ring[r][1:]
                    dve.wait_ge(s_ready, it * NS + (j * NKT + t + 1))
                    nc.vector.tensor_reduce(mx[:, j % 2, t:t + 1], s_ps[:, r % 2, :], AX_X, ALU.max)\
                      .then_inc(max_done, 1)
                    if t < NKT - 1:
                        return
                    dve.wait_ge(max_done, it * NS + (j * NKT + t + 1))
                    if not (is_int(it, 0) and j < 2):
                        dve.wait_ge(m_ready, it * NM + (j - 1))
                    part = [m_parts[:, j % 2, :, STACK + n] for n in range(3)]
                    base = it * (4 * REP) + 4 * j
                    nc.vector.tensor_scalar(part[0], mx[:, j % 2, :], -1.0, None, ALU.mult).then_inc(m_step, 1)
                    dve.wait_ge(m_step, base + 1)
                    nc.vector.scalar_tensor_tensor(rest1[:, :], mx[:, j % 2, :], -1.0, part[0], ALU.mult,
                                                   ALU.subtract).then_inc(m_step, 1)
                    dve.wait_ge(m_step, base + 2)
                    nc.vector.tensor_copy(part[1], rest1[:, :]).then_inc(m_step, 1)
                    dve.wait_ge(m_step, base + 3)
                    nc.vector.tensor_tensor(rest2[:, :], rest1[:, :], part[1], ALU.subtract).then_inc(m_step, 1)
                    dve.wait_ge(m_step, base + 4)
                    nc.vector.tensor_copy(part[2], rest2[:, :]).then_inc(m_made, 1)

                for r in range(NRING):
                    entry(0, 0, r)

                def divide(half, par):
                    dve.wait_ge(pv_done, half * NKT + NKT)
                    nc.vector.tensor_copy(den_sb[:, :], den_ps[:, :]).then_inc(den_taken, 1)
                    dve.wait_ge(den_taken, half + 1)
                    nc.vector.reciprocal(rden[:, :], den_sb[:, :]).then_inc(rden_done, 1)
                    dve.wait_ge(rden_done, half + 1)
                    dve.wait_ge(num_taken, half + 1)
                    if not (is_int(half, 0) or is_int(half, 1)):
                        dve.wait_ge(a_out[par], (half - par) * 8)
                    nc.vector.tensor_tensor(a_sb[:, par, :], num_sb[:, :], rden[:, :], ALU.mult).then_inc(a_ready, 1)

                def do(it, u, first, more):
                    for s in range(STEPS):
                        if s % NKT == 1 and not (first and s == 1):
                            divide(it * 2 + (s // NKT - 1), (s // NKT - 1) % 2)
                        if more:
                            for r in PLAN[s]:
                                entry(it + 1, 1 - u, r)

                iterations(dve, do)
                divide(2 * NIT - 1, 1)

            @block.tensor
            def _(pe):
                pe.wait_ge(consts, 2)

                def entry(it, u, r):
                    if r >= 2:
                        before = r - 2
                        kind, s_n, m_n = ring[before][0], s_count(before) + 1, m_count(before) + 1
                        if kind == "s":
                            pe.wait_ge(max_done, it * NS + s_n)
                        else:
                            pe.wait_ge(m_put, it * NM + m_n)
                    elif not is_int(it, 0):
                        if r == 0:
                            pe.wait_ge(max_done, it * NS)
                        else:
                            pe.wait_ge(m_put, it * NM)
                    if ring[r][0] == "s":
                        j, t = ring[r][1:]
                        if r == 0:
                            pe.wait_ge(qk_in[u], (it - u) * 48 + 96)
                        for n in range(NQW):
                            last = nc.tensor.matmul(s_ps[:, r % 2, n * QW:(n + 1) * QW],
                                                    q_st[0:STACK, u, j, t * P:(t + 1) * P],
                                                    k_st[0:STACK, u, n * QW:(n + 1) * QW], start=True, stop=True)
                        last.then_inc(s_ready, 1)
                    else:
                        j = ring[r][1]
                        pe.wait_ge(m_made, it * NM + (j + 1))
                        for t in range(NKT):
                            last = nc.tensor.matmul(s_ps[:, r % 2, t * P:(t + 1) * P], m_parts[:, j % 2, t, :],
                                                    ident_b[:, :], start=True, stop=True)
                        last.then_inc(m_ready, 1)

                for r in range(NRING):
                    entry(0, 0, r)

                def scores(it, u, s, j):
                    tile = it * TILES + (s * REP + j)
                    if not (is_int(it, 0) and s == 0 and j < 2):
                        pe.wait_ge(exp_done, tile - 1)
                    if s == 0:
                        pe.wait_ge(m_put, it * NM + (j + 1))
                    half, kt = s // NKT, s % NKT
                    nc.tensor.matmul(st_ps[:, j % 2, :], k_st[:, u, kt * P:(kt + 1) * P],
                                     q_st[:, u, j, half * QW:(half + 1) * QW], start=True, stop=True)\
                      .then_inc(st_ready, 1)

                def add(it, u, s, which):
                    kt = s % NKT
                    half = it * 2 + s // NKT
                    if which == "num":
                        pe.wait_ge(exp_done, it * TILES + (s * REP + REP))
                        if s == 0:
                            pe.wait_ge(v_in[u], (it - u) * 8 + 16)
                        if kt == 0 and not is_int(half, 0):
                            pe.wait_ge(num_taken, half)
                    elif kt == 0 and not is_int(half, 0):
                        pe.wait_ge(den_taken, half)
                    for j in range(REP):
                        rows = slice(j * HD, (j + 1) * HD)
                        lhs = v_sb[:, u, kt, :] if which == "num" else ones[:, :]
                        last = nc.tensor.matmul((num_ps if which == "num" else den_ps)[rows, :], lhs,
                                                p_t[:, s % PT, j, :], start=kt == 0, stop=kt == NKT - 1)
                    if which == "den":
                        last.then_inc(pv_done, 1)

                def do(it, u, first, more):
                    for s in range(STEPS):
                        plan = PLAN[s] if more else []
                        prev = (it, u, s - 1) if s else (it - 1, 1 - u, STEPS - 1)
                        scores(it, u, s, 0)
                        scores(it, u, s, 1)
                        if plan:
                            entry(it + 1, 1 - u, plan[0])
                        if not (first and s == 0):
                            add(*prev, "num")
                        if len(plan) > 3:
                            entry(it + 1, 1 - u, plan[3 - 2])
                        scores(it, u, s, 2)
                        scores(it, u, s, 3)
                        for r in plan[2 if len(plan) > 3 else 1:][:1]:
                            entry(it + 1, 1 - u, r)
                        if not (first and s == 0):
                            add(*prev, "den")
                        for r in plan[3 if len(plan) > 3 else 2:]:
                            entry(it + 1, 1 - u, r)

                iterations(pe, do)
                add(NIT - 1, 1, STEPS - 1, "num")
                add(NIT - 1, 1, STEPS - 1, "den")


def finish(nc, x, b_o, lora_in, lora_out, earlier_in, ident, wo_hi, wo_lo, att_d, mod_raw_d, mod_gate_d, out):
    NTOK, D = x.shape
    KT = D // P
    NB = mod_raw_d.shape[1]
    G = att_d.shape[0] // NB
    E = 4
    ER = lora_out.shape[0]
    R = ER // E
    LORA_SCALE = 4.0
    NT = NTOK // P
    TPB = NT // NB
    HW = 512
    XR = 8

    with ExitStack() as ctx:
        def sb(name, shape, dt):
            return ctx.enter_context(nc.sbuf_tensor(name, shape, dt))

        def ps(name, shape):
            return ctx.enter_context(nc.psum_tensor(name, shape, F32))

        def sem(name):
            return ctx.enter_context(nc.semaphore(name))

        ga = sb("ga", [P, NB, D], F32)
        up = sb("up", [ER, NB, D], F32)
        up_w = sb("up_w", [ER, D], F32)
        down = sb("down", [P, KT, P], F32)
        mod_rows = sb("mod_rows", [NB * KT, 2, P], F32)
        shift2 = sb("shift2", [P, NB, KT], F32)
        scale2 = sb("scale2", [P, NB, KT], F32)
        earlier = sb("earlier", [P, E, E], F32)
        bo_f = sb("bo_f", [1, D], F32)
        bo = sb("bo", [P, D], F32R)
        ones = sb("ones2", [P, P], F32R)
        eps = sb("eps2", [P, 1], F32)
        a_f = sb("a_f", [P, 2, KT, P], F32)
        a_hi = sb("a_hi", [P, 2, KT, P], F32R)
        a_lo = sb("a_lo", [P, 2, KT, P], F32R)
        x_sb = sb("x_sb", [P, 4, D], F32)
        x1 = sb("x1", [P, XR, D], F32)
        xn = sb("xn2", [P, D], F32)
        h_t = sb("h_t", [P, 2, KT, P], F32)
        stats = sb("stats2", [P, 2, 6], F32)
        mv = sb("mv2", [P, 2], F32)
        std = sb("std2", [P, 1], F32)
        rstd = sb("rstd2", [P, 1], F32)
        mid = sb("mid", [P, ER + E], F32)
        above = sb("above", [P, E, E], F32)
        tied = sb("tied", [P, E, E], F32)
        rank = sb("rank", [P, E], F32)
        top = sb("top", [P, 1], F32)
        low = sb("low", [P, E], F32)
        ex = sb("ex", [P, E], F32)
        wts = sb("wts", [P, E], F32)
        total = sb("total", [P, 1], F32)
        gate = sb("gate", [P, E], F32)
        gmid = sb("gmid", [P, ER], F32)
        gmid_t = sb("gmid_t", [ER, 2, P], F32)

        o_ps = ps("o2_ps", [P, 2, D])
        t_ps = ps("t2_ps", [P, D])
        g_ps = ps("g_ps", [P, 512])
        d_ps = ps("d_ps", [P, HW])
        MID_T = slice(P, 2 * P)

        tables_in = sem("tables_in")
        consts = sem("consts2")
        prep = sem("prep")
        mod_turned = sem("mod_turned")
        a_in = [sem(f"a_in{u}") for u in range(2)]
        x_in = [sem(f"x_in{u}") for u in range(4)]
        a_hi_done = sem("a_hi_done")
        a_lo_done = sem("a_lo_done")
        o_ready = sem("o2_ready")
        x1_ready = sem("x1_ready")
        ln_step = sem("ln2_step")
        var_done = sem("var_done")
        std_done = sem("std2_done")
        xn_ready = sem("xn2_ready")
        waited = sem("waited2")
        waited_pe = sem("waited_pe")
        turned = sem("turned2")
        h_ready = sem("h2_ready")
        mid_ready = sem("mid_ready")
        r_step = sem("r_step")
        low_ready = sem("low_ready")
        ex_done = sem("ex_done")
        gmid_ready = sem("gmid_ready")
        gmid_turned = sem("gmid_turned")
        gmid_taken = sem("gmid_taken")
        d_ready = sem("d_ready")
        y_ready = sem("y_ready")
        y_out = [sem(f"y_out{u}") for u in range(XR)]
        TABLES = 16 * (6 + 2 * NB)

        def slots(eng, do):
            for t in range(TPB):
                do(t, 0, t)
            with eng.Fori(1, NB) as b:
                for t in range(TPB):
                    do(b * TPB + t, b, t)
            for t in range(LAG):
                do(NT + t, NB, t)

        LAG = 4

        def tile_of(slot, b, t, lag):
            if isinstance(slot, int) and not 0 <= slot - lag < NT:
                return None
            return slot - lag, (b if t >= lag else b - 1), (t - lag) % TPB

        def batch(table, b):
            return table[:, bass.ds(b, 1), :].rearrange("p b n -> p (b n)")

        with nc.Block() as block:

            @block.sync
            def _(sp):
                sp.dma_start(bo_f[:, :], b_o).then_inc(tables_in, 16)
                sp.dma_start(down[:, :, :], lora_in).then_inc(tables_in, 16)
                for b in range(NB):
                    sp.dma_start(ga[:, b, :], mod_gate_d[0, b, :].partition_broadcast(P)).then_inc(tables_in, 16)
                sp.dma_start(earlier[:, :, :], earlier_in).then_inc(tables_in, 16)
                sp.dma_start(up_w[:, :], lora_out).then_inc(tables_in, 16)
                for b in range(NB):
                    sp.dma_start(up[:, b, :], mod_gate_d[3, b, :].partition_broadcast(ER)).then_inc(tables_in, 16)
                for v in range(2):
                    sp.dma_start(mod_rows[:, v, :], mod_raw_d[1 + v].rearrange("b (k p) -> (b k) p", p=P))\
                      .then_inc(tables_in, 16)

                def do(slot, b, t):
                    now = tile_of(slot, b, t, 0)
                    if now:
                        T, b, t = now
                        u = t % 2
                        if not (is_int(T, 0) or is_int(T, 1)):
                            sp.wait_ge(a_lo_done, T - 1)
                        src = att_d.rearrange("i p s -> (i p) s")[bass.ds(b * (G * P), G * P), t * P:(t + 1) * P]
                        sp.dma_start(a_f[:, u, :, :], src.rearrange("(k p) s -> p k s", p=P)).then_inc(a_in[u], 16)
                        if not (isinstance(T, int) and T < 4):
                            sp.wait_ge(x1_ready, T - 3)
                        sp.dma_start(x_sb[:, t % 4, :], x[bass.ds(T * P, P), :]).then_inc(x_in[t % 4], 16)

                def both(slot, b, t):
                    do(slot, b, t)
                    old = tile_of(slot, b, t, LAG)
                    if old:
                        T, _, t = old
                        sp.wait_ge(y_ready, T * 2 + 2)
                        sp.dma_start(out[bass.ds(T * P, P), :], x1[:, t % XR, :]).then_inc(y_out[t % XR], 16)

                slots(sp, both)
                for u in range(XR):
                    sp.wait_ge(y_out[u], 16 * NT // XR)

            @block.gpsimd
            def _(pool):
                def do(slot, b, t):
                    now = tile_of(slot, b, t, 0)
                    if now:
                        T, b, t = now
                        u = t % 2
                        pool.wait_ge(a_hi_done, T + 1)
                        nc.gpsimd.tensor_tensor(a_lo[:, u, :, :], a_f[:, u, :, :], a_hi[:, u, :, :].bitcast(F32),
                                                ALU.subtract).then_inc(a_lo_done, 1)

                slots(pool, do)

            @block.scalar
            def _(act):
                def do(slot, b, t):
                    now = tile_of(slot, b, t, 0)
                    if now:
                        T, _, tt = now
                        u = tt % 2
                        act.wait_ge(a_in[u], (T - u) * 8 + 16)
                        if not (is_int(T, 0) or is_int(T, 1)):
                            act.wait_ge(o_ready, T * 2 - 2)
                        nc.scalar.copy(a_hi[:, u, :, :], a_f[:, u, :, :]).then_inc(a_hi_done, 1)
                    now = tile_of(slot, b, t, 2)
                    if now:
                        act.wait_ge(var_done, now[0] + 1)
                        nc.scalar.activation(std[:, :], mv[:, 1:2], ACT.Sqrt, bias=eps[:, 0:1]).then_inc(std_done, 1)
                    now = tile_of(slot, b, t, 3)
                    if now:
                        act.wait_ge(low_ready, now[0] + 1)
                        nc.scalar.activation(ex[:, :], low[:, :], ACT.Exp).then_inc(ex_done, 1)
                    now = tile_of(slot, b, t, 2)
                    if now:
                        T, bb, tt = now
                        act.wait_ge(prep, 3)
                        act.wait_ge(turned, T + 1)
                        for kt in range(KT):
                            last = nc.scalar.activation(h_t[:, tt % 2, kt, :], t_ps[:, kt * P:(kt + 1) * P],
                                                        ACT.Identity, bias=batch(shift2, bb)[:, kt:kt + 1],
                                                        scale=batch(scale2, bb)[:, kt:kt + 1])
                        last.then_inc(h_ready, 1)
                    now = tile_of(slot, b, t, 3)
                    if now:
                        T, _, tt = now
                        act.wait_ge(gmid_turned, T + 1)
                        nc.scalar.copy(gmid_t[:, tt % 2, :], g_ps[0:ER, MID_T]).then_inc(gmid_taken, 1)

                act.wait_ge(consts, 1)
                act.wait_ge(prep, 3)
                slots(act, do)

            @block.vector
            def _(dve):
                nc.vector.memset(eps[:, :], EPS)
                nc.vector.memset(ones[:, :].bitcast(F32), 1.0)
                nc.vector.memset(bo[:, :].bitcast(F32), 0.0).then_inc(consts, 1)
                dve.wait_ge(consts, 1)
                dve.wait_ge(tables_in, TABLES)
                nc.vector.tensor_copy(bo[0:1, :], bo_f[:, :])
                nc.vector.scalar_tensor_tensor(up[:, :, :], up[:, :, :], LORA_SCALE,
                                               up_w[:, :].unsqueeze(1).broadcast_to([ER, NB, D]), ALU.mult, ALU.mult)
                dve.wait_ge(mod_turned, 1)
                nc.vector.tensor_copy(shift2[:, :, :].rearrange("p b k -> p (b k)"), t_ps[:, 0:NB * KT])
                nc.vector.tensor_scalar(scale2[:, :, :].rearrange("p b k -> p (b k)"), t_ps[:, P:P + NB * KT],
                                        1.0, None, ALU.add).then_inc(prep, 1)
                dve.wait_ge(prep, 1)
                nc.vector.tensor_tensor(bo[32:33, :], bo_f[:, :], bo[0:1, :].bitcast(F32), ALU.subtract)\
                  .then_inc(prep, 2)

                def do(slot, b, t):
                    now = tile_of(slot, b, t, 2)
                    if now:
                        T, bb, tt = now
                        xs = x1[:, tt % XR, :]
                        if not (isinstance(T, int) and T < XR):
                            dve.wait_ge(y_out[tt % XR], (T - tt) * (16 // XR))
                        dve.wait_ge(o_ready, T * 2 + 2)
                        nc.vector.tensor_tensor(xs, o_ps[:, tt % 2, :], batch(ga, bb), ALU.mult).then_inc(ln_step, 1)
                        dve.wait_ge(ln_step, T * 3 + 1)
                        dve.wait_ge(x_in[tt % 4], (T - tt % 4) * 4 + 16)
                        nc.vector.tensor_tensor(xs, xs, x_sb[:, tt % 4, :], ALU.add).then_inc(x1_ready, 1)
                        dve.wait_ge(x1_ready, T + 1)
                        for c in range(2):
                            last = nc.vector.bn_stats(stats[:, c, :], xs[:, c * HW:(c + 1) * HW])
                        last.then_inc(ln_step, 1)
                        dve.wait_ge(ln_step, T * 3 + 2)
                        dve.sem_inc(waited, 1)
                        nc.vector.bn_aggr(mv[:, :], stats[:, :, :].rearrange("p c s -> p (c s)")).then_inc(var_done, 1)
                        dve.wait_ge(std_done, T + 1)
                        nc.vector.reciprocal(rstd[:, :], std[:, :]).then_inc(ln_step, 1)
                        dve.wait_ge(ln_step, T * 3 + 3)
                        if not is_int(T, 0):
                            dve.wait_ge(turned, T)
                        nc.vector.tensor_scalar(xn[:, :], xs, mv[:, 0:1], rstd[:, :], ALU.subtract, ALU.mult)\
                          .then_inc(xn_ready, 1)
                    mids = tile_of(slot, b, t, 3)
                    if mids:
                        T = mids[0]
                        at = [0]

                        def step(ins):
                            at[0] += 1
                            ins.then_inc(r_step, 1)
                            dve.wait_ge(r_step, T * STEPS + at[0])

                        STEPS = 9
                        dve.wait_ge(mid_ready, T + 1)
                        step(nc.vector.tensor_copy(mid[:, :], g_ps[:, 0:ER + E]))
                        logit = mid[:, ER:ER + E]
                        rows = logit.unsqueeze(2).broadcast_to([P, E, E])
                        cols = logit.unsqueeze(1).broadcast_to([P, E, E])
                        nc.vector.tensor_tensor(above[:, :, :], cols, rows, ALU.is_gt)
                        nc.vector.tensor_tensor(tied[:, :, :], cols, rows, ALU.is_equal)
                        step(nc.vector.tensor_reduce(top[:, :], logit, AX_X, ALU.max))
                        nc.vector.tensor_scalar(low[:, :], logit, top[:, 0:1], None, ALU.subtract).then_inc(low_ready, 1)
                        step(nc.vector.tensor_tensor(tied[:, :, :], tied[:, :, :], earlier[:, :, :], ALU.mult))
                        step(nc.vector.tensor_tensor(above[:, :, :], above[:, :, :], tied[:, :, :], ALU.add))
                        step(nc.vector.tensor_reduce(rank[:, :], above[:, :, :], AX_X, ALU.add))
                    now = tile_of(slot, b, t, 4)
                    if now:
                        add(now, 0)
                    if mids:
                        dve.wait_ge(ex_done, T + 1)
                        step(nc.vector.scalar_tensor_tensor(wts[:, :], rank[:, :], 2.0, ex[:, :], ALU.is_lt, ALU.mult))
                        step(nc.vector.reduce_sum(total[:, :], wts[:, :], AX_X))
                        step(nc.vector.reciprocal(top[:, :], total[:, :]))
                        step(nc.vector.tensor_scalar(gate[:, :], wts[:, :], top[:, 0:1], None, ALU.mult))
                        assert at[0] == STEPS
                        if not is_int(T, 0):
                            dve.wait_ge(gmid_turned, T)
                        nc.vector.tensor_tensor(gmid[:, :].rearrange("p (e r) -> p e r", e=E),
                                                mid[:, 0:ER].rearrange("p (e r) -> p e r", e=E),
                                                gate[:, :].unsqueeze(2).broadcast_to([P, E, R]), ALU.mult)\
                          .then_inc(gmid_ready, 1)
                    if now:
                        add(now, 1)

                def add(now, half):
                    T, _, tt = now
                    cols = slice(half * HW, (half + 1) * HW)
                    dve.wait_ge(d_ready, T * 2 + (half + 1))
                    nc.vector.tensor_tensor(x1[:, tt % XR, cols], d_ps[:, :], x1[:, tt % XR, cols], ALU.add)\
                      .then_inc(y_ready, 1)

                slots(dve, do)

            @block.tensor
            def _(pe):
                pe.wait_ge(tables_in, TABLES)
                for v in range(2):
                    last = nc.tensor.transpose(t_ps[:, v * P:v * P + NB * KT], mod_rows[:, v, :],
                                               ident[0:NB * KT, 0:NB * KT])
                last.then_inc(mod_turned, 1)
                pe.wait_ge(prep, 3)

                def project_half(now, half):
                    T, _, tt = now
                    cols = slice(half * HW, (half + 1) * HW)
                    u = tt % 2
                    if half == 0:
                        pe.wait_ge(a_lo_done, T + 1)
                        if not (is_int(T, 0) or is_int(T, 1)):
                            pe.wait_ge(x1_ready, T - 1)
                    for k in range(KT):
                        for n, (a, w) in enumerate(((a_hi, wo_hi), (a_hi, wo_lo), (a_lo, wo_hi))):
                            nc.tensor.matmul(o_ps[:, u, cols], a[:, u, k, :], w[:, k, cols],
                                             start=(k == 0 and n == 0), stop=False)
                    nc.tensor.matmul(o_ps[:, u, cols], ones[:, :], bo[:, cols], start=False, stop=True)\
                      .then_inc(o_ready, 1)

                def experts_half(now, half):
                    T, bb, tt = now
                    if half == 0:
                        pe.wait_ge(gmid_taken, T + 1)
                    if not (is_int(T, 0) and half == 0):
                        pe.wait_ge(y_ready, T * 2 + half)
                    pe.sem_inc(waited_pe, 1)
                    nc.tensor.matmul(d_ps[:, :], gmid_t[:, tt % 2, :], batch(up, bb)[:, half * HW:(half + 1) * HW],
                                     start=True, stop=True).then_inc(d_ready, 1)

                def do(slot, b, t):
                    proj, turn, mids, add = (tile_of(slot, b, t, lag) for lag in (1, 2, 3, 4))
                    if proj:
                        project_half(proj, 0)
                    if mids:
                        T, _, tt = mids
                        pe.wait_ge(h_ready, T + 1)
                        if not is_int(T, 0):
                            pe.wait_ge(gmid_taken, T)
                        for k in range(KT):
                            last = nc.tensor.matmul(g_ps[:, 0:P], h_t[:, tt % 2, k, :], down[:, k, :],
                                                    start=k == 0, stop=k == KT - 1)
                        last.then_inc(mid_ready, 1)
                    if add:
                        experts_half(add, 0)
                    if proj:
                        project_half(proj, 1)
                    if turn:
                        T = turn[0]
                        pe.wait_ge(xn_ready, T + 1)
                        if not is_int(T, 0):
                            pe.wait_ge(h_ready, T)
                        for k in range(KT):
                            last = nc.tensor.transpose(t_ps[:, k * P:(k + 1) * P], xn[:, k * P:(k + 1) * P], ident[:, :])
                        last.then_inc(turned, 1)
                    if mids:
                        T = mids[0]
                        pe.wait_ge(prep, 3)
                        pe.wait_ge(gmid_ready, T + 1)
                        nc.tensor.transpose(g_ps[0:ER, MID_T], gmid[:, :], ident[:, :]).then_inc(gmid_turned, 1)
                    if add:
                        experts_half(add, 1)

                slots(pe, do)


def kernel(L0_attn_x, L0_attn_wq_w, L0_attn_wq_b, L0_attn_wk_w, L0_attn_wk_b, L0_attn_wv_w, L0_attn_wv_b,
           L0_attn_wo_w, L0_attn_wo_b, L0_ffn_router_w, L0_ffn_A, L0_ffn_B, L0_c, L0_wmod):
    import numpy as np
    import concourse.bacc as bacc
    from concourse.bass_utils import run_bass_kernel_spmd

    def tiles(a):
        return np.ascontiguousarray(a.reshape(-1, P, a.shape[-1]).transpose(1, 0, 2))

    x = np.asarray(L0_attn_x)
    bsz, s, d = x.shape
    lora_a, router, lora_b = np.asarray(L0_ffn_A), np.asarray(L0_ffn_router_w), np.asarray(L0_ffn_B)
    e, r, _ = lora_a.shape
    down = np.zeros((d, P), np.float32)
    down[:, :e * r] = lora_a.reshape(e * r, d).T
    down[:, e * r:e * r + e] = router.T
    arrays = {
        "x": np.ascontiguousarray(x.reshape(bsz * s, d)),
        "w_q": np.asarray(L0_attn_wq_w), "w_k": np.asarray(L0_attn_wk_w), "w_v": np.asarray(L0_attn_wv_w),
        "w_o": np.asarray(L0_attn_wo_w),
        "b_q": np.ascontiguousarray(np.asarray(L0_attn_wq_b).reshape(-1, P).T),
        "b_k": np.ascontiguousarray(np.asarray(L0_attn_wk_b).reshape(-1, P).T),
        "b_v": np.asarray(L0_attn_wv_b),
        "b_o": np.asarray(L0_attn_wo_b).reshape(1, d),
        "lora_in": tiles(down),
        "lora_out": np.ascontiguousarray(lora_b.transpose(0, 2, 1).reshape(e * r, d)),
        "c_t": tiles(np.asarray(L0_c).T),
        "w_mod": np.asarray(L0_wmod),
        "ident_in": np.eye(P, dtype=np.float32),
        "earlier_in": np.ascontiguousarray(np.broadcast_to(np.tril(np.ones((e, e), np.float32), -1), (P, e, e))),
    }
    nc = bacc.Bacc("TRN2", target_bir_lowering=False, num_devices=1)
    args = {n: nc.dram_tensor(n, a.shape, mybir.dt.from_np(a.dtype), kind="ExternalInput").ap()
            for n, a in arrays.items()}
    out = nc.dram_tensor("out", (bsz * s, d), F32, kind="ExternalOutput").ap()
    adaln_block(nc, **args, out=out)
    r = run_bass_kernel_spmd(nc, [arrays], core_ids=[0])
    return r.results[0]["out"].reshape(bsz, s, d)
```

```python
from contextlib import ExitStack

import concourse.bass as bass
from concourse import mybir

ALU = mybir.AluOpType
ACT = mybir.ActivationFunctionType
F32 = mybir.dt.float32
F32R = mybir.dt.float32r
BF16 = mybir.dt.bfloat16
AX_X = mybir.AxisListType.X

P = 128
EPS = 1e-5
GATE_FLOOR = 0.25


def is_int(i, value):
    return isinstance(i, int) and i == value


def adaln_block(nc, x, w_q, w_k, w_v, w_o, b_q, b_k, b_v, b_o, lora_in, lora_out, c_t, w_mod, ident_in, earlier_in, out):
    NTOK, D = x.shape
    NB = c_t.shape[2]
    S = NTOK // NB
    KT = D // P
    NKV = w_k.shape[1]
    HD = 32
    REP = D // NKV
    G = NKV // HD
    E = 4
    R = lora_out.shape[0] // E
    BLK = 512
    NBLK = NTOK // BLK
    KVT = NKV // P
    assert S == 2 * BLK and REP * HD == P and KT == 8 and NBLK == 8 and G == 8

    NIT = NB * G
    q_hi_d = nc.dram_tensor("q_hi_d", (NIT, P, S), F32, kind="Internal").ap()
    q_lo_d = nc.dram_tensor("q_lo_d", (NIT, P, S), F32, kind="Internal").ap()
    k_hi_d = nc.dram_tensor("k_hi_d", (NIT * HD, S), F32, kind="Internal").ap()
    k_lo_d = nc.dram_tensor("k_lo_d", (NIT * HD, S), F32, kind="Internal").ap()
    v_d = nc.dram_tensor("v_d", (NIT, P, S // P, HD), F32, kind="Internal").ap()
    att_d = nc.dram_tensor("att_d", (NIT, P, S), F32, kind="Internal").ap()
    mod_raw_d = nc.dram_tensor("mod_raw_d", (4, NB, D), F32, kind="Internal").ap()
    mod_gate_d = nc.dram_tensor("mod_gate_d", (4, NB, D), F32, kind="Internal").ap()

    with ExitStack() as whole:
        def keep(name, shape, dt):
            return whole.enter_context(nc.sbuf_tensor(name, shape, dt))

        ident = keep("ident", [P, P], F32)
        project(nc, x, w_q, w_k, w_v, b_q, b_k, b_v, c_t, w_mod, ident_in, ident,
                q_hi_d, q_lo_d, k_hi_d, k_lo_d, v_d, mod_raw_d, mod_gate_d)
        wo_hi = keep("wo_hi", [P, KT, D], F32R)
        wo_lo = keep("wo_lo", [P, KT, D], F32R)
        attend(nc, w_o, ident, wo_hi, wo_lo, q_hi_d, q_lo_d, k_hi_d, k_lo_d, v_d, att_d)
        finish(nc, x, b_o, lora_in, lora_out, earlier_in, ident, wo_hi, wo_lo, att_d, mod_raw_d, mod_gate_d, out)


def project(nc, x, w_q, w_k, w_v, b_q, b_k, b_v, c_t, w_mod, ident_in, ident,
            q_hi_d, q_lo_d, k_hi_d, k_lo_d, v_d, mod_raw_d, mod_gate_d):
    NTOK, D = x.shape
    NB = c_t.shape[2]
    KT = D // P
    NKV = w_k.shape[1]
    KVT = NKV // P
    HD = 32
    G = NKV // HD
    NW = D + 2 * NKV
    BLK = 512
    HALF = 256
    HT = HALF // P
    QG, KG, VG = KT, KVT, BLK // P
    NG = QG + KG + VG
    QK = QG + KG
    SLOTS = 4
    MOD_CHUNKS = 2 * KT
    W_CHUNKS = 2 * KT
    OBANKS = 4
    NBLK = NTOK // BLK

    PREPARE = {-1: [("fetch", 0)], 0: [("stats", 0)], 1: [("norm", 0)], 2: [("turn", 0, 0), ("turn", 0, 1)],
               3: [("turn", 0, 2), ("turn", 0, 3)], 4: [("turn", 0, 4), ("turn", 0, 5)],
               5: [("turn", 0, 6), ("turn", 0, 7), ("fetch", 1)], 7: [("stats", 1)], 8: [("norm", 1)],
               9: [("turn", 1, 0), ("turn", 1, 1)], 10: [("turn", 1, 2), ("turn", 1, 3)],
               11: [("turn", 1, 4), ("turn", 1, 5)], 12: [("turn", 1, 6), ("turn", 1, 7)]}
    MODULATE = {-1: [("rows", 0)], 3: [("mod", 0), ("rows", 1)], 11: [("mod", 1)]}
    FIRST = [ev for hf in range(2) for ev in
             [("fetch", hf), ("stats", hf), ("norm", hf)] + [("turn", hf, kt) for kt in range(KT)]]

    def events(prepare, modulate):
        seen = []
        for g in range(-1, NG):
            if g >= 0:
                seen.append(("group", g))
            if modulate:
                seen += MODULATE.get(g, [])
            if prepare:
                seen += PREPARE.get(g, [])
        return seen

    def blocks(eng, do):
        do(0, 0, 0, events(True, True), 0)
        with eng.Fori(0, NBLK // 2 - 1) as n:
            do(n * 2 + 1, n, 1, events(True, False), None)
            do(n * 2 + 2, n + 1, 0, events(True, True), n + 1)
        do(NBLK - 1, NB - 1, 1, events(False, False), None)

    with ExitStack() as ctx:
        def sb(name, shape, dt):
            return ctx.enter_context(nc.sbuf_tensor(name, shape, dt))

        def sem(name):
            return ctx.enter_context(nc.semaphore(name))

        w_hi = sb("w_hi", [P, KT, NW], F32R)
        w_lo = sb("w_lo", [P, KT, NW], F32R)
        h_hi = sb("h_hi", [P, 2, KT, BLK], F32R)
        h_lo = sb("h_lo", [P, 2, KT, BLK], F32R)
        xn = sb("xn", [P, HT, D], F32)
        stage = sb("stage", [P, SLOTS, D], F32)
        h_f = sb("h_f", [P, 2, HALF], F32)
        o_f = sb("o_f", [P, 2, BLK], F32)
        o_hi = sb("o_hi", [P, 2, BLK], F32R)
        o_lo = sb("o_lo", [P, 2, BLK], F32R)
        v_f = sb("v_f", [P, 2, NKV], F32)
        cs = sb("cs", [P, KT, NB], F32)
        ce = sb("ce", [P, KT, NB], F32)
        cr = sb("cr", [P, KT, NB], F32)
        c_rep = sb("c_rep", [P, KT, 32], F32)
        shift = sb("shift", [P, KT, NB], F32)
        scale1 = sb("scale1", [P, KT, NB], F32)
        bias_qk = sb("bias_qk", [P, QK], F32)
        bias_v = sb("bias_v", [P, NKV], F32)
        stats = sb("stats", [P, HT, 2, 6], F32)
        mv = sb("mv", [P, HT, 2], F32)
        std = sb("std", [P, HT], F32)
        rstd = sb("rstd", [P, HT], F32)
        eps = sb("eps", [P, 1], F32)
        mrow = sb("mrow", [P, HALF], F32)
        mmax = sb("mmax", [P, HALF], F32)
        mmin = sb("mmin", [P, HALF], F32)
        mgate = sb("mgate", [P, HALF], F32)

        t_ps = ctx.enter_context(nc.psum_tensor("t_ps", [P, 2, 512], F32))
        o_ps = ctx.enter_context(nc.psum_tensor("o_ps", [P, OBANKS, 512], F32))
        m_ps = ctx.enter_context(nc.psum_tensor("m_ps", [P, 512], F32))

        small_in = sem("small_in")
        stage_in = [sem(f"stage_in{s}") for s in range(SLOTS)]
        stage_used = sem("stage_used")
        w_hi_done = sem("w_hi_done")
        w_lo_done = sem("w_lo_done")
        c_exp = sem("c_exp")
        c_step = sem("c_step")
        c_done = sem("c_done")
        x_in = sem("x_in")
        stats_done = sem("stats_done")
        std_done = sem("std_done")
        xn_ready = sem("xn_ready")
        waited = sem("waited")
        ln_step = sem("ln_step")
        turned = sem("turned")
        h_ready = sem("h_ready")
        h_hi_done = sem("h_hi_done")
        h_lo_done = sem("h_lo_done")
        o_ready = sem("o_ready")
        o_taken = sem("o_taken")
        o_hi_done = sem("o_hi_done")
        o_lo_done = sem("o_lo_done")
        qk_out = [sem(f"qk_out{s}") for s in range(2)]
        v_out = [sem(f"v_out{s}") for s in range(2)]
        row_ready = sem("row_ready")
        row_step = sem("row_step")
        row_out = sem("row_out")

        w_mod_t = w_mod.rearrange("(k p) n -> p k n", p=P)
        x_half = x.rearrange("(h t p) d -> h p t d", p=P, t=HT)

        with nc.Block() as block:

            @block.sync
            def _(sp):
                def fetch(half):
                    sp.wait_ge(turned, half * KT)
                    sp.dma_start(xn[:, :, :], x[bass.ds(half * HALF, HALF), :].rearrange("(t p) d -> p t d", p=P))\
                      .then_inc(x_in, 16)

                sp.dma_start(cs[:, :, :], c_t).then_inc(small_in, 16)
                sp.dma_start(ident[:, :], ident_in).then_inc(small_in, 16)
                sp.dma_start(bias_qk[:, 0:QG], b_q).then_inc(small_in, 16)
                sp.dma_start(bias_qk[:, QG:QK], b_k).then_inc(small_in, 16)
                sp.dma_start(bias_v[:, :], b_v.partition_broadcast(P)).then_inc(small_in, 16)
                fetch(0)
                for ch in range(MOD_CHUNKS):
                    if ch >= SLOTS:
                        sp.wait_ge(stage_used, ch - SLOTS + 1)
                    sp.dma_start(stage[:, ch % SLOTS, :].rearrange("p (k n) -> p k n", k=KT),
                                 w_mod_t[:, :, ch * P:(ch + 1) * P]).then_inc(stage_in[ch % SLOTS], 16)
                for ch in range(W_CHUNKS):
                    slot = ch % SLOTS
                    if ch < SLOTS:
                        sp.wait_ge(stage_used, MOD_CHUNKS - SLOTS + ch + 1)
                    else:
                        if ch == SLOTS:
                            fetch(1)
                        sp.wait_ge(w_lo_done, ch - SLOTS + 1)
                    rows = slice((ch // 2) * P, (ch // 2 + 1) * P)
                    if ch % 2 == 0:
                        sp.dma_start(stage[:, slot, :], w_q[rows, :]).then_inc(stage_in[slot], 16)
                    else:
                        sp.dma_start(stage[:, slot, 0:NKV], w_k[rows, :]).then_inc(stage_in[slot], 16)
                        sp.dma_start(stage[:, slot, NKV:2 * NKV], w_v[rows, :]).then_inc(stage_in[slot], 16)
                sp.wait_ge(w_lo_done, W_CHUNKS)

                def do(i, b, par, evs, vec):
                    cols = slice(par * BLK, (par + 1) * BLK)
                    for ev in evs:
                        if ev[0] == "fetch":
                            fetch(i * 2 + (2 + ev[1]))
                        elif ev[0] == "group" and ev[1] < QK:
                            g = ev[1]
                            if g < QG:
                                dst_hi = q_hi_d.rearrange("i p s -> (i p) s")
                                dst_lo = q_lo_d.rearrange("i p s -> (i p) s")
                                rows = bass.ds(b * (G * P) + g * P, P)
                            else:
                                dst_hi, dst_lo = k_hi_d, k_lo_d
                                rows = bass.ds(b * (G * HD) + (g - QG) * P, P)
                            sp.wait_ge(o_hi_done, i * QK + (g + 1))
                            sp.dma_start(dst_hi[rows, cols], o_hi[:, g % 2, :].bitcast(F32)).then_inc(qk_out[g % 2], 16)
                            sp.wait_ge(o_lo_done, i * QK + (g + 1))
                            sp.dma_start(dst_lo[rows, cols], o_lo[:, g % 2, :].bitcast(F32)).then_inc(qk_out[g % 2], 16)
                        elif ev[0] == "group":
                            v = ev[1] - QK
                            sp.wait_ge(o_taken, i * NG + (ev[1] + 1))
                            dst = v_d.rearrange("i p t c -> t p i c")[par * VG + v][:, bass.ds(b * G, G), :]
                            sp.dma_start(dst, v_f[:, v % 2, :].rearrange("p (i c) -> p i c", c=HD))\
                              .then_inc(v_out[v % 2], 16)
                        elif ev[0] == "rows":
                            sp.wait_ge(stage_used, vec * (2 * SLOTS) + (MOD_CHUNKS + ev[1] * SLOTS))
                            for s in range(SLOTS):
                                sp.dma_start(stage[:, s, :],
                                             w_mod_t[:, ev[1] * SLOTS + s, bass.ds(vec * D + 2 * D, D)])\
                                  .then_inc(stage_in[s], 16)
                        elif ev == ("mod", 1):
                            sp.wait_ge(row_ready, vec + 1)
                            for j in range(4):
                                src = slice(32 * j, 32 * j + 25, 8)
                                for d, t in ((mod_raw_d, mrow), (mod_gate_d, mgate)):
                                    dst = d.rearrange("v b n -> (v b) n")[bass.ds(vec * NB, NB),
                                                                          j * HALF:(j + 1) * HALF]
                                    sp.dma_start(dst, t[src, :]).then_inc(row_out, 16)

                blocks(sp, do)
                for s in range(2):
                    sp.wait_ge(qk_out[s], 32 * NBLK * QK // 2)
                    sp.wait_ge(v_out[s], 16 * NBLK * VG // 2)
                sp.wait_ge(row_out, 16 * 8 * NB)

            @block.scalar
            def _(act):
                act.wait_ge(small_in, 80)
                nc.scalar.activation(ce[:, :, :], cs[:, :, :], ACT.Exp, scale=-1.0).then_inc(c_exp, 1)
                count = [0] * SLOTS

                def weights():
                    for ch in range(W_CHUNKS):
                        slot, kt = ch % SLOTS, ch // 2
                        count[slot] += 16 if ch % 2 == 0 else 32
                        act.wait_ge(stage_in[slot], 16 * MOD_CHUNKS // SLOTS + count[slot])
                        cols = slice(0, D) if ch % 2 == 0 else slice(D, NW)
                        nc.scalar.copy(w_hi[:, kt, cols], stage[:, slot, 0:cols.stop - cols.start])\
                          .then_inc(w_hi_done, 1)

                def do(i, b, par, evs, vec):
                    for ev in evs:
                        if ev[0] == "stats":
                            half = i * 2 + (2 + ev[1])
                            act.wait_ge(stats_done, half + 1)
                            nc.scalar.activation(std[:, :], mv[:, :, 1], ACT.Sqrt, bias=eps[:, 0:1])\
                              .then_inc(std_done, 1)
                        elif ev[0] == "turn":
                            hf, kt = ev[1:]
                            tile = i * (2 * KT) + ((2 + hf) * KT + kt)
                            if kt == 0 and hf == 0 and not is_int(i, -1):
                                act.wait_ge(o_ready, i * NG)
                            act.wait_ge(h_ready, tile + 1)
                            nc.scalar.copy(h_hi[:, 1 - par, kt, hf * HALF:(hf + 1) * HALF], h_f[:, kt % 2, :])\
                              .then_inc(h_hi_done, 1)
                        elif ev[0] == "group" and ev[1] < QK:
                            g = ev[1]
                            act.wait_ge(o_taken, i * NG + (g + 1))
                            act.wait_ge(qk_out[g % 2], i * (32 * QK // 2) + 32 * (g // 2))
                            nc.scalar.copy(o_hi[:, g % 2, :], o_f[:, g % 2, :]).then_inc(o_hi_done, 1)

                do(-1, -1, 1, FIRST, None)
                weights()
                blocks(act, do)

            @block.gpsimd
            def _(pool):
                def weights():
                    for ch in range(W_CHUNKS):
                        slot, kt = ch % SLOTS, ch // 2
                        cols = slice(0, D) if ch % 2 == 0 else slice(D, NW)
                        pool.wait_ge(w_hi_done, ch + 1)
                        nc.gpsimd.tensor_tensor(w_lo[:, kt, cols], stage[:, slot, 0:cols.stop - cols.start],
                                                w_hi[:, kt, cols].bitcast(F32), ALU.subtract).then_inc(w_lo_done, 1)

                def do(i, b, par, evs, vec):
                    for ev in evs:
                        if ev[0] == "turn":
                            hf, kt = ev[1:]
                            tile = i * (2 * KT) + ((2 + hf) * KT + kt)
                            cols = slice(hf * HALF, (hf + 1) * HALF)
                            pool.wait_ge(h_hi_done, tile + 1)
                            nc.gpsimd.tensor_tensor(h_lo[:, 1 - par, kt, cols], h_f[:, kt % 2, :],
                                                    h_hi[:, 1 - par, kt, cols].bitcast(F32), ALU.subtract)\
                              .then_inc(h_lo_done, 1)
                        elif ev[0] == "group" and ev[1] < QK:
                            g = ev[1]
                            pool.wait_ge(o_hi_done, i * QK + (g + 1))
                            nc.gpsimd.tensor_tensor(o_lo[:, g % 2, :], o_f[:, g % 2, :],
                                                    o_hi[:, g % 2, :].bitcast(F32), ALU.subtract)\
                              .then_inc(o_lo_done, 1)

                do(-1, -1, 1, FIRST, None)
                weights()
                blocks(pool, do)

            @block.vector
            def _(dve):
                nc.vector.memset(eps[:, :], EPS)
                dve.wait_ge(c_exp, 1)
                nc.vector.tensor_scalar(cr[:, :, :], ce[:, :, :], 1.0, None, ALU.add).then_inc(c_step, 1)
                dve.wait_ge(c_step, 1)
                nc.vector.reciprocal(ce[:, :, :], cr[:, :, :]).then_inc(c_step, 1)
                dve.wait_ge(c_step, 2)
                nc.vector.tensor_tensor(cr[:, :, :], cs[:, :, :], ce[:, :, :], ALU.mult).then_inc(c_step, 1)
                dve.wait_ge(c_step, 3)
                nc.vector.tensor_copy(c_rep[:, :, :].rearrange("p k (b r) -> p k b r", b=NB),
                                      cr[:, :, :].unsqueeze(3).broadcast_to([P, KT, NB, 8])).then_inc(c_done, 1)

                def do(i, b, par, evs, vec):
                    for ev in evs:
                        if ev[0] == "stats":
                            half = i * 2 + (2 + ev[1])
                            dve.wait_ge(x_in, half * 16 + 16)
                            for t in range(HT):
                                for c in range(2):
                                    last = nc.vector.bn_stats(stats[:, t, c, :], xn[:, t, c * 512:(c + 1) * 512])
                            last.then_inc(ln_step, 1)
                            dve.wait_ge(ln_step, half * 2 + 1)
                            dve.sem_inc(waited, 1)
                            for t in range(HT):
                                last = nc.vector.bn_aggr(mv[:, t, :], stats[:, t, :, :].rearrange("p c s -> p (c s)"))
                            last.then_inc(stats_done, 1)
                        elif ev[0] == "norm":
                            half = i * 2 + (2 + ev[1])
                            dve.wait_ge(std_done, half + 1)
                            nc.vector.reciprocal(rstd[:, :], std[:, :]).then_inc(ln_step, 1)
                            dve.wait_ge(ln_step, half * 2 + 2)
                            for t in range(HT):
                                last = nc.vector.tensor_scalar(xn[:, t, :], xn[:, t, :], mv[:, t, 0:1],
                                                               rstd[:, t:t + 1], ALU.subtract, ALU.mult)
                            last.then_inc(xn_ready, 1)
                        elif ev[0] == "turn":
                            hf, kt = ev[1:]
                            tile = i * (2 * KT) + ((2 + hf) * KT + kt)
                            if is_int(i, -1) and hf == 0 and kt == 0:
                                dve.wait_ge(stage_used, MOD_CHUNKS)
                                m = m_ps[:, 0:2 * KT * NB].rearrange("p (v k b) -> p v k b", v=2, k=KT)
                                nc.vector.tensor_copy(shift[:, :, :], m[:, 0])
                                nc.vector.tensor_scalar(scale1[:, :, :], m[:, 1], 1.0, None, ALU.add)\
                                  .then_inc(c_step, 1)
                                dve.wait_ge(c_step, 4)
                            dve.wait_ge(turned, tile + 1)
                            if not (is_int(i, -1) and hf == 0 and kt < 2):
                                dve.wait_ge(h_lo_done, tile - 1)
                            at = b + par
                            nc.vector.tensor_scalar(h_f[:, kt % 2, :], t_ps[:, kt % 2, 0:HALF],
                                                    scale1[:, kt, bass.ds(at, 1)], shift[:, kt, bass.ds(at, 1)],
                                                    ALU.mult, ALU.add).then_inc(h_ready, 1)
                        elif ev[0] == "group":
                            g = ev[1]
                            dve.wait_ge(o_ready, i * NG + (g + 1))
                            bank = (par * NG + g) % OBANKS
                            if g < QK:
                                if not (is_int(i, 0) and g < 2):
                                    dve.wait_ge(o_lo_done, i * QK + (g - 1))
                                nc.vector.tensor_scalar(o_f[:, g % 2, :], o_ps[:, bank, :], bias_qk[:, g:g + 1],
                                                        None, ALU.add).then_inc(o_taken, 1)
                            else:
                                v = g - QK
                                dve.wait_ge(v_out[v % 2], i * (16 * VG // 2) + 16 * (v // 2))
                                nc.vector.tensor_tensor(v_f[:, v % 2, :], o_ps[:, bank, 0:NKV], bias_v[:, :],
                                                        ALU.add).then_inc(o_taken, 1)
                        elif ev == ("mod", 1):
                            dve.wait_ge(stage_used, vec * (2 * SLOTS) + (MOD_CHUNKS + 2 * SLOTS))
                            dve.wait_ge(row_out, vec * (16 * 8))
                            nc.vector.tensor_copy(mrow[:, :], m_ps[:, 0:HALF]).then_inc(row_step, 1)
                            dve.wait_ge(row_step, vec * 3 + 1)
                            nc.vector.tensor_scalar(mmax[:, :], mrow[:, :], GATE_FLOOR, None, ALU.max)
                            nc.vector.tensor_scalar(mmin[:, :], mrow[:, :], -GATE_FLOOR, None, ALU.min)\
                              .then_inc(row_step, 1)
                            dve.wait_ge(row_step, vec * 3 + 2)
                            nc.vector.scalar_tensor_tensor(mmax[:, :], mrow[:, :], 0.0, mmax[:, :], ALU.is_ge, ALU.mult)
                            nc.vector.scalar_tensor_tensor(mmin[:, :], mrow[:, :], 0.0, mmin[:, :], ALU.is_lt, ALU.mult)\
                              .then_inc(row_step, 1)
                            dve.wait_ge(row_step, vec * 3 + 3)
                            nc.vector.tensor_tensor(mgate[:, :], mmax[:, :], mmin[:, :], ALU.add).then_inc(row_ready, 1)

                do(-1, -1, 1, FIRST, None)
                blocks(dve, do)

            @block.tensor
            def _(pe):
                pe.wait_ge(c_done, 1)
                for ch in range(MOD_CHUNKS):
                    pe.wait_ge(stage_in[ch % SLOTS], 16 * (ch // SLOTS + 1))
                    w = stage[:, ch % SLOTS, :].rearrange("p (k n) -> p k n", k=KT)
                    for kt in range(KT):
                        last = nc.tensor.matmul(m_ps[:, ch * NB:(ch + 1) * NB], w[:, kt, :], cr[:, kt, :],
                                                start=(kt == 0), stop=(kt == KT - 1))
                    last.then_inc(stage_used, 1)

                def do(i, b, par, evs, vec):
                    for ev in evs:
                        if ev[0] == "turn":
                            hf, kt = ev[1:]
                            half = i * 2 + (2 + hf)
                            tile = i * (2 * KT) + ((2 + hf) * KT + kt)
                            pe.wait_ge(xn_ready, half + 1)
                            if not (is_int(i, -1) and hf == 0 and kt < 2):
                                pe.wait_ge(h_ready, tile - 1)
                            for t in range(HT):
                                last = nc.tensor.transpose(t_ps[:, kt % 2, t * P:(t + 1) * P],
                                                           xn[:, t, kt * P:(kt + 1) * P], ident[:, :])
                            last.then_inc(turned, 1)
                        elif ev[0] == "group":
                            g = ev[1]
                            if g == 0:
                                pe.wait_ge(h_lo_done, i * (2 * KT) + 2 * KT)
                            if not (is_int(i, 0) and g < OBANKS):
                                pe.wait_ge(o_taken, i * NG + (g - OBANKS + 1))
                            bank = (par * NG + g) % OBANKS
                            for kt in range(KT):
                                for n, (h, w) in enumerate(((h_hi, w_hi), (h_hi, w_lo), (h_lo, w_hi))):
                                    begin, end = kt == 0 and n == 0, kt == KT - 1 and n == 2
                                    if g < QK:
                                        last = nc.tensor.matmul(o_ps[:, bank, :], w[:, kt, g * P:(g + 1) * P],
                                                                h[:, par, kt, :], start=begin, stop=end)
                                    else:
                                        v = g - QK
                                        last = nc.tensor.matmul(o_ps[:, bank, 0:NKV],
                                                                h[:, par, kt, v * P:(v + 1) * P],
                                                                w[:, kt, D + NKV:NW], start=begin, stop=end)
                            last.then_inc(o_ready, 1)
                        elif ev[0] == "mod":
                            part = ev[1]
                            if part == 0 and not (is_int(vec, 0)):
                                pe.wait_ge(row_ready, vec)
                            for s in range(SLOTS):
                                pe.wait_ge(stage_in[s], vec * 32 + (stage_base[s] + 16 * (part + 1)))
                                for j in range(4):
                                    last = nc.tensor.matmul(m_ps[32 * j:32 * j + 32, 0:HALF],
                                                            c_rep[:, part * SLOTS + s, :],
                                                            stage[:, s, j * HALF:(j + 1) * HALF],
                                                            start=(part == 0 and s == 0),
                                                            stop=(part == 1 and s == SLOTS - 1))
                                last.then_inc(stage_used, 1)

                stage_base = [16 * MOD_CHUNKS // SLOTS + sum(16 if ch % 2 == 0 else 32 for ch in range(W_CHUNKS)
                                                             if ch % SLOTS == s) for s in range(SLOTS)]

                do(-1, -1, 1, FIRST, None)
                pe.wait_ge(w_lo_done, W_CHUNKS)
                blocks(pe, do)


def attend(nc, w_o, ident, wo_hi, wo_lo, q_hi_d, q_lo_d, k_hi_d, k_lo_d, v_d, att_d):
    NIT, _, S = q_hi_d.shape
    HD = 32
    REP = P // HD
    KT = w_o.shape[0] // P
    D = w_o.shape[1]
    SCALE = float(HD) ** -0.5
    QW = 512
    NQW = S // QW
    HEADS = REP // NQW
    NPAIR = NIT * REP // HEADS
    NKT = S // P
    STEPS = NKT
    TILES = STEPS * REP
    STACK = 3 * HD
    ROWS = STACK + 3
    QR = 4
    SUMMED = 6
    SUMS = SUMMED - 1
    RAWS = NKT - SUMMED
    LATE_DEN = 3
    DIVIDE = 4
    PIECES = 4

    LATE = 3
    ring = []
    for jj in range(HEADS):
        for t in range(NKT):
            if t == LATE:
                ring.append(("m", jj - 1))
            ring.append(("s", jj, t))
    NRING = len(ring)
    NS = HEADS * NKT
    assert NRING % 2 == 0
    AHEAD = 8
    order = [(1, e) for e in range(AHEAD, NRING)] + [(2, e) for e in range(AHEAD)]
    per_step = [2, 2, 3, 2, 2, 2, 3, 2]
    PLAN, at = [], 0
    for n in per_step:
        PLAN.append(order[at:at + n])
        at += n
    assert at == NRING
    assert all(ring[e][0] == "s" for step in PLAN for _, e in step[1:])

    def exists(pair, e):
        if isinstance(pair, int):
            if ring[e] == ("m", -1):
                return 1 <= pair <= NPAIR
            return pair < NPAIR
        return True

    def s_index(e):
        return sum(x[0] == "s" for x in ring[:e + 1])

    def below(i, value):
        return isinstance(i, int) and i < value

    with ExitStack() as ctx:
        def sb(name, shape, dt):
            return ctx.enter_context(nc.sbuf_tensor(name, shape, dt))

        def ps(name, shape):
            return ctx.enter_context(nc.psum_tensor(name, shape, F32))

        def sem(name):
            return ctx.enter_context(nc.semaphore(name))

        q_st = sb("q_st", [ROWS, QR, HEADS, S], F32R)
        k_st = sb("k_st", [ROWS, 2, S], F32R)
        v_sb = sb("v_sb", [P, 2, NKT, HD], F32)
        p_t = sb("p_t", [P, NKT, REP, QW], F32)
        p_sum = sb("p_sum", [P, 2, REP, QW], F32)
        ones = sb("ones", [P, HD], F32)
        ident_b = sb("ident_b", [P, P], BF16)
        mx = sb("mx", [P, HEADS, NKT], F32)
        rest1 = sb("rest1", [P, NKT], F32)
        rest2 = sb("rest2", [P, NKT], F32)
        m_parts = sb("m_parts", [P, HEADS, NKT, P], BF16)
        num_sb = sb("num_sb", [P, QW], F32)
        den_t = sb("den_t", [P, QW // 32, 32], F32)
        rden_c = sb("rden_c", [P, QW // 32], F32)
        rden = sb("rden", [P, QW], F32)
        a_sb = sb("a_sb", [P, 2, QW], F32)
        wo_st = sb("wo_st", [P, D], F32)

        st_ps = ps("st_ps", [P, 2, QW])
        s_ps = ps("s_ps", [P, 2, S])
        num_ps = ps("num_ps", [P, QW])
        den_ps = ps("den_ps", [P, QW])

        q_in = [sem(f"q_in{u}") for u in range(QR)]
        k_in = [sem(f"k_in{u}") for u in range(2)]
        v_in = [sem(f"v_in{u}") for u in range(2)]
        wo_in = sem("wo_in")
        wo_hi_done = sem("wo_hi_done")
        wo_lo_done = sem("wo_lo_done")
        consts = sem("consts")
        s_ready = sem("s_ready")
        max_done = sem("max_done")
        m_step = sem("m_step")
        m_made = sem("m_made")
        m_ready = sem("m_ready")
        m_put = sem("m_put")
        st_ready = sem("st_ready")
        exp_done = sem("exp_done")
        num_done = sem("num_done")
        den_done = sem("den_done")
        sum_done = sem("sum_done")
        sum_used = sem("sum_used")
        num_taken = sem("num_taken")
        den_taken = sem("den_taken")
        rden_step = sem("rden_step")
        a_ready = sem("a_ready")
        a_out = [sem(f"a_out{u}") for u in range(2)]

        def pairs(eng, do):
            for pair in range(QR):
                do(pair, pair, pair // 2)
            with eng.Fori(1, NPAIR // QR - 1) as n:
                for slot in range(QR):
                    do(n * QR + slot, slot, n * 2 + slot // 2)
            for pair in range(NPAIR - QR, NPAIR):
                do(pair, pair % QR, pair // 2)

        def start(do):
            for e in range(NRING):
                do(0, 0, e)
            for e in range(AHEAD):
                do(1, 1, e)

        with nc.Block() as block:

            @block.sync
            def _(sp):
                def load_q(pair, slot):
                    for row, src in ((0, q_hi_d), (1, q_lo_d), (2, q_hi_d)):
                        sp.dma_start(q_st[row * HD:(row + 1) * HD, slot, :, :].bitcast(F32),
                                     src.rearrange("i (j d) s -> (i j) d s", d=HD)[bass.ds(pair * HEADS, HEADS)]
                                     .rearrange("j d s -> d j s")).then_inc(q_in[slot], 16)

                def load_k(it, u):
                    for row, src in ((0, k_hi_d), (1, k_hi_d), (2, k_lo_d)):
                        sp.dma_start(k_st[row * HD:(row + 1) * HD, u, :].bitcast(F32), src[bass.ds(it * HD, HD), :])\
                          .then_inc(k_in[u], 16)

                def load_v(it, u):
                    sp.dma_start(v_sb[:, u, :, :], v_d.rearrange("i p t c -> (i p) t c")[bass.ds(it * P, P)])\
                      .then_inc(v_in[u], 16)

                def store(pair, slot):
                    par = slot % 2
                    sp.wait_ge(a_ready, pair + 1)
                    for h in range(NQW):
                        sp.dma_start(att_d.rearrange("i p s -> (i p) s")[bass.ds(pair * (HEADS * HD), HEADS * HD),
                                                                         h * QW:(h + 1) * QW],
                                     a_sb[h * HEADS * HD:(h + 1) * HEADS * HD, par, :]).then_inc(a_out[par], 16)

                load_k(0, 0)
                load_q(0, 0)
                load_q(1, 1)
                load_v(0, 0)
                load_q(2, 2)

                def do(pair, slot, it):
                    u = slot // 2
                    if not below(pair, 1):
                        sp.wait_ge(st_ready, pair * TILES)
                    if slot % 2 == 0 and not is_int(it, NIT - 1):
                        load_k(it + 1, 1 - u)
                    if below(pair, NPAIR - QR + 1) or not isinstance(pair, int):
                        load_q(pair + (QR - 1), (slot + QR - 1) % QR)
                    if not below(pair, 1):
                        store(pair - 1, (slot - 1) % QR)
                    if slot % 2 == 1 and not is_int(it, NIT - 1):
                        if not below(pair, 2):
                            sp.wait_ge(num_done, (pair - 1) * STEPS)
                        load_v(it + 1, 1 - u)

                pairs(sp, do)
                store(NPAIR - 1, QR - 1)
                for u in range(2):
                    sp.wait_ge(a_out[u], 16 * NQW * NPAIR // 2)

            @block.gpsimd
            def _(pool):
                nc.gpsimd.memset(ones[:, :], 1.0)
                nc.gpsimd.memset(m_parts[:, :, :, :], 0.0)
                nc.gpsimd.tensor_copy(ident_b[:, :], ident[:, :]).then_inc(consts, 1)
                def split(n):
                    if not is_int(n, 0):
                        pool.wait_ge(wo_lo_done, n)
                    pool.dma_start(wo_st[:, :], w_o[bass.ds(n * P, P), :]).then_inc(wo_in, 16)
                    pool.wait_ge(wo_in, n * 16 + 16)
                    hi = wo_hi[:, bass.ds(n, 1), :].rearrange("p k n -> p (k n)")
                    lo = wo_lo[:, bass.ds(n, 1), :].rearrange("p k n -> p (k n)")
                    nc.gpsimd.tensor_copy(hi, wo_st[:, :]).then_inc(wo_hi_done, 1)
                    pool.wait_ge(wo_hi_done, n + 1)
                    nc.gpsimd.tensor_tensor(lo, wo_st[:, :], hi.bitcast(F32), ALU.subtract).then_inc(wo_lo_done, 1)

                split(0)
                with pool.Fori(1, KT) as n:
                    split(n)

                def do(pair, slot, it):
                    total = p_sum[:, slot % 2, :, :]
                    for kt in range(1, SUMMED):
                        pool.wait_ge(exp_done, pair * TILES + (kt * REP + REP))
                        if kt == 1:
                            if not below(pair, 2):
                                pool.wait_ge(sum_used, pair - 1)
                            before = p_t[:, 0, :, :]
                        else:
                            pool.wait_ge(sum_done, pair * SUMS + (kt - 1))
                            before = total
                        nc.gpsimd.tensor_tensor(total, before, p_t[:, kt, :, :], ALU.add).then_inc(sum_done, 1)

                pairs(pool, do)

            @block.scalar
            def _(act):
                def put(pair, slot, e):
                    if ring[e][0] != "m" or not exists(pair, e):
                        return
                    jj = ring[e][1]
                    if jj < 0:
                        pair, slot, jj = pair - 1, (slot - 1) % QR, HEADS - 1
                    if not below(pair, QR):
                        act.wait_ge(st_ready, (pair - (QR - 1)) * TILES)
                    act.wait_ge(m_ready, pair * HEADS + (jj + 1))
                    nc.scalar.copy(q_st[STACK:ROWS, slot, jj, :], s_ps[STACK:ROWS, e % 2, :]).then_inc(m_put, 1)

                start(put)

                def take_num(pair):
                    act.wait_ge(num_done, pair * STEPS + STEPS)
                    if not below(pair, 1):
                        act.wait_ge(a_ready, pair)
                    nc.scalar.copy(num_sb[:, :], num_ps[:, :]).then_inc(num_taken, 1)

                def do(pair, slot, it):
                    for s in range(STEPS):
                        if s == 1 and not below(pair, 1):
                            take_num(pair - 1)
                        if not below(pair, 1):
                            act.wait_ge(num_done, (pair - 1) * STEPS + (s + 1))
                            if s < SUMMED:
                                act.wait_ge(sum_done, (pair - 1) * SUMS + max(s, 1))
                            else:
                                act.wait_ge(den_done, (pair - 1) * RAWS + (s - SUMMED + 1))
                        for c in range(REP):
                            act.wait_ge(st_ready, pair * TILES + (s * REP + c + 1))
                            nc.scalar.activation(p_t[:, s, c, :], st_ps[:, c % 2, :], ACT.Exp, scale=SCALE)\
                              .then_inc(exp_done, 1)
                            if c == 1:
                                ahead, e = PLAN[s][0]
                                put(pair + ahead, (slot + ahead) % QR, e)

                pairs(act, do)
                take_num(NPAIR - 1)

            @block.vector
            def _(dve):
                nc.vector.memset(k_st[STACK:ROWS, :, :].bitcast(F32), 1.0).then_inc(consts, 1)
                dve.wait_ge(consts, 2)

                def entry(pair, slot, e):
                    if ring[e][0] != "s" or not exists(pair, e):
                        return
                    jj, t = ring[e][1:]
                    done = jj * NKT + t + 1
                    dve.wait_ge(s_ready, pair * NS + done)
                    nc.vector.tensor_reduce(mx[:, jj, t:t + 1], s_ps[:, e % 2, :], AX_X, ALU.max)\
                      .then_inc(max_done, 1)
                    if t < NKT - 1:
                        return
                    dve.wait_ge(max_done, pair * NS + done)
                    if not below(pair, 1):
                        dve.wait_ge(m_ready, (pair - 1) * HEADS + (jj + 1))
                    part = [m_parts[:, jj, :, STACK + n] for n in range(3)]
                    base = pair * (4 * HEADS) + 4 * jj
                    nc.vector.tensor_scalar(part[0], mx[:, jj, :], -1.0, None, ALU.mult).then_inc(m_step, 1)
                    dve.wait_ge(m_step, base + 1)
                    nc.vector.scalar_tensor_tensor(rest1[:, :], mx[:, jj, :], -1.0, part[0], ALU.mult,
                                                   ALU.subtract).then_inc(m_step, 1)
                    dve.wait_ge(m_step, base + 2)
                    nc.vector.tensor_copy(part[1], rest1[:, :]).then_inc(m_step, 1)
                    dve.wait_ge(m_step, base + 3)
                    nc.vector.tensor_tensor(rest2[:, :], rest1[:, :], part[1], ALU.subtract).then_inc(m_step, 1)
                    dve.wait_ge(m_step, base + 4)
                    nc.vector.tensor_copy(part[2], rest2[:, :]).then_inc(m_made, 1)

                start(entry)

                def divide(pair, par, piece):
                    if piece == 0:
                        dve.wait_ge(sum_used, pair + 1)
                        nc.vector.transpose(den_t[:, :, :].rearrange("p c r -> p (c r)"), den_ps[:, :])\
                          .then_inc(den_taken, 1)
                    elif piece == 1:
                        dve.wait_ge(den_taken, pair + 1)
                        nc.vector.reciprocal(rden_c[:, :], den_t[:, :, 0]).then_inc(rden_step, 1)
                    elif piece == 2:
                        dve.wait_ge(rden_step, pair * 2 + 1)
                        nc.vector.transpose(rden[:, :], rden_c[:, :].unsqueeze(2).broadcast_to([P, QW // 32, 32]))\
                          .then_inc(rden_step, 1)
                    else:
                        dve.wait_ge(rden_step, pair * 2 + 2)
                        dve.wait_ge(num_taken, pair + 1)
                        if not below(pair, 2):
                            dve.wait_ge(a_out[par], (pair - par) * (8 * NQW))
                        nc.vector.tensor_tensor(a_sb[:, par, :], num_sb[:, :], rden[:, :], ALU.mult)\
                          .then_inc(a_ready, 1)

                def do(pair, slot, it):
                    for s in range(STEPS):
                        if s >= DIVIDE and not below(pair, 1):
                            divide(pair - 1, (slot - 1) % 2, s - DIVIDE)
                        for ahead, e in PLAN[s]:
                            entry(pair + ahead, (slot + ahead) % QR, e)

                pairs(dve, do)
                for piece in range(PIECES):
                    divide(NPAIR - 1, (NPAIR - 1) % 2, piece)

            @block.tensor
            def _(pe):
                pe.wait_ge(consts, 2)

                def entry(pair, slot, e):
                    if not exists(pair, e):
                        return
                    if is_int(pair, NPAIR):
                        pe.wait_ge(max_done, NPAIR * NS)
                    elif e < 2:
                        if not below(pair, 1):
                            pe.wait_ge(max_done, (pair - 1) * NS + s_index(NRING - 2 + e))
                    elif ring[e - 2][0] == "s" or not exists(pair, e - 2):
                        pe.wait_ge(max_done, pair * NS + s_index(e - 2))
                    else:
                        pe.wait_ge(m_put, pair * HEADS + (ring[e - 2][1] + 1))
                    if e == 0:
                        pe.wait_ge(q_in[slot], (pair - slot) * (48 // QR) + 48)
                        if slot % 2 == 0:
                            pe.wait_ge(k_in[slot // 2], (pair - slot) * (48 // QR) + 48)
                    if ring[e][0] == "s":
                        jj, t = ring[e][1:]
                        for n in range(NQW):
                            last = nc.tensor.matmul(s_ps[:, e % 2, n * QW:(n + 1) * QW],
                                                    q_st[0:STACK, slot, jj, t * P:(t + 1) * P],
                                                    k_st[0:STACK, slot // 2, n * QW:(n + 1) * QW],
                                                    start=True, stop=True)
                        last.then_inc(s_ready, 1)
                    else:
                        jj = ring[e][1]
                        pe.wait_ge(m_made, pair * HEADS + (jj + 1))
                        for t in range(NKT):
                            last = nc.tensor.matmul(s_ps[:, e % 2, t * P:(t + 1) * P],
                                                    m_parts[:, jj % HEADS, t, :], ident_b[:, :], start=True, stop=True)
                        last.then_inc(m_ready, 1)

                start(entry)

                def scores(pair, slot, s, c):
                    h, jj = c // HEADS, c % HEADS
                    if not (below(pair, 1) and s == 0 and c < 2):
                        pe.wait_ge(exp_done, pair * TILES + (s * REP + c - 1))
                    if s == 0 and h == 0:
                        pe.wait_ge(m_put, pair * HEADS + (jj + 1))
                    nc.tensor.matmul(st_ps[:, c % 2, :], k_st[:, slot // 2, s * P:(s + 1) * P],
                                     q_st[:, slot, jj, h * QW:(h + 1) * QW], start=True, stop=True)\
                      .then_inc(st_ready, 1)

                def add_num(pair, slot, s):
                    pe.wait_ge(exp_done, pair * TILES + (s * REP + REP))
                    if s == 0:
                        if slot % 2 == 0:
                            pe.wait_ge(v_in[slot // 2], (pair - slot) * (16 // QR) + 16)
                        if not below(pair, 1):
                            pe.wait_ge(num_taken, pair)
                    for c in range(REP):
                        last = nc.tensor.matmul(num_ps[c * HD:(c + 1) * HD, :], v_sb[:, slot // 2, s, :],
                                                p_t[:, s, c, :], start=s == 0, stop=s == NKT - 1)
                    last.then_inc(num_done, 1)

                def add_den(pair, s):
                    if s == SUMMED and not below(pair, 1):
                        pe.wait_ge(den_taken, pair)
                    for c in range(REP):
                        last = nc.tensor.matmul(den_ps[c * HD:(c + 1) * HD, :], ones[:, :], p_t[:, s, c, :],
                                                start=s == SUMMED, stop=False)
                    last.then_inc(den_done, 1)

                def add_sum(pair, par):
                    pe.wait_ge(sum_done, pair * SUMS + SUMS)
                    for c in range(REP):
                        last = nc.tensor.matmul(den_ps[c * HD:(c + 1) * HD, :], ones[:, :], p_sum[:, par, c, :],
                                                start=False, stop=True)
                    last.then_inc(sum_used, 1)

                def do(pair, slot, it):
                    for s in range(STEPS):
                        plan = [(pair + ahead, (slot + ahead) % QR, e) for ahead, e in PLAN[s]]
                        before = (pair, slot, s - 1) if s else (pair - 1, (slot - 1) % QR, STEPS - 1)
                        is_first = below(pair, 1) and s == 0
                        scores(pair, slot, s, 0)
                        entry(*plan[0])
                        scores(pair, slot, s, 1)
                        if not is_first:
                            add_num(*before)
                        scores(pair, slot, s, 2)
                        entry(*plan[1])
                        scores(pair, slot, s, 3)
                        for item in plan[2:]:
                            entry(*item)
                        if not is_first and before[2] >= SUMMED:
                            add_den(before[0], before[2])
                        if s == LATE_DEN and not below(pair, 1):
                            add_sum(pair - 1, (slot - 1) % 2)

                pairs(pe, do)
                add_num(NPAIR - 1, QR - 1, STEPS - 1)
                add_den(NPAIR - 1, STEPS - 1)
                add_sum(NPAIR - 1, 1)


def finish(nc, x, b_o, lora_in, lora_out, earlier_in, ident, wo_hi, wo_lo, att_d, mod_raw_d, mod_gate_d, out):
    NTOK, D = x.shape
    KT = D // P
    NB = mod_raw_d.shape[1]
    G = att_d.shape[0] // NB
    E = 4
    ER = lora_out.shape[0]
    R = ER // E
    LORA_SCALE = 4.0
    NT = NTOK // P
    TPB = NT // NB
    HW = 512
    XR = 8

    with ExitStack() as ctx:
        def sb(name, shape, dt):
            return ctx.enter_context(nc.sbuf_tensor(name, shape, dt))

        def ps(name, shape):
            return ctx.enter_context(nc.psum_tensor(name, shape, F32))

        def sem(name):
            return ctx.enter_context(nc.semaphore(name))

        ga = sb("ga", [P, NB, D], F32)
        up = sb("up", [ER, NB, D], F32)
        up_w = sb("up_w", [ER, D], F32)
        down = sb("down", [P, KT, P], F32)
        mod_rows = sb("mod_rows", [NB * KT, 2, P], F32)
        shift2 = sb("shift2", [P, NB, KT], F32)
        scale2 = sb("scale2", [P, NB, KT], F32)
        earlier = sb("earlier", [P, E, E], F32)
        bo_f = sb("bo_f", [1, D], F32)
        bo = sb("bo", [P, D], F32R)
        ones = sb("ones2", [P, P], F32R)
        eps = sb("eps2", [P, 1], F32)
        a_f = sb("a_f", [P, 2, KT, P], F32)
        a_hi = sb("a_hi", [P, 2, KT, P], F32R)
        a_lo = sb("a_lo", [P, 2, KT, P], F32R)
        x_sb = sb("x_sb", [P, 4, D], F32)
        x1 = sb("x1", [P, XR, D], F32)
        xn = sb("xn2", [P, D], F32)
        h_t = sb("h_t", [P, 2, KT, P], F32)
        stats = sb("stats2", [P, 2, 6], F32)
        mv = sb("mv2", [P, 2], F32)
        std = sb("std2", [P, 1], F32)
        rstd = sb("rstd2", [P, 1], F32)
        mid = sb("mid", [P, ER + E], F32)
        above = sb("above", [P, E, E], F32)
        tied = sb("tied", [P, E, E], F32)
        rank = sb("rank", [P, E], F32)
        top = sb("top", [P, 1], F32)
        low = sb("low", [P, E], F32)
        ex = sb("ex", [P, E], F32)
        wts = sb("wts", [P, E], F32)
        total = sb("total", [P, 1], F32)
        gate = sb("gate", [P, E], F32)
        gmid = sb("gmid", [P, ER], F32)
        gmid_t = sb("gmid_t", [ER, 2, P], F32)

        o_ps = ps("o2_ps", [P, 2, D])
        t_ps = ps("t2_ps", [P, D])
        g_ps = ps("g_ps", [P, 512])
        d_ps = ps("d_ps", [P, HW])
        MID_T = slice(P, 2 * P)

        tables_in = sem("tables_in")
        consts = sem("consts2")
        prep = sem("prep")
        mod_turned = sem("mod_turned")
        a_in = [sem(f"a_in{u}") for u in range(2)]
        x_in = [sem(f"x_in{u}") for u in range(4)]
        a_hi_done = sem("a_hi_done")
        a_lo_done = sem("a_lo_done")
        o_ready = sem("o2_ready")
        x1_ready = sem("x1_ready")
        ln_step = sem("ln2_step")
        var_done = sem("var_done")
        std_done = sem("std2_done")
        xn_ready = sem("xn2_ready")
        waited = sem("waited2")
        waited_pe = sem("waited_pe")
        turned = sem("turned2")
        h_ready = sem("h2_ready")
        mid_ready = sem("mid_ready")
        r_step = sem("r_step")
        low_ready = sem("low_ready")
        ex_done = sem("ex_done")
        gmid_ready = sem("gmid_ready")
        gmid_turned = sem("gmid_turned")
        gmid_taken = sem("gmid_taken")
        d_ready = sem("d_ready")
        y_ready = sem("y_ready")
        y_out = [sem(f"y_out{u}") for u in range(XR)]
        TABLES = 16 * (6 + 2 * NB)

        def slots(eng, do):
            for t in range(TPB):
                do(t, 0, t)
            with eng.Fori(1, NB) as b:
                for t in range(TPB):
                    do(b * TPB + t, b, t)
            for t in range(LAG):
                do(NT + t, NB, t)

        LAG = 4

        def tile_of(slot, b, t, lag):
            if isinstance(slot, int) and not 0 <= slot - lag < NT:
                return None
            return slot - lag, (b if t >= lag else b - 1), (t - lag) % TPB

        def batch(table, b):
            return table[:, bass.ds(b, 1), :].rearrange("p b n -> p (b n)")

        with nc.Block() as block:

            @block.sync
            def _(sp):
                for u in range(XR):
                    sp.sem_inc(y_out[u], 16)
                sp.dma_start(bo_f[:, :], b_o).then_inc(tables_in, 16)
                sp.dma_start(down[:, :, :], lora_in).then_inc(tables_in, 16)
                for b in range(NB):
                    sp.dma_start(ga[:, b, :], mod_gate_d[0, b, :].partition_broadcast(P)).then_inc(tables_in, 16)
                sp.dma_start(earlier[:, :, :], earlier_in).then_inc(tables_in, 16)
                sp.dma_start(up_w[:, :], lora_out).then_inc(tables_in, 16)
                for b in range(NB):
                    sp.dma_start(up[:, b, :], mod_gate_d[3, b, :].partition_broadcast(ER)).then_inc(tables_in, 16)
                for v in range(2):
                    sp.dma_start(mod_rows[:, v, :], mod_raw_d[1 + v].rearrange("b (k p) -> (b k) p", p=P))\
                      .then_inc(tables_in, 16)

                def do(slot, b, t):
                    now = tile_of(slot, b, t, 0)
                    if now:
                        T, b, t = now
                        u = t % 2
                        if not (is_int(T, 0) or is_int(T, 1)):
                            sp.wait_ge(a_lo_done, T - 1)
                        src = att_d.rearrange("i p s -> (i p) s")[bass.ds(b * (G * P), G * P), t * P:(t + 1) * P]
                        sp.dma_start(a_f[:, u, :, :], src.rearrange("(k p) s -> p k s", p=P)).then_inc(a_in[u], 16)
                        if not (isinstance(T, int) and T < 4):
                            sp.wait_ge(x1_ready, T - 3)
                        sp.dma_start(x_sb[:, t % 4, :], x[bass.ds(T * P, P), :]).then_inc(x_in[t % 4], 16)

                def both(slot, b, t):
                    do(slot, b, t)
                    old = tile_of(slot, b, t, LAG)
                    if old:
                        T, _, t = old
                        sp.wait_ge(y_ready, T * 2 + 2)
                        sp.dma_start(out[bass.ds(T * P, P), :], x1[:, t % XR, :]).then_inc(y_out[t % XR], 16)

                slots(sp, both)
                for u in range(XR):
                    sp.wait_ge(y_out[u], 16 * NT // XR + 16)

            @block.gpsimd
            def _(pool):
                def do(slot, b, t):
                    now = tile_of(slot, b, t, 0)
                    if now:
                        T, b, t = now
                        u = t % 2
                        pool.wait_ge(a_hi_done, T + 1)
                        nc.gpsimd.tensor_tensor(a_lo[:, u, :, :], a_f[:, u, :, :], a_hi[:, u, :, :].bitcast(F32),
                                                ALU.subtract).then_inc(a_lo_done, 1)

                slots(pool, do)

            @block.scalar
            def _(act):
                def do(slot, b, t):
                    now = tile_of(slot, b, t, 0)
                    if now:
                        T, _, tt = now
                        u = tt % 2
                        act.wait_ge(a_in[u], (T - u) * 8 + 16)
                        if not (is_int(T, 0) or is_int(T, 1)):
                            act.wait_ge(o_ready, T * 2 - 2)
                        nc.scalar.copy(a_hi[:, u, :, :], a_f[:, u, :, :]).then_inc(a_hi_done, 1)
                    now = tile_of(slot, b, t, 2)
                    if now:
                        act.wait_ge(var_done, now[0] + 1)
                        nc.scalar.activation(std[:, :], mv[:, 1:2], ACT.Sqrt, bias=eps[:, 0:1]).then_inc(std_done, 1)
                    now = tile_of(slot, b, t, 3)
                    if now:
                        act.wait_ge(low_ready, now[0] + 1)
                        nc.scalar.activation(ex[:, :], low[:, :], ACT.Exp).then_inc(ex_done, 1)
                    now = tile_of(slot, b, t, 2)
                    if now:
                        T, bb, tt = now
                        act.wait_ge(prep, 3)
                        act.wait_ge(turned, T + 1)
                        for kt in range(KT):
                            last = nc.scalar.activation(h_t[:, tt % 2, kt, :], t_ps[:, kt * P:(kt + 1) * P],
                                                        ACT.Identity, bias=batch(shift2, bb)[:, kt:kt + 1],
                                                        scale=batch(scale2, bb)[:, kt:kt + 1])
                        last.then_inc(h_ready, 1)
                    now = tile_of(slot, b, t, 3)
                    if now:
                        T, _, tt = now
                        act.wait_ge(gmid_turned, T + 1)
                        nc.scalar.copy(gmid_t[:, tt % 2, :], g_ps[0:ER, MID_T]).then_inc(gmid_taken, 1)

                act.wait_ge(consts, 1)
                act.wait_ge(prep, 3)
                slots(act, do)

            @block.vector
            def _(dve):
                nc.vector.memset(eps[:, :], EPS)
                nc.vector.memset(ones[:, :].bitcast(F32), 1.0)
                nc.vector.memset(bo[:, :].bitcast(F32), 0.0).then_inc(consts, 1)
                dve.wait_ge(consts, 1)
                dve.wait_ge(tables_in, TABLES)
                nc.vector.tensor_copy(bo[0:1, :], bo_f[:, :])
                nc.vector.scalar_tensor_tensor(up[:, :, :], up[:, :, :], LORA_SCALE,
                                               up_w[:, :].unsqueeze(1).broadcast_to([ER, NB, D]), ALU.mult, ALU.mult)
                dve.wait_ge(mod_turned, 1)
                nc.vector.tensor_copy(shift2[:, :, :].rearrange("p b k -> p (b k)"), t_ps[:, 0:NB * KT])
                nc.vector.tensor_scalar(scale2[:, :, :].rearrange("p b k -> p (b k)"), t_ps[:, P:P + NB * KT],
                                        1.0, None, ALU.add).then_inc(prep, 1)
                dve.wait_ge(prep, 1)
                nc.vector.tensor_tensor(bo[32:33, :], bo_f[:, :], bo[0:1, :].bitcast(F32), ALU.subtract)\
                  .then_inc(prep, 2)

                def do(slot, b, t):
                    now = tile_of(slot, b, t, 2)
                    if now:
                        T, bb, tt = now
                        xs = x1[:, tt % XR, :]
                        if not (isinstance(T, int) and T < XR):
                            dve.wait_ge(y_out[tt % XR], (T - tt) * (16 // XR) + 16)
                        dve.wait_ge(o_ready, T * 2 + 2)
                        nc.vector.tensor_tensor(xs, o_ps[:, tt % 2, :], batch(ga, bb), ALU.mult).then_inc(ln_step, 1)
                        dve.wait_ge(ln_step, T * 3 + 1)
                        dve.wait_ge(x_in[tt % 4], (T - tt % 4) * 4 + 16)
                        nc.vector.tensor_tensor(xs, xs, x_sb[:, tt % 4, :], ALU.add).then_inc(x1_ready, 1)
                        dve.wait_ge(x1_ready, T + 1)
                        for c in range(2):
                            last = nc.vector.bn_stats(stats[:, c, :], xs[:, c * HW:(c + 1) * HW])
                        last.then_inc(ln_step, 1)
                        dve.wait_ge(ln_step, T * 3 + 2)
                        dve.sem_inc(waited, 1)
                        nc.vector.bn_aggr(mv[:, :], stats[:, :, :].rearrange("p c s -> p (c s)")).then_inc(var_done, 1)
                        dve.wait_ge(std_done, T + 1)
                        nc.vector.reciprocal(rstd[:, :], std[:, :]).then_inc(ln_step, 1)
                        dve.wait_ge(ln_step, T * 3 + 3)
                        if not is_int(T, 0):
                            dve.wait_ge(turned, T)
                        nc.vector.tensor_scalar(xn[:, :], xs, mv[:, 0:1], rstd[:, :], ALU.subtract, ALU.mult)\
                          .then_inc(xn_ready, 1)
                    mids = tile_of(slot, b, t, 3)
                    if mids:
                        T = mids[0]
                        at = [0]

                        def step(ins):
                            at[0] += 1
                            ins.then_inc(r_step, 1)
                            dve.wait_ge(r_step, T * STEPS + at[0])

                        STEPS = 9
                        dve.wait_ge(mid_ready, T + 1)
                        step(nc.vector.tensor_copy(mid[:, :], g_ps[:, 0:ER + E]))
                        logit = mid[:, ER:ER + E]
                        rows = logit.unsqueeze(2).broadcast_to([P, E, E])
                        cols = logit.unsqueeze(1).broadcast_to([P, E, E])
                        nc.vector.tensor_tensor(above[:, :, :], cols, rows, ALU.is_gt)
                        nc.vector.tensor_tensor(tied[:, :, :], cols, rows, ALU.is_equal)
                        step(nc.vector.tensor_reduce(top[:, :], logit, AX_X, ALU.max))
                        nc.vector.tensor_scalar(low[:, :], logit, top[:, 0:1], None, ALU.subtract).then_inc(low_ready, 1)
                        step(nc.vector.tensor_tensor(tied[:, :, :], tied[:, :, :], earlier[:, :, :], ALU.mult))
                        step(nc.vector.tensor_tensor(above[:, :, :], above[:, :, :], tied[:, :, :], ALU.add))
                        step(nc.vector.tensor_reduce(rank[:, :], above[:, :, :], AX_X, ALU.add))
                    now = tile_of(slot, b, t, 4)
                    if now:
                        add(now, 0)
                    if mids:
                        dve.wait_ge(ex_done, T + 1)
                        step(nc.vector.scalar_tensor_tensor(wts[:, :], rank[:, :], 2.0, ex[:, :], ALU.is_lt, ALU.mult))
                        step(nc.vector.reduce_sum(total[:, :], wts[:, :], AX_X))
                        step(nc.vector.reciprocal(top[:, :], total[:, :]))
                        step(nc.vector.tensor_scalar(gate[:, :], wts[:, :], top[:, 0:1], None, ALU.mult))
                        assert at[0] == STEPS
                        if not is_int(T, 0):
                            dve.wait_ge(gmid_turned, T)
                        nc.vector.tensor_tensor(gmid[:, :].rearrange("p (e r) -> p e r", e=E),
                                                mid[:, 0:ER].rearrange("p (e r) -> p e r", e=E),
                                                gate[:, :].unsqueeze(2).broadcast_to([P, E, R]), ALU.mult)\
                          .then_inc(gmid_ready, 1)
                    if now:
                        add(now, 1)

                def add(now, half):
                    T, _, tt = now
                    cols = slice(half * HW, (half + 1) * HW)
                    dve.wait_ge(d_ready, T * 2 + (half + 1))
                    nc.vector.tensor_tensor(x1[:, tt % XR, cols], d_ps[:, :], x1[:, tt % XR, cols], ALU.add)\
                      .then_inc(y_ready, 1)

                slots(dve, do)

            @block.tensor
            def _(pe):
                pe.wait_ge(tables_in, TABLES)
                for v in range(2):
                    last = nc.tensor.transpose(t_ps[:, v * P:v * P + NB * KT], mod_rows[:, v, :],
                                               ident[0:NB * KT, 0:NB * KT])
                last.then_inc(mod_turned, 1)
                pe.wait_ge(prep, 3)

                def project_half(now, half):
                    T, _, tt = now
                    cols = slice(half * HW, (half + 1) * HW)
                    u = tt % 2
                    if half == 0:
                        pe.wait_ge(a_lo_done, T + 1)
                        if not (is_int(T, 0) or is_int(T, 1)):
                            pe.wait_ge(x1_ready, T - 1)
                    for k in range(KT):
                        for n, (a, w) in enumerate(((a_hi, wo_hi), (a_hi, wo_lo), (a_lo, wo_hi))):
                            nc.tensor.matmul(o_ps[:, u, cols], a[:, u, k, :], w[:, k, cols],
                                             start=(k == 0 and n == 0), stop=False)
                    nc.tensor.matmul(o_ps[:, u, cols], ones[:, :], bo[:, cols], start=False, stop=True)\
                      .then_inc(o_ready, 1)

                def experts_half(now, half):
                    T, bb, tt = now
                    if half == 0:
                        pe.wait_ge(gmid_taken, T + 1)
                    if not (is_int(T, 0) and half == 0):
                        pe.wait_ge(y_ready, T * 2 + half)
                    pe.sem_inc(waited_pe, 1)
                    nc.tensor.matmul(d_ps[:, :], gmid_t[:, tt % 2, :], batch(up, bb)[:, half * HW:(half + 1) * HW],
                                     start=True, stop=True).then_inc(d_ready, 1)

                def do(slot, b, t):
                    proj, turn, mids, add = (tile_of(slot, b, t, lag) for lag in (1, 2, 3, 4))
                    if proj:
                        project_half(proj, 0)
                    if mids:
                        T, _, tt = mids
                        pe.wait_ge(h_ready, T + 1)
                        if not is_int(T, 0):
                            pe.wait_ge(gmid_taken, T)
                        for k in range(KT):
                            last = nc.tensor.matmul(g_ps[:, 0:P], h_t[:, tt % 2, k, :], down[:, k, :],
                                                    start=k == 0, stop=k == KT - 1)
                        last.then_inc(mid_ready, 1)
                    if add:
                        experts_half(add, 0)
                    if proj:
                        project_half(proj, 1)
                    if turn:
                        T = turn[0]
                        pe.wait_ge(xn_ready, T + 1)
                        if not is_int(T, 0):
                            pe.wait_ge(h_ready, T)
                        for k in range(KT):
                            last = nc.tensor.transpose(t_ps[:, k * P:(k + 1) * P], xn[:, k * P:(k + 1) * P], ident[:, :])
                        last.then_inc(turned, 1)
                    if mids:
                        T = mids[0]
                        pe.wait_ge(prep, 3)
                        pe.wait_ge(gmid_ready, T + 1)
                        nc.tensor.transpose(g_ps[0:ER, MID_T], gmid[:, :], ident[:, :]).then_inc(gmid_turned, 1)
                    if add:
                        experts_half(add, 1)

                slots(pe, do)


def kernel(L0_attn_x, L0_attn_wq_w, L0_attn_wq_b, L0_attn_wk_w, L0_attn_wk_b, L0_attn_wv_w, L0_attn_wv_b,
           L0_attn_wo_w, L0_attn_wo_b, L0_ffn_router_w, L0_ffn_A, L0_ffn_B, L0_c, L0_wmod):
    import numpy as np
    import concourse.bacc as bacc
    from concourse.bass_utils import run_bass_kernel_spmd

    def tiles(a):
        return np.ascontiguousarray(a.reshape(-1, P, a.shape[-1]).transpose(1, 0, 2))

    x = np.asarray(L0_attn_x)
    bsz, s, d = x.shape
    lora_a, router, lora_b = np.asarray(L0_ffn_A), np.asarray(L0_ffn_router_w), np.asarray(L0_ffn_B)
    e, r, _ = lora_a.shape
    down = np.zeros((d, P), np.float32)
    down[:, :e * r] = lora_a.reshape(e * r, d).T
    down[:, e * r:e * r + e] = router.T
    arrays = {
        "x": np.ascontiguousarray(x.reshape(bsz * s, d)),
        "w_q": np.asarray(L0_attn_wq_w), "w_k": np.asarray(L0_attn_wk_w), "w_v": np.asarray(L0_attn_wv_w),
        "w_o": np.asarray(L0_attn_wo_w),
        "b_q": np.ascontiguousarray(np.asarray(L0_attn_wq_b).reshape(-1, P).T),
        "b_k": np.ascontiguousarray(np.asarray(L0_attn_wk_b).reshape(-1, P).T),
        "b_v": np.asarray(L0_attn_wv_b),
        "b_o": np.asarray(L0_attn_wo_b).reshape(1, d),
        "lora_in": tiles(down),
        "lora_out": np.ascontiguousarray(lora_b.transpose(0, 2, 1).reshape(e * r, d)),
        "c_t": tiles(np.asarray(L0_c).T),
        "w_mod": np.asarray(L0_wmod),
        "ident_in": np.eye(P, dtype=np.float32),
        "earlier_in": np.ascontiguousarray(np.broadcast_to(np.tril(np.ones((e, e), np.float32), -1), (P, e, e))),
    }
    nc = bacc.Bacc("TRN2", target_bir_lowering=False, num_devices=1)
    args = {n: nc.dram_tensor(n, a.shape, mybir.dt.from_np(a.dtype), kind="ExternalInput").ap()
            for n, a in arrays.items()}
    out = nc.dram_tensor("out", (bsz * s, d), F32, kind="ExternalOutput").ap()
    adaln_block(nc, **args, out=out)
    r = run_bass_kernel_spmd(nc, [arrays], core_ids=[0])
    return r.results[0]["out"].reshape(bsz, s, d)
```

```python
from contextlib import ExitStack

import concourse.bass as bass
from concourse import mybir

ALU = mybir.AluOpType
ACT = mybir.ActivationFunctionType
F32 = mybir.dt.float32
F32R = mybir.dt.float32r
BF16 = mybir.dt.bfloat16
AX_X = mybir.AxisListType.X

P = 128
EPS = 1e-5
GATE_FLOOR = 0.25


def is_int(i, value):
    return isinstance(i, int) and i == value


def adaln_block(nc, x, w_q, w_k, w_v, w_o, b_q, b_k, b_v, b_o, lora_in, lora_out, c_t, w_mod, ident_in, earlier_in, out):
    NTOK, D = x.shape
    NB = c_t.shape[2]
    S = NTOK // NB
    KT = D // P
    NKV = w_k.shape[1]
    HD = 32
    REP = D // NKV
    G = NKV // HD
    E = 4
    R = lora_out.shape[0] // E
    BLK = 512
    NBLK = NTOK // BLK
    KVT = NKV // P
    assert S == 2 * BLK and REP * HD == P and KT == 8 and NBLK == 8 and G == 8

    NIT = NB * G
    q_hi_d = nc.dram_tensor("q_hi_d", (NIT, P, S), F32, kind="Internal").ap()
    q_lo_d = nc.dram_tensor("q_lo_d", (NIT, P, S), F32, kind="Internal").ap()
    k_hi_d = nc.dram_tensor("k_hi_d", (NIT * HD, S), F32, kind="Internal").ap()
    k_lo_d = nc.dram_tensor("k_lo_d", (NIT * HD, S), F32, kind="Internal").ap()
    v_d = nc.dram_tensor("v_d", (NIT, P, S // P, HD), F32, kind="Internal").ap()
    att_d = nc.dram_tensor("att_d", (NIT, P, S), F32, kind="Internal").ap()
    mod_raw_d = nc.dram_tensor("mod_raw_d", (4, NB, D), F32, kind="Internal").ap()
    mod_gate_d = nc.dram_tensor("mod_gate_d", (4, NB, D), F32, kind="Internal").ap()

    with ExitStack() as whole:
        def keep(name, shape, dt):
            return whole.enter_context(nc.sbuf_tensor(name, shape, dt))

        ident = keep("ident", [P, P], F32)
        project(nc, x, w_q, w_k, w_v, b_q, b_k, b_v, c_t, w_mod, ident_in, ident,
                q_hi_d, q_lo_d, k_hi_d, k_lo_d, v_d, mod_raw_d, mod_gate_d)
        wo_hi = keep("wo_hi", [P, KT, D], F32R)
        wo_lo = keep("wo_lo", [P, KT, D], F32R)
        attend(nc, w_o, ident, wo_hi, wo_lo, q_hi_d, q_lo_d, k_hi_d, k_lo_d, v_d, att_d)
        finish(nc, x, b_o, lora_in, lora_out, earlier_in, ident, wo_hi, wo_lo, att_d, mod_raw_d, mod_gate_d, out)


def project(nc, x, w_q, w_k, w_v, b_q, b_k, b_v, c_t, w_mod, ident_in, ident,
            q_hi_d, q_lo_d, k_hi_d, k_lo_d, v_d, mod_raw_d, mod_gate_d):
    NTOK, D = x.shape
    NB = c_t.shape[2]
    KT = D // P
    NKV = w_k.shape[1]
    KVT = NKV // P
    HD = 32
    G = NKV // HD
    NW = D + 2 * NKV
    BLK = 512
    HALF = 256
    HT = HALF // P
    QG, KG, VG = KT, KVT, BLK // P
    NG = QG + KG + VG
    QK = QG + KG
    SLOTS = 4
    MOD_CHUNKS = 2 * KT
    W_CHUNKS = 2 * KT
    OBANKS = 4
    NBLK = NTOK // BLK

    PREPARE = {-1: [("fetch", 0)], 0: [("stats", 0)], 1: [("norm", 0)], 2: [("turn", 0, 0), ("turn", 0, 1)],
               3: [("turn", 0, 2), ("turn", 0, 3)], 4: [("turn", 0, 4), ("turn", 0, 5)],
               5: [("turn", 0, 6), ("turn", 0, 7), ("fetch", 1)], 7: [("stats", 1)], 8: [("norm", 1)],
               9: [("turn", 1, 0), ("turn", 1, 1)], 10: [("turn", 1, 2), ("turn", 1, 3)],
               11: [("turn", 1, 4), ("turn", 1, 5)], 12: [("turn", 1, 6), ("turn", 1, 7)]}
    MODULATE = {-1: [("rows", 0)], 3: [("mod", 0), ("rows", 1)], 11: [("mod", 1)]}
    FIRST = [("stats", 0), ("norm", 0), ("stats", 1), ("norm", 1), ("shift",)]
    for kt in range(KT):
        FIRST += [("w", kt), ("turn", 0, kt), ("turn", 1, kt)]
    FIRST += [("w", KT + kt) for kt in range(KT)]

    def tile_at(i, hf, kt):
        return 2 * kt + hf if is_int(i, -1) else i * (2 * KT) + ((2 + hf) * KT + kt)

    def bank_at(i, hf, kt):
        return hf if is_int(i, -1) else kt % 2

    def w_count(ch):
        return 16 * MOD_CHUNKS // SLOTS + sum(16 if c < KT else 32 for c in range(ch + 1) if c % SLOTS == ch % SLOTS)

    def events(prepare, modulate):
        seen = []
        for g in range(-1, NG):
            if g >= 0:
                seen.append(("group", g))
            if modulate:
                seen += MODULATE.get(g, [])
            if prepare:
                seen += PREPARE.get(g, [])
        return seen

    def blocks(eng, do):
        do(0, 0, 0, events(True, True), 0)
        with eng.Fori(0, NBLK // 2 - 1) as n:
            do(n * 2 + 1, n, 1, events(True, False), None)
            do(n * 2 + 2, n + 1, 0, events(True, True), n + 1)
        do(NBLK - 1, NB - 1, 1, events(False, False), None)

    with ExitStack() as ctx:
        def sb(name, shape, dt):
            return ctx.enter_context(nc.sbuf_tensor(name, shape, dt))

        def sem(name):
            return ctx.enter_context(nc.semaphore(name))

        w_hi = sb("w_hi", [P, KT, NW], F32R)
        w_lo = sb("w_lo", [P, KT, NW], F32R)
        h_hi = sb("h_hi", [P, 2, KT, BLK], F32R)
        h_lo = sb("h_lo", [P, 2, KT, BLK], F32R)
        xn = sb("xn", [P, HT, D], F32)
        stage = sb("stage", [P, SLOTS, D], F32)
        h_f = sb("h_f", [P, 2, HALF], F32)
        side = sb("side", [P, 3 * BLK + 4 * HALF], F32)
        o_hi = sb("o_hi", [P, 2, BLK], F32R)
        o_lo = sb("o_lo", [P, 2, BLK], F32R)
        cs = sb("cs", [P, KT, NB], F32)
        ce = sb("ce", [P, KT, NB], F32)
        cr = sb("cr", [P, KT, NB], F32)
        c_rep = sb("c_rep", [P, KT, 32], F32)
        shift = sb("shift", [P, KT, NB], F32)
        scale1 = sb("scale1", [P, KT, NB], F32)
        bias_qk = sb("bias_qk", [P, QK], F32)
        bias_v = sb("bias_v", [P, NKV], F32)
        stats = sb("stats", [P, HT, 2, 6], F32)
        mv = sb("mv", [P, HT, 2], F32)
        std = sb("std", [P, HT], F32)
        rstd = sb("rstd", [P, HT], F32)
        eps = sb("eps", [P, 1], F32)
        o_f = side[:, 0:2 * BLK].rearrange("p (u s) -> p u s", u=2)
        v_f = side[:, 2 * BLK:3 * BLK].rearrange("p (u n) -> p u n", u=2)
        mrow, mmax, mmin, mgate = (side[:, 3 * BLK + n * HALF:3 * BLK + (n + 1) * HALF] for n in range(4))

        t_ps = ctx.enter_context(nc.psum_tensor("t_ps", [P, 2, 512], F32))
        o_ps = ctx.enter_context(nc.psum_tensor("o_ps", [P, OBANKS, 512], F32))
        m_ps = ctx.enter_context(nc.psum_tensor("m_ps", [P, 512], F32))

        small_in = sem("small_in")
        stage_in = [sem(f"stage_in{s}") for s in range(SLOTS)]
        stage_used = sem("stage_used")
        w_hi_done = sem("w_hi_done")
        wq_lo_done = sem("wq_lo_done")
        wkv_lo_done = sem("wkv_lo_done")
        mod_step = sem("mod_step")
        c_exp = sem("c_exp")
        c_step = sem("c_step")
        c_done = sem("c_done")
        x_in = sem("x_in")
        x1_in = sem("x1_in")
        stats_done = sem("stats_done")
        std_done = sem("std_done")
        xn_ready = sem("xn_ready")
        waited = sem("waited")
        ln_step = sem("ln_step")
        turned = sem("turned")
        h_ready = sem("h_ready")
        h_hi_done = sem("h_hi_done")
        h_lo_done = sem("h_lo_done")
        o_ready = sem("o_ready")
        o_taken = sem("o_taken")
        o_hi_done = sem("o_hi_done")
        o_lo_done = sem("o_lo_done")
        qk_out = [sem(f"qk_out{s}") for s in range(2)]
        v_out = [sem(f"v_out{s}") for s in range(2)]
        row_ready = sem("row_ready")
        row_step = sem("row_step")
        row_out = sem("row_out")

        w_mod_t = w_mod.rearrange("(k p) n -> p k n", p=P)
        xn1 = side[:, BLK:BLK + HT * D].rearrange("p (t d) -> p t d", t=HT)

        def normed(i, hf):
            return xn1 if is_int(i, -1) and hf == 1 else xn

        with nc.Block() as block:

            @block.sync
            def _(sp):
                def fetch(half):
                    if not is_int(half, 0):
                        sp.wait_ge(turned, half * KT)
                    sp.dma_start(xn[:, :, :], x[bass.ds(half * HALF, HALF), :].rearrange("(t p) d -> p t d", p=P))\
                      .then_inc(x_in, 16)

                sp.dma_start(cs[:, :, :], c_t).then_inc(small_in, 16)
                sp.dma_start(ident[:, :], ident_in).then_inc(small_in, 16)
                sp.dma_start(bias_qk[:, 0:QG], b_q).then_inc(small_in, 16)
                sp.dma_start(bias_qk[:, QG:QK], b_k).then_inc(small_in, 16)
                sp.dma_start(bias_v[:, :], b_v.partition_broadcast(P)).then_inc(small_in, 16)
                for ch in range(MOD_CHUNKS):
                    if ch == SLOTS:
                        fetch(0)
                        sp.dma_start(xn1, x[HALF:2 * HALF, :].rearrange("(t p) d -> p t d", p=P))\
                          .then_inc(x1_in, 16)
                    if ch >= SLOTS:
                        sp.wait_ge(stage_used, ch - SLOTS + 1)
                    sp.dma_start(stage[:, ch % SLOTS, :], w_mod_t[:, ch // 2, (ch % 2) * D:(ch % 2 + 1) * D])\
                      .then_inc(stage_in[ch % SLOTS], 16)
                for ch in range(W_CHUNKS):
                    slot = ch % SLOTS
                    if ch == KT + SLOTS:
                        fetch(2)
                    if ch < SLOTS:
                        sp.wait_ge(stage_used, MOD_CHUNKS - SLOTS + ch + 1)
                    elif ch - SLOTS < KT:
                        sp.wait_ge(wq_lo_done, ch - SLOTS + 1)
                    else:
                        sp.wait_ge(wkv_lo_done, ch - SLOTS - KT + 1)
                    rows = slice((ch % KT) * P, (ch % KT + 1) * P)
                    if ch < KT:
                        sp.dma_start(stage[:, slot, :], w_q[rows, :]).then_inc(stage_in[slot], 16)
                    else:
                        sp.dma_start(stage[:, slot, 0:NKV], w_k[rows, :]).then_inc(stage_in[slot], 16)
                        sp.dma_start(stage[:, slot, NKV:2 * NKV], w_v[rows, :]).then_inc(stage_in[slot], 16)

                def do(i, b, par, evs, vec):
                    cols = slice(par * BLK, (par + 1) * BLK)
                    for ev in evs:
                        if ev == ("fetch", 0) and is_int(i, 0):
                            pass
                        elif ev[0] == "fetch":
                            fetch(i * 2 + (2 + ev[1]))
                        elif ev[0] == "group" and ev[1] < QK:
                            g = ev[1]
                            if g < QG:
                                dst_hi = q_hi_d.rearrange("i p s -> (i p) s")
                                dst_lo = q_lo_d.rearrange("i p s -> (i p) s")
                                rows = bass.ds(b * (G * P) + g * P, P)
                            else:
                                dst_hi, dst_lo = k_hi_d, k_lo_d
                                rows = bass.ds(b * (G * HD) + (g - QG) * P, P)
                            sp.wait_ge(o_hi_done, i * QK + (g + 1))
                            sp.dma_start(dst_hi[rows, cols], o_hi[:, g % 2, :].bitcast(F32)).then_inc(qk_out[g % 2], 16)
                            sp.wait_ge(o_lo_done, i * QK + (g + 1))
                            sp.dma_start(dst_lo[rows, cols], o_lo[:, g % 2, :].bitcast(F32)).then_inc(qk_out[g % 2], 16)
                        elif ev[0] == "group":
                            v = ev[1] - QK
                            sp.wait_ge(o_taken, i * NG + (ev[1] + 1))
                            dst = v_d.rearrange("i p t c -> t p i c")[par * VG + v][:, bass.ds(b * G, G), :]
                            sp.dma_start(dst, v_f[:, v % 2, :].rearrange("p (i c) -> p i c", c=HD))\
                              .then_inc(v_out[v % 2], 16)
                        elif ev[0] == "rows":
                            if ev == ("rows", 0) and is_int(vec, 0):
                                sp.wait_ge(wkv_lo_done, KT)
                            sp.wait_ge(stage_used, vec * (2 * SLOTS) + (MOD_CHUNKS + ev[1] * SLOTS))
                            for s in range(SLOTS):
                                sp.dma_start(stage[:, s, :],
                                             w_mod_t[:, ev[1] * SLOTS + s, bass.ds(vec * D + 2 * D, D)])\
                                  .then_inc(stage_in[s], 16)
                        elif ev == ("mod", 1):
                            sp.wait_ge(row_ready, vec + 1)
                            for j in range(4):
                                src = slice(32 * j, 32 * j + 25, 8)
                                for d, t in ((mod_raw_d, mrow), (mod_gate_d, mgate)):
                                    dst = d.rearrange("v b n -> (v b) n")[bass.ds(vec * NB, NB),
                                                                          j * HALF:(j + 1) * HALF]
                                    sp.dma_start(dst, t[src, :]).then_inc(row_out, 16)

                blocks(sp, do)
                for s in range(2):
                    sp.wait_ge(qk_out[s], 32 * NBLK * QK // 2)
                    sp.wait_ge(v_out[s], 16 * NBLK * VG // 2)
                sp.wait_ge(row_out, 16 * 8 * NB)

            @block.scalar
            def _(act):
                act.wait_ge(small_in, 80)
                nc.scalar.activation(ce[:, :, :], cs[:, :, :], ACT.Exp, scale=-1.0).then_inc(c_exp, 1)

                def weights(ch):
                    slot, kt = ch % SLOTS, ch % KT
                    act.wait_ge(stage_in[slot], w_count(ch))
                    cols = slice(0, D) if ch < KT else slice(D, NW)
                    nc.scalar.copy(w_hi[:, kt, cols], stage[:, slot, 0:cols.stop - cols.start])\
                      .then_inc(w_hi_done, 1)

                def do(i, b, par, evs, vec):
                    for ev in evs:
                        if ev[0] == "stats":
                            half = i * 2 + (2 + ev[1])
                            act.wait_ge(stats_done, half + 1)
                            nc.scalar.activation(std[:, :], mv[:, :, 1], ACT.Sqrt, bias=eps[:, 0:1])\
                              .then_inc(std_done, 1)
                        elif ev[0] == "w":
                            weights(ev[1])
                        elif ev[0] == "turn":
                            hf, kt = ev[1:]
                            tile = tile_at(i, hf, kt)
                            if kt == 0 and hf == 0 and not is_int(i, -1):
                                act.wait_ge(o_ready, i * NG)
                            act.wait_ge(h_ready, tile + 1)
                            nc.scalar.copy(h_hi[:, 1 - par, kt, hf * HALF:(hf + 1) * HALF], h_f[:, bank_at(i, hf, kt), :])\
                              .then_inc(h_hi_done, 1)
                        elif ev[0] == "group" and ev[1] < QK:
                            g = ev[1]
                            act.wait_ge(o_taken, i * NG + (g + 1))
                            act.wait_ge(qk_out[g % 2], i * (32 * QK // 2) + 32 * (g // 2))
                            nc.scalar.copy(o_hi[:, g % 2, :], o_f[:, g % 2, :]).then_inc(o_hi_done, 1)

                do(-1, -1, 1, FIRST, None)
                blocks(act, do)

            @block.gpsimd
            def _(pool):
                def weights(ch):
                    slot, kt = ch % SLOTS, ch % KT
                    pool.wait_ge(w_hi_done, ch + 1)
                    nc.gpsimd.tensor_tensor(w_lo[:, kt, D:NW], stage[:, slot, 0:NW - D],
                                            w_hi[:, kt, D:NW].bitcast(F32),
                                            ALU.subtract).then_inc(wkv_lo_done, 1)

                def do(i, b, par, evs, vec):
                    for ev in evs:
                        if ev[0] == "turn":
                            hf, kt = ev[1:]
                            tile = tile_at(i, hf, kt)
                            cols = slice(hf * HALF, (hf + 1) * HALF)
                            pool.wait_ge(h_hi_done, tile + 1)
                            nc.gpsimd.tensor_tensor(h_lo[:, 1 - par, kt, cols], h_f[:, bank_at(i, hf, kt), :],
                                                    h_hi[:, 1 - par, kt, cols].bitcast(F32), ALU.subtract)\
                              .then_inc(h_lo_done, 1)
                        elif ev[0] == "w" and ev[1] >= KT:
                            weights(ev[1])
                        elif ev[0] == "group" and ev[1] < QK:
                            g = ev[1]
                            pool.wait_ge(o_hi_done, i * QK + (g + 1))
                            nc.gpsimd.tensor_tensor(o_lo[:, g % 2, :], o_f[:, g % 2, :],
                                                    o_hi[:, g % 2, :].bitcast(F32), ALU.subtract)\
                              .then_inc(o_lo_done, 1)

                do(-1, -1, 1, FIRST, None)
                blocks(pool, do)

            @block.vector
            def _(dve):
                nc.vector.memset(eps[:, :], EPS)
                dve.wait_ge(c_exp, 1)
                nc.vector.tensor_scalar(cr[:, :, :], ce[:, :, :], 1.0, None, ALU.add).then_inc(c_step, 1)
                dve.wait_ge(c_step, 1)
                nc.vector.reciprocal(ce[:, :, :], cr[:, :, :]).then_inc(c_step, 1)
                dve.wait_ge(c_step, 2)
                nc.vector.tensor_tensor(cr[:, :, :], cs[:, :, :], ce[:, :, :], ALU.mult).then_inc(c_step, 1)
                dve.wait_ge(c_step, 3)
                nc.vector.tensor_copy(c_rep[:, :, :].rearrange("p k (b r) -> p k b r", b=NB),
                                      cr[:, :, :].unsqueeze(3).broadcast_to([P, KT, NB, 8])).then_inc(c_done, 1)

                def do(i, b, par, evs, vec):
                    for ev in evs:
                        if ev[0] == "stats":
                            half = i * 2 + (2 + ev[1])
                            xs = normed(i, ev[1])
                            if not is_int(i, -1):
                                dve.wait_ge(x_in, half * 16)
                            else:
                                dve.wait_ge(x1_in if ev[1] else x_in, 16)
                            for t in range(HT):
                                for c in range(2):
                                    last = nc.vector.bn_stats(stats[:, t, c, :], xs[:, t, c * 512:(c + 1) * 512])
                            last.then_inc(ln_step, 1)
                            dve.wait_ge(ln_step, half * 2 + 1)
                            dve.sem_inc(waited, 1)
                            for t in range(HT):
                                last = nc.vector.bn_aggr(mv[:, t, :], stats[:, t, :, :].rearrange("p c s -> p (c s)"))
                            last.then_inc(stats_done, 1)
                        elif ev[0] == "norm":
                            half = i * 2 + (2 + ev[1])
                            dve.wait_ge(std_done, half + 1)
                            nc.vector.reciprocal(rstd[:, :], std[:, :]).then_inc(ln_step, 1)
                            dve.wait_ge(ln_step, half * 2 + 2)
                            for t in range(HT):
                                xs = normed(i, ev[1])[:, t, :]
                                last = nc.vector.tensor_scalar(xs, xs, mv[:, t, 0:1], rstd[:, t:t + 1],
                                                               ALU.subtract, ALU.mult)
                            last.then_inc(xn_ready, 1)
                        elif ev[0] == "shift":
                            dve.wait_ge(stage_used, MOD_CHUNKS)
                            nc.vector.tensor_copy(o_f[:, 0, :], m_ps[:, :]).then_inc(mod_step, 1)
                            dve.wait_ge(mod_step, 2)
                            m = t_ps[:, 0, :].rearrange("p (c v j b r) -> p v j c b r", c=KT // 2, v=2, j=2, b=NB)
                            nc.vector.tensor_copy(shift[:, :, :].rearrange("p (j c) b -> p j c b", j=2),
                                                  m[:, 0, :, :, :, 0])
                            nc.vector.tensor_scalar(scale1[:, :, :].rearrange("p (j c) b -> p j c b", j=2),
                                                    m[:, 1, :, :, :, 0], 1.0, None, ALU.add).then_inc(mod_step, 1)
                            dve.wait_ge(mod_step, 3)
                        elif ev[0] == "w" and ev[1] < KT:
                            ch = ev[1]
                            dve.wait_ge(w_hi_done, ch + 1)
                            nc.vector.tensor_tensor(w_lo[:, ch, 0:D], stage[:, ch % SLOTS, :],
                                                    w_hi[:, ch, 0:D].bitcast(F32), ALU.subtract)\
                              .then_inc(wq_lo_done, 1)
                        elif ev[0] == "turn":
                            hf, kt = ev[1:]
                            tile = tile_at(i, hf, kt)
                            bank = bank_at(i, hf, kt)
                            dve.wait_ge(turned, tile + 1)
                            if not (is_int(i, -1) and kt == 0):
                                dve.wait_ge(h_lo_done, tile - 1)
                            at = b + par
                            nc.vector.tensor_scalar(h_f[:, bank, :], t_ps[:, bank, 0:HALF],
                                                    scale1[:, kt, bass.ds(at, 1)], shift[:, kt, bass.ds(at, 1)],
                                                    ALU.mult, ALU.add).then_inc(h_ready, 1)
                        elif ev[0] == "group":
                            g = ev[1]
                            dve.wait_ge(o_ready, i * NG + (g + 1))
                            bank = (par * NG + g) % OBANKS
                            if g < QK:
                                if not (is_int(i, 0) and g < 2):
                                    dve.wait_ge(o_lo_done, i * QK + (g - 1))
                                nc.vector.tensor_scalar(o_f[:, g % 2, :], o_ps[:, bank, :], bias_qk[:, g:g + 1],
                                                        None, ALU.add).then_inc(o_taken, 1)
                            else:
                                v = g - QK
                                dve.wait_ge(v_out[v % 2], i * (16 * VG // 2) + 16 * (v // 2))
                                nc.vector.tensor_tensor(v_f[:, v % 2, :], o_ps[:, bank, 0:NKV], bias_v[:, :],
                                                        ALU.add).then_inc(o_taken, 1)
                        elif ev == ("mod", 1):
                            dve.wait_ge(stage_used, vec * (2 * SLOTS) + (MOD_CHUNKS + 2 * SLOTS))
                            dve.wait_ge(row_out, vec * (16 * 8))
                            nc.vector.tensor_copy(mrow[:, :], m_ps[:, 0:HALF]).then_inc(row_step, 1)
                            dve.wait_ge(row_step, vec * 3 + 1)
                            nc.vector.tensor_scalar(mmax[:, :], mrow[:, :], GATE_FLOOR, None, ALU.max)
                            nc.vector.tensor_scalar(mmin[:, :], mrow[:, :], -GATE_FLOOR, None, ALU.min)\
                              .then_inc(row_step, 1)
                            dve.wait_ge(row_step, vec * 3 + 2)
                            nc.vector.scalar_tensor_tensor(mmax[:, :], mrow[:, :], 0.0, mmax[:, :], ALU.is_ge, ALU.mult)
                            nc.vector.scalar_tensor_tensor(mmin[:, :], mrow[:, :], 0.0, mmin[:, :], ALU.is_lt, ALU.mult)\
                              .then_inc(row_step, 1)
                            dve.wait_ge(row_step, vec * 3 + 3)
                            nc.vector.tensor_tensor(mgate[:, :], mmax[:, :], mmin[:, :], ALU.add).then_inc(row_ready, 1)

                do(-1, -1, 1, FIRST, None)
                blocks(dve, do)

            @block.tensor
            def _(pe):
                pe.wait_ge(c_done, 1)
                for kt in range(KT):
                    for v in range(2):
                        ch = 2 * kt + v
                        pe.wait_ge(stage_in[ch % SLOTS], 16 * (ch // SLOTS + 1))
                    for j in range(4):
                        last = nc.tensor.matmul(m_ps[32 * j:32 * j + 32, :], c_rep[:, kt, :],
                                                stage[:, (2 * kt + j // 2) % SLOTS, (j % 2) * 512:(j % 2 + 1) * 512],
                                                start=kt == 0, stop=kt == KT - 1)
                    last.then_inc(stage_used, 2)

                def first_groups(kt):
                    pe.wait_ge(h_lo_done, 2 * kt + 2)
                    pe.wait_ge(wq_lo_done, kt + 1)
                    for g in range(OBANKS):
                        for n, (h, w) in enumerate(((h_hi, w_hi), (h_hi, w_lo), (h_lo, w_hi))):
                            last = nc.tensor.matmul(o_ps[:, g, :], w[:, kt, g * P:(g + 1) * P], h[:, 0, kt, :],
                                                    start=kt == 0 and n == 0, stop=kt == KT - 1 and n == 2)
                        if kt == KT - 1:
                            last.then_inc(o_ready, 1)

                def do(i, b, par, evs, vec):
                    for ev in evs:
                        if ev[0] == "turn":
                            hf, kt = ev[1:]
                            half = i * 2 + (2 + hf)
                            tile = tile_at(i, hf, kt)
                            pe.wait_ge(xn_ready, half + 1)
                            if not (is_int(i, -1) and kt == 0):
                                pe.wait_ge(h_ready, tile - 1)
                            for t in range(HT):
                                last = nc.tensor.transpose(t_ps[:, bank_at(i, hf, kt), t * P:(t + 1) * P],
                                                           normed(i, hf)[:, t, kt * P:(kt + 1) * P], ident[:, :])
                            last.then_inc(turned, 1)
                        elif ev[0] == "shift":
                            pe.wait_ge(mod_step, 1)
                            for c in range(KT // 2):
                                last = nc.tensor.transpose(t_ps[:, 0, c * P:(c + 1) * P],
                                                           o_f[:, 0, c * P:(c + 1) * P], ident[:, :])
                            last.then_inc(mod_step, 1)
                            pe.wait_ge(mod_step, 3)
                        elif ev[0] == "w":
                            if 2 <= ev[1] <= KT + 1:
                                first_groups(ev[1] - 2)
                        elif ev[0] == "group" and is_int(i, 0) and ev[1] < OBANKS:
                            pass
                        elif ev[0] == "group":
                            g = ev[1]
                            if g == 0:
                                pe.wait_ge(h_lo_done, i * (2 * KT) + 2 * KT)
                            if is_int(i, 0) and g == QG:
                                pe.wait_ge(wkv_lo_done, KT)
                            pe.wait_ge(o_taken, i * NG + (g - OBANKS + 1))
                            bank = (par * NG + g) % OBANKS
                            for kt in range(KT):
                                for n, (h, w) in enumerate(((h_hi, w_hi), (h_hi, w_lo), (h_lo, w_hi))):
                                    begin, end = kt == 0 and n == 0, kt == KT - 1 and n == 2
                                    if g < QK:
                                        last = nc.tensor.matmul(o_ps[:, bank, :], w[:, kt, g * P:(g + 1) * P],
                                                                h[:, par, kt, :], start=begin, stop=end)
                                    else:
                                        v = g - QK
                                        last = nc.tensor.matmul(o_ps[:, bank, 0:NKV],
                                                                h[:, par, kt, v * P:(v + 1) * P],
                                                                w[:, kt, D + NKV:NW], start=begin, stop=end)
                            last.then_inc(o_ready, 1)
                        elif ev[0] == "mod":
                            part = ev[1]
                            if part == 0 and not (is_int(vec, 0)):
                                pe.wait_ge(row_ready, vec)
                            for s in range(SLOTS):
                                pe.wait_ge(stage_in[s], vec * 32 + (stage_base[s] + 16 * (part + 1)))
                                for j in range(4):
                                    last = nc.tensor.matmul(m_ps[32 * j:32 * j + 32, 0:HALF],
                                                            c_rep[:, part * SLOTS + s, :],
                                                            stage[:, s, j * HALF:(j + 1) * HALF],
                                                            start=(part == 0 and s == 0),
                                                            stop=(part == 1 and s == SLOTS - 1))
                                last.then_inc(stage_used, 1)

                stage_base = [w_count(W_CHUNKS - SLOTS + slot) for slot in range(SLOTS)]

                do(-1, -1, 1, FIRST, None)
                blocks(pe, do)


def attend(nc, w_o, ident, wo_hi, wo_lo, q_hi_d, q_lo_d, k_hi_d, k_lo_d, v_d, att_d):
    NIT, _, S = q_hi_d.shape
    HD = 32
    REP = P // HD
    KT = w_o.shape[0] // P
    D = w_o.shape[1]
    SCALE = float(HD) ** -0.5
    QW = 512
    NQW = S // QW
    HEADS = REP // NQW
    NPAIR = NIT * REP // HEADS
    NKT = S // P
    STEPS = NKT
    TILES = STEPS * REP
    STACK = 3 * HD
    ROWS = STACK + 3
    QR = 4
    SUMMED = 6
    SUMS = SUMMED - 1
    RAWS = NKT - SUMMED
    LATE_DEN = 3
    DIVIDE = 4
    PIECES = 4
    assert KT == NKT

    LATE = 3
    ring = []
    for jj in range(HEADS):
        for t in range(NKT):
            if t == LATE:
                ring.append(("m", jj - 1))
            ring.append(("s", jj, t))
    NRING = len(ring)
    NS = HEADS * NKT
    assert NRING % 2 == 0
    AHEAD = 8
    order = [(1, e) for e in range(AHEAD, NRING)] + [(2, e) for e in range(AHEAD)]
    per_step = [2, 2, 2, 3, 2, 2, 2, 3]
    PLAN, at = [], 0
    for n in per_step:
        PLAN.append(order[at:at + n])
        at += n
    assert at == NRING
    assert all(ring[e][0] == "s" for step in PLAN for _, e in step[1:])

    def exists(pair, e):
        if isinstance(pair, int):
            if ring[e] == ("m", -1):
                return 1 <= pair <= NPAIR
            return pair < NPAIR
        return True

    def s_index(e):
        return sum(x[0] == "s" for x in ring[:e + 1])

    def below(i, value):
        return isinstance(i, int) and i < value

    with ExitStack() as ctx:
        def sb(name, shape, dt):
            return ctx.enter_context(nc.sbuf_tensor(name, shape, dt))

        def ps(name, shape):
            return ctx.enter_context(nc.psum_tensor(name, shape, F32))

        def sem(name):
            return ctx.enter_context(nc.semaphore(name))

        q_st = sb("q_st", [ROWS, QR, HEADS, S], F32R)
        k_st = sb("k_st", [ROWS, 2, S], F32R)
        v_sb = sb("v_sb", [P, 2, NKT, HD], F32)
        p_t = sb("p_t", [P, NKT, REP, QW], F32)
        p_sum = sb("p_sum", [P, 2, REP, QW], F32)
        ones = sb("ones", [P, HD], F32)
        ident_b = sb("ident_b", [P, P], BF16)
        mx = sb("mx", [P, HEADS, NKT], F32)
        rest1 = sb("rest1", [P, NKT], F32)
        rest2 = sb("rest2", [P, NKT], F32)
        m_parts = sb("m_parts", [P, HEADS, NKT, P], BF16)
        num_sb = sb("num_sb", [P, QW], F32)
        den_t = sb("den_t", [P, QW // 32, 32], F32)
        rden_c = sb("rden_c", [P, QW // 32], F32)
        rden = sb("rden", [P, QW], F32)
        a_sb = sb("a_sb", [P, 2, QW], F32)

        st_ps = ps("st_ps", [P, 2, QW])
        s_ps = ps("s_ps", [P, 2, S])
        num_ps = ps("num_ps", [P, QW])
        den_ps = ps("den_ps", [P, QW])

        q_in = [sem(f"q_in{u}") for u in range(QR)]
        k_in = [sem(f"k_in{u}") for u in range(2)]
        v_in = [sem(f"v_in{u}") for u in range(2)]
        wo_in = [sem(f"wo_in{k}") for k in range(2)]
        wo_hi_done = sem("wo_hi_done")
        wo_lo_done = sem("wo_lo_done")
        consts = sem("consts")
        s_ready = sem("s_ready")
        max_done = sem("max_done")
        m_step = sem("m_step")
        m_made = sem("m_made")
        m_ready = sem("m_ready")
        m_put = sem("m_put")
        st_ready = sem("st_ready")
        exp_done = sem("exp_done")
        num_done = sem("num_done")
        den_done = sem("den_done")
        sum_done = sem("sum_done")
        sum_used = sem("sum_used")
        num_taken = sem("num_taken")
        den_taken = sem("den_taken")
        rden_step = sem("rden_step")
        a_ready = sem("a_ready")
        a_out = [sem(f"a_out{u}") for u in range(2)]

        def pairs(eng, do):
            for pair in range(QR):
                do(pair, pair, pair // 2)
            with eng.Fori(1, NPAIR // QR - 1) as n:
                for slot in range(QR):
                    do(n * QR + slot, slot, n * 2 + slot // 2)
            for pair in range(NPAIR - QR, NPAIR):
                do(pair, pair % QR, pair // 2)

        def start(do):
            for e in range(NRING):
                do(0, 0, e)
            for e in range(AHEAD):
                do(1, 1, e)

        with nc.Block() as block:

            @block.sync
            def _(sp):
                def load_q(pair, slot):
                    for row, src in ((0, q_hi_d), (1, q_lo_d), (2, q_hi_d)):
                        sp.dma_start(q_st[row * HD:(row + 1) * HD, slot, :, :].bitcast(F32),
                                     src.rearrange("i (j d) s -> (i j) d s", d=HD)[bass.ds(pair * HEADS, HEADS)]
                                     .rearrange("j d s -> d j s")).then_inc(q_in[slot], 16)

                def load_k(it, u):
                    for row, src in ((0, k_hi_d), (1, k_hi_d), (2, k_lo_d)):
                        sp.dma_start(k_st[row * HD:(row + 1) * HD, u, :].bitcast(F32), src[bass.ds(it * HD, HD), :])\
                          .then_inc(k_in[u], 16)

                def load_v(it, u):
                    sp.dma_start(v_sb[:, u, :, :], v_d.rearrange("i p t c -> (i p) t c")[bass.ds(it * P, P)])\
                      .then_inc(v_in[u], 16)

                def store(pair, slot):
                    par = slot % 2
                    sp.wait_ge(a_ready, pair + 1)
                    for h in range(NQW):
                        sp.dma_start(att_d.rearrange("i p s -> (i p) s")[bass.ds(pair * (HEADS * HD), HEADS * HD),
                                                                         h * QW:(h + 1) * QW],
                                     a_sb[h * HEADS * HD:(h + 1) * HEADS * HD, par, :]).then_inc(a_out[par], 16)

                load_k(0, 0)
                load_q(0, 0)
                load_q(1, 1)
                for part in range(2):
                    ks = slice(part * KT // 2, (part + 1) * KT // 2)
                    sp.dma_start(p_t[:, ks, 0:D // QW, :],
                                 w_o.rearrange("(k p) (j n) -> p k j n", p=P, n=QW)[:, ks]).then_inc(wo_in[part], 16)
                load_v(0, 0)
                load_q(2, 2)

                def do(pair, slot, it):
                    u = slot // 2
                    if not below(pair, 1):
                        sp.wait_ge(st_ready, pair * TILES)
                    if slot % 2 == 0 and not is_int(it, NIT - 1):
                        load_k(it + 1, 1 - u)
                    if below(pair, NPAIR - QR + 1) or not isinstance(pair, int):
                        load_q(pair + (QR - 1), (slot + QR - 1) % QR)
                    if not below(pair, 1):
                        store(pair - 1, (slot - 1) % QR)
                    if slot % 2 == 1 and not is_int(it, NIT - 1):
                        if not below(pair, 2):
                            sp.wait_ge(num_done, (pair - 1) * STEPS)
                        load_v(it + 1, 1 - u)

                pairs(sp, do)
                store(NPAIR - 1, QR - 1)
                for u in range(2):
                    sp.wait_ge(a_out[u], 16 * NQW * NPAIR // 2)

            @block.gpsimd
            def _(pool):
                nc.gpsimd.memset(ones[:, :], 1.0)
                nc.gpsimd.memset(m_parts[:, :, :, :], 0.0)
                nc.gpsimd.tensor_copy(ident_b[:, :], ident[:, :]).then_inc(consts, 1)
                for k in range(KT):
                    pool.wait_ge(wo_hi_done, k + 1)
                    nc.gpsimd.tensor_tensor(wo_lo[:, k, :], p_t[:, k, 0:D // QW, :].rearrange("p j n -> p (j n)"),
                                            wo_hi[:, k, :].bitcast(F32), ALU.subtract).then_inc(wo_lo_done, 1)

                def do(pair, slot, it):
                    total = p_sum[:, slot % 2, :, :]
                    for kt in range(1, SUMMED):
                        pool.wait_ge(exp_done, pair * TILES + (kt * REP + REP))
                        if kt == 1:
                            if not below(pair, 2):
                                pool.wait_ge(sum_used, pair - 1)
                            before = p_t[:, 0, :, :]
                        else:
                            pool.wait_ge(sum_done, pair * SUMS + (kt - 1))
                            before = total
                        nc.gpsimd.tensor_tensor(total, before, p_t[:, kt, :, :], ALU.add).then_inc(sum_done, 1)

                pairs(pool, do)

            @block.scalar
            def _(act):
                def put(pair, slot, e):
                    if ring[e][0] != "m" or not exists(pair, e):
                        return
                    jj = ring[e][1]
                    if jj < 0:
                        pair, slot, jj = pair - 1, (slot - 1) % QR, HEADS - 1
                    if not below(pair, QR):
                        act.wait_ge(st_ready, (pair - (QR - 1)) * TILES)
                    act.wait_ge(m_ready, pair * HEADS + (jj + 1))
                    nc.scalar.copy(q_st[STACK:ROWS, slot, jj, :], s_ps[STACK:ROWS, e % 2, :]).then_inc(m_put, 1)

                for k in range(KT):
                    act.wait_ge(wo_in[k // (KT // 2)], 16)
                    nc.scalar.copy(wo_hi[:, k, :], p_t[:, k, 0:D // QW, :].rearrange("p j n -> p (j n)"))\
                      .then_inc(wo_hi_done, 1)

                start(put)

                def take_num(pair):
                    act.wait_ge(num_done, pair * STEPS + STEPS)
                    if not below(pair, 1):
                        act.wait_ge(a_ready, pair)
                    nc.scalar.copy(num_sb[:, :], num_ps[:, :]).then_inc(num_taken, 1)

                def do(pair, slot, it):
                    for s in range(STEPS):
                        if s == 1 and not below(pair, 1):
                            take_num(pair - 1)
                        if not below(pair, 1):
                            act.wait_ge(num_done, (pair - 1) * STEPS + (s + 1))
                            if s < SUMMED:
                                act.wait_ge(sum_done, (pair - 1) * SUMS + max(s, 1))
                            else:
                                act.wait_ge(den_done, (pair - 1) * RAWS + (s - SUMMED + 1))
                        else:
                            act.wait_ge(wo_lo_done, s + 1)
                        for c in range(REP):
                            act.wait_ge(st_ready, pair * TILES + (s * REP + c + 1))
                            nc.scalar.activation(p_t[:, s, c, :], st_ps[:, c % 2, :], ACT.Exp, scale=SCALE)\
                              .then_inc(exp_done, 1)
                            if c == 1:
                                ahead, e = PLAN[s][0]
                                put(pair + ahead, (slot + ahead) % QR, e)

                pairs(act, do)
                take_num(NPAIR - 1)

            @block.vector
            def _(dve):
                nc.vector.memset(k_st[STACK:ROWS, :, :].bitcast(F32), 1.0).then_inc(consts, 1)
                dve.wait_ge(consts, 2)

                def entry(pair, slot, e):
                    if ring[e][0] != "s" or not exists(pair, e):
                        return
                    jj, t = ring[e][1:]
                    done = jj * NKT + t + 1
                    dve.wait_ge(s_ready, pair * NS + done)
                    nc.vector.tensor_reduce(mx[:, jj, t:t + 1], s_ps[:, e % 2, :], AX_X, ALU.max)\
                      .then_inc(max_done, 1)
                    if t < NKT - 1:
                        return
                    dve.wait_ge(max_done, pair * NS + done)
                    if not below(pair, 1):
                        dve.wait_ge(m_ready, (pair - 1) * HEADS + (jj + 1))
                    part = [m_parts[:, jj, :, STACK + n] for n in range(3)]
                    base = pair * (4 * HEADS) + 4 * jj
                    nc.vector.tensor_scalar(part[0], mx[:, jj, :], -1.0, None, ALU.mult).then_inc(m_step, 1)
                    dve.wait_ge(m_step, base + 1)
                    nc.vector.scalar_tensor_tensor(rest1[:, :], mx[:, jj, :], -1.0, part[0], ALU.mult,
                                                   ALU.subtract).then_inc(m_step, 1)
                    dve.wait_ge(m_step, base + 2)
                    nc.vector.tensor_copy(part[1], rest1[:, :]).then_inc(m_step, 1)
                    dve.wait_ge(m_step, base + 3)
                    nc.vector.tensor_tensor(rest2[:, :], rest1[:, :], part[1], ALU.subtract).then_inc(m_step, 1)
                    dve.wait_ge(m_step, base + 4)
                    nc.vector.tensor_copy(part[2], rest2[:, :]).then_inc(m_made, 1)

                start(entry)

                def divide(pair, par, piece):
                    if piece == 0:
                        dve.wait_ge(sum_used, pair + 1)
                        nc.vector.transpose(den_t[:, :, :].rearrange("p c r -> p (c r)"), den_ps[:, :])\
                          .then_inc(den_taken, 1)
                    elif piece == 1:
                        dve.wait_ge(den_taken, pair + 1)
                        nc.vector.reciprocal(rden_c[:, :], den_t[:, :, 0]).then_inc(rden_step, 1)
                    elif piece == 2:
                        dve.wait_ge(rden_step, pair * 2 + 1)
                        nc.vector.transpose(rden[:, :], rden_c[:, :].unsqueeze(2).broadcast_to([P, QW // 32, 32]))\
                          .then_inc(rden_step, 1)
                    else:
                        dve.wait_ge(rden_step, pair * 2 + 2)
                        dve.wait_ge(num_taken, pair + 1)
                        if not below(pair, 2):
                            dve.wait_ge(a_out[par], (pair - par) * (8 * NQW))
                        nc.vector.tensor_tensor(a_sb[:, par, :], num_sb[:, :], rden[:, :], ALU.mult)\
                          .then_inc(a_ready, 1)

                def do(pair, slot, it):
                    for s in range(STEPS):
                        if s >= DIVIDE and not below(pair, 1):
                            divide(pair - 1, (slot - 1) % 2, s - DIVIDE)
                        for ahead, e in PLAN[s]:
                            entry(pair + ahead, (slot + ahead) % QR, e)

                pairs(dve, do)
                for piece in range(PIECES):
                    divide(NPAIR - 1, (NPAIR - 1) % 2, piece)

            @block.tensor
            def _(pe):
                pe.wait_ge(consts, 2)

                def entry(pair, slot, e):
                    if not exists(pair, e):
                        return
                    if is_int(pair, NPAIR):
                        pe.wait_ge(max_done, NPAIR * NS)
                    elif e < 2:
                        if not below(pair, 1):
                            pe.wait_ge(max_done, (pair - 1) * NS + s_index(NRING - 2 + e))
                    elif ring[e - 2][0] == "s" or not exists(pair, e - 2):
                        pe.wait_ge(max_done, pair * NS + s_index(e - 2))
                    else:
                        pe.wait_ge(m_put, pair * HEADS + (ring[e - 2][1] + 1))
                    if e == 0:
                        pe.wait_ge(q_in[slot], (pair - slot) * (48 // QR) + 48)
                        if slot % 2 == 0:
                            pe.wait_ge(k_in[slot // 2], (pair - slot) * (48 // QR) + 48)
                    if ring[e][0] == "s":
                        jj, t = ring[e][1:]
                        for n in range(NQW):
                            last = nc.tensor.matmul(s_ps[:, e % 2, n * QW:(n + 1) * QW],
                                                    q_st[0:STACK, slot, jj, t * P:(t + 1) * P],
                                                    k_st[0:STACK, slot // 2, n * QW:(n + 1) * QW],
                                                    start=True, stop=True)
                        last.then_inc(s_ready, 1)
                    else:
                        jj = ring[e][1]
                        pe.wait_ge(m_made, pair * HEADS + (jj + 1))
                        for t in range(NKT):
                            last = nc.tensor.matmul(s_ps[:, e % 2, t * P:(t + 1) * P],
                                                    m_parts[:, jj % HEADS, t, :], ident_b[:, :], start=True, stop=True)
                        last.then_inc(m_ready, 1)

                start(entry)

                def scores(pair, slot, s, c):
                    h, jj = c // HEADS, c % HEADS
                    if not (below(pair, 1) and s == 0 and c < 2):
                        pe.wait_ge(exp_done, pair * TILES + (s * REP + c - 1))
                    if s == 0 and h == 0:
                        pe.wait_ge(m_put, pair * HEADS + (jj + 1))
                    nc.tensor.matmul(st_ps[:, c % 2, :], k_st[:, slot // 2, s * P:(s + 1) * P],
                                     q_st[:, slot, jj, h * QW:(h + 1) * QW], start=True, stop=True)\
                      .then_inc(st_ready, 1)

                def add_num(pair, slot, s):
                    pe.wait_ge(exp_done, pair * TILES + (s * REP + REP))
                    if s == 0:
                        if slot % 2 == 0:
                            pe.wait_ge(v_in[slot // 2], (pair - slot) * (16 // QR) + 16)
                        if not below(pair, 1):
                            pe.wait_ge(num_taken, pair)
                    for c in range(REP):
                        last = nc.tensor.matmul(num_ps[c * HD:(c + 1) * HD, :], v_sb[:, slot // 2, s, :],
                                                p_t[:, s, c, :], start=s == 0, stop=s == NKT - 1)
                    last.then_inc(num_done, 1)

                def add_den(pair, s):
                    if s == SUMMED and not below(pair, 1):
                        pe.wait_ge(den_taken, pair)
                    for c in range(REP):
                        last = nc.tensor.matmul(den_ps[c * HD:(c + 1) * HD, :], ones[:, :], p_t[:, s, c, :],
                                                start=s == SUMMED, stop=False)
                    last.then_inc(den_done, 1)

                def add_sum(pair, par):
                    pe.wait_ge(sum_done, pair * SUMS + SUMS)
                    for c in range(REP):
                        last = nc.tensor.matmul(den_ps[c * HD:(c + 1) * HD, :], ones[:, :], p_sum[:, par, c, :],
                                                start=False, stop=True)
                    last.then_inc(sum_used, 1)

                def do(pair, slot, it):
                    for s in range(STEPS):
                        plan = [(pair + ahead, (slot + ahead) % QR, e) for ahead, e in PLAN[s]]
                        before = (pair, slot, s - 1) if s else (pair - 1, (slot - 1) % QR, STEPS - 1)
                        is_first = below(pair, 1) and s == 0
                        scores(pair, slot, s, 0)
                        entry(*plan[0])
                        scores(pair, slot, s, 1)
                        if not is_first:
                            add_num(*before)
                        scores(pair, slot, s, 2)
                        entry(*plan[1])
                        scores(pair, slot, s, 3)
                        for item in plan[2:]:
                            entry(*item)
                        if not is_first and before[2] >= SUMMED:
                            add_den(before[0], before[2])
                        if s == LATE_DEN and not below(pair, 1):
                            add_sum(pair - 1, (slot - 1) % 2)

                pairs(pe, do)
                add_num(NPAIR - 1, QR - 1, STEPS - 1)
                add_den(NPAIR - 1, STEPS - 1)
                add_sum(NPAIR - 1, 1)


def finish(nc, x, b_o, lora_in, lora_out, earlier_in, ident, wo_hi, wo_lo, att_d, mod_raw_d, mod_gate_d, out):
    NTOK, D = x.shape
    KT = D // P
    NB = mod_raw_d.shape[1]
    G = att_d.shape[0] // NB
    E = 4
    ER = lora_out.shape[0]
    R = ER // E
    LORA_SCALE = 4.0
    NT = NTOK // P
    TPB = NT // NB
    HW = 512
    XR = 4

    with ExitStack() as ctx:
        def sb(name, shape, dt):
            return ctx.enter_context(nc.sbuf_tensor(name, shape, dt))

        def ps(name, shape):
            return ctx.enter_context(nc.psum_tensor(name, shape, F32))

        def sem(name):
            return ctx.enter_context(nc.semaphore(name))

        ga = sb("ga", [P, NB, D], F32)
        up_w = sb("up_w", [2 * ER, D], F32)
        up_hi = sb("up_hi", [2 * ER, NB, D], F32R)
        up_lo = sb("up_lo", [2 * ER, NB, D], F32R)
        up_f = sb("up_f", [2 * ER, D], F32)
        down = sb("down", [P, KT, P], F32)
        mod_rows = sb("mod_rows", [NB * KT, 2, P], F32)
        shift2 = sb("shift2", [P, NB, KT], F32)
        scale2 = sb("scale2", [P, NB, KT], F32)
        earlier = sb("earlier", [P, E, E], F32)
        bo = sb("bo", [P, D], F32)
        eps = sb("eps2", [P, 1], F32)
        a_f = sb("a_f", [P, 2, KT, P], F32)
        a_hi = sb("a_hi", [P, 2, KT, P], F32R)
        a_lo = sb("a_lo", [P, 2, KT, P], F32R)
        x_sb = sb("x_sb", [P, 4, D], F32)
        x1 = sb("x1", [P, XR, D], F32)
        xn = sb("xn2", [P, D], F32)
        h_t = sb("h_t", [P, 2, KT, P], F32)
        stats = sb("stats2", [P, 2, 6], F32)
        mv = sb("mv2", [P, 2], F32)
        std = sb("std2", [P, 1], F32)
        rstd = sb("rstd2", [P, 1], F32)
        mid = sb("mid", [P, ER + E], F32)
        above = sb("above", [P, E, E], F32)
        tied = sb("tied", [P, E, E], F32)
        rank = sb("rank", [P, E], F32)
        top = sb("top", [P, 1], F32)
        low = sb("low", [P, E], F32)
        ex = sb("ex", [P, E], F32)
        wts = sb("wts", [P, E], F32)
        total = sb("total", [P, 1], F32)
        gate = sb("gate", [P, E], F32)
        gmid = sb("gmid", [P, 2, ER], F32)
        gmid_f = sb("gmid_f", [2 * ER, P], F32)
        gmid_t = sb("gmid_t", [2 * ER, 2, P], F32R)

        o_ps = ps("o2_ps", [P, 2, D])
        t_ps = ps("t2_ps", [P, D])
        g_ps = ps("g_ps", [P, 512])
        d_ps = ps("d_ps", [P, HW])
        MID_T = slice(P, 2 * P)

        bo_in = sem("bo_in")
        mod_in = sem("mod_in")
        ga_in = sem("ga_in")
        lora_loaded = sem("lora_loaded")
        LORA_LOADS = 16 * (4 + NB)
        mod_ready = sem("mod_ready")
        up_step = sem("up_step")
        consts = sem("consts2")
        mod_turned = sem("mod_turned")
        a_in = [sem(f"a_in{u}") for u in range(2)]
        x_in = [sem(f"x_in{u}") for u in range(4)]
        a_hi_done = sem("a_hi_done")
        a_lo_done = sem("a_lo_done")
        o_ready = sem("o2_ready")
        o_taken = sem("o2_taken")
        x1_ready = sem("x1_ready")
        ln_step = sem("ln2_step")
        var_done = sem("var_done")
        std_done = sem("std2_done")
        xn_ready = sem("xn2_ready")
        waited = sem("waited2")
        waited_pe = sem("waited_pe")
        turned = sem("turned2")
        h_ready = sem("h2_ready")
        mid_ready = sem("mid_ready")
        r_step = sem("r_step")
        low_ready = sem("low_ready")
        ex_done = sem("ex_done")
        gmid_ready = sem("gmid_ready")
        gmid_turned = sem("gmid_turned")
        gmid_taken = sem("gmid_taken")
        gmid_lo_done = sem("gmid_lo_done")
        d_ready = sem("d_ready")
        y_ready = sem("y_ready")
        y_out = [sem(f"y_out{u}") for u in range(XR)]

        def slots(eng, do):
            for t in range(TPB):
                do(t, 0, t)
            with eng.Fori(1, NB) as b:
                for t in range(TPB):
                    do(b * TPB + t, b, t)
            for t in range(LAG):
                do(NT + t, NB, t)

        LAG = 4

        def tile_of(slot, b, t, lag):
            if isinstance(slot, int) and not 0 <= slot - lag < NT:
                return None
            return slot - lag, (b if t >= lag else b - 1), (t - lag) % TPB

        def batch(table, b):
            return table[:, bass.ds(b, 1), :].rearrange("p b n -> p (b n)")

        with nc.Block() as block:

            @block.sync
            def _(sp):
                for u in range(XR):
                    sp.sem_inc(y_out[u], 16)
                def tables(slot):
                    if slot == 0:
                        sp.dma_start(bo[:, :], b_o[0, :].partition_broadcast(P)).then_inc(bo_in, 16)
                    if slot == 1:
                        for v in range(2):
                            sp.dma_start(mod_rows[:, v, :], mod_raw_d[1 + v].rearrange("b (k p) -> (b k) p", p=P))\
                              .then_inc(mod_in, 16)
                        for b in range(NB):
                            sp.dma_start(ga[:, b, :], mod_gate_d[0, b, :].partition_broadcast(P)).then_inc(ga_in, 16)
                    if slot == 2:
                        sp.dma_start(down[:, :, :], lora_in).then_inc(lora_loaded, 16)
                        sp.dma_start(earlier[:, :, :], earlier_in).then_inc(lora_loaded, 16)
                        for n in range(2):
                            sp.dma_start(up_w[n * ER:(n + 1) * ER, :], lora_out).then_inc(lora_loaded, 16)
                        for b in range(NB):
                            sp.dma_start(up_hi[:, b, :].bitcast(F32), mod_gate_d[3, b, :].partition_broadcast(2 * ER))\
                              .then_inc(lora_loaded, 16)

                def do(slot, b, t):
                    now = tile_of(slot, b, t, 0)
                    if now:
                        T, b, t = now
                        u = t % 2
                        if not (is_int(T, 0) or is_int(T, 1)):
                            sp.wait_ge(a_lo_done, T - 1)
                        src = att_d.rearrange("i p s -> (i p) s")[bass.ds(b * (G * P), G * P), t * P:(t + 1) * P]
                        sp.dma_start(a_f[:, u, :, :], src.rearrange("(k p) s -> p k s", p=P)).then_inc(a_in[u], 16)
                        if not (isinstance(T, int) and T < 4):
                            sp.wait_ge(x1_ready, T - 3)
                        sp.dma_start(x_sb[:, t % 4, :], x[bass.ds(T * P, P), :]).then_inc(x_in[t % 4], 16)

                def both(slot, b, t):
                    do(slot, b, t)
                    if isinstance(slot, int):
                        tables(slot)
                    old = tile_of(slot, b, t, LAG + 1)
                    if old:
                        store(old)

                def store(old):
                    T, _, t = old
                    sp.wait_ge(y_ready, T * 2 + 2)
                    sp.dma_start(out[bass.ds(T * P, P), :], x1[:, t % XR, :]).then_inc(y_out[t % XR], 16)

                slots(sp, both)
                store((NT - 1, NB - 1, TPB - 1))
                for u in range(XR):
                    sp.wait_ge(y_out[u], 16 * NT // XR + 16)

            @block.gpsimd
            def _(pool):
                def do(slot, b, t):
                    now = tile_of(slot, b, t, 0)
                    if now:
                        T, b, t = now
                        u = t % 2
                        pool.wait_ge(a_hi_done, T + 1)
                        nc.gpsimd.tensor_tensor(a_lo[:, u, :, :], a_f[:, u, :, :], a_hi[:, u, :, :].bitcast(F32),
                                                ALU.subtract).then_inc(a_lo_done, 1)
                    if is_int(slot, 2):
                        pool.wait_ge(lora_loaded, LORA_LOADS)
                        nc.gpsimd.tensor_scalar(up_w[:, :], up_w[:, :], LORA_SCALE, None, ALU.mult)\
                          .then_inc(up_step, 1)
                        pool.wait_ge(up_step, 1)
                        nc.gpsimd.memset(up_lo[ER:2 * ER, :, :].bitcast(F32), 0.0).then_inc(up_step, 1)
                        pool.wait_ge(up_step, 2)
                    if isinstance(slot, int) and 2 <= slot < 2 + NB:
                        bb = slot - 2
                        nc.gpsimd.tensor_tensor(up_f[:, :], up_hi[:, bb, :].bitcast(F32), up_w[:, :], ALU.mult)\
                          .then_inc(up_step, 1)
                        pool.wait_ge(up_step, 3 * bb + 3)
                        nc.gpsimd.tensor_copy(up_hi[:, bb, :], up_f[:, :]).then_inc(up_step, 1)
                        pool.wait_ge(up_step, 3 * bb + 4)
                        nc.gpsimd.tensor_tensor(up_lo[0:ER, bb, :], up_f[0:ER, :], up_hi[0:ER, bb, :].bitcast(F32),
                                                ALU.subtract).then_inc(up_step, 1)
                        pool.wait_ge(up_step, 3 * bb + 5)

                slots(pool, do)

            @block.scalar
            def _(act):
                def do(slot, b, t):
                    now = tile_of(slot, b, t, 0)
                    if now:
                        T, _, tt = now
                        u = tt % 2
                        act.wait_ge(a_in[u], (T - u) * 8 + 16)
                        if not (is_int(T, 0) or is_int(T, 1)):
                            act.wait_ge(o_ready, T * 2 - 2)
                        nc.scalar.copy(a_hi[:, u, :, :], a_f[:, u, :, :]).then_inc(a_hi_done, 1)
                    now = tile_of(slot, b, t, 2)
                    if now:
                        act.wait_ge(var_done, now[0] + 1)
                        nc.scalar.activation(std[:, :], mv[:, 1:2], ACT.Sqrt, bias=eps[:, 0:1]).then_inc(std_done, 1)
                    now = tile_of(slot, b, t, 3)
                    if now:
                        act.wait_ge(low_ready, now[0] + 1)
                        nc.scalar.activation(ex[:, :], low[:, :], ACT.Exp).then_inc(ex_done, 1)
                    now = tile_of(slot, b, t, 2)
                    if now:
                        T, bb, tt = now
                        act.wait_ge(mod_ready, 1)
                        act.wait_ge(turned, T + 1)
                        for kt in range(KT):
                            last = nc.scalar.activation(h_t[:, tt % 2, kt, :], t_ps[:, kt * P:(kt + 1) * P],
                                                        ACT.Identity, bias=batch(shift2, bb)[:, kt:kt + 1],
                                                        scale=batch(scale2, bb)[:, kt:kt + 1])
                        last.then_inc(h_ready, 1)
                    now = tile_of(slot, b, t, 3)
                    if now:
                        T, _, tt = now
                        act.wait_ge(gmid_turned, T + 1)
                        if not is_int(T, 0):
                            act.wait_ge(gmid_lo_done, T)
                        nc.scalar.copy(gmid_t[:, tt % 2, :], g_ps[:, MID_T])
                        nc.scalar.copy(gmid_f[ER:2 * ER, :], g_ps[ER:2 * ER, MID_T]).then_inc(gmid_taken, 1)

                act.wait_ge(consts, 1)
                slots(act, do)

            @block.vector
            def _(dve):
                nc.vector.memset(eps[:, :], EPS).then_inc(consts, 1)
                dve.wait_ge(bo_in, 16)
                dve.wait_ge(mod_turned, 1)
                nc.vector.tensor_copy(shift2[:, :, :].rearrange("p b k -> p (b k)"), t_ps[:, 0:NB * KT])
                nc.vector.tensor_scalar(scale2[:, :, :].rearrange("p b k -> p (b k)"), t_ps[:, P:P + NB * KT],
                                        1.0, None, ALU.add).then_inc(mod_ready, 1)
                dve.wait_ge(ga_in, 16 * NB)

                def do(slot, b, t):
                    now = tile_of(slot, b, t, 2)
                    if now:
                        T, bb, tt = now
                        xs = x1[:, tt % XR, :]
                        if not (isinstance(T, int) and T < XR):
                            dve.wait_ge(y_out[tt % XR], (T - tt % XR) * (16 // XR) + 16)
                        dve.wait_ge(o_ready, T * 2 + 2)
                        nc.vector.tensor_tensor(xs, o_ps[:, tt % 2, :], bo[:, :], ALU.add).then_inc(o_taken, 1)
                        dve.wait_ge(o_taken, T + 1)
                        nc.vector.tensor_tensor(xs, xs, batch(ga, bb), ALU.mult).then_inc(ln_step, 1)
                        dve.wait_ge(ln_step, T * 3 + 1)
                        dve.wait_ge(x_in[tt % 4], (T - tt % 4) * 4 + 16)
                        nc.vector.tensor_tensor(xs, xs, x_sb[:, tt % 4, :], ALU.add).then_inc(x1_ready, 1)
                        dve.wait_ge(x1_ready, T + 1)
                        for c in range(2):
                            last = nc.vector.bn_stats(stats[:, c, :], xs[:, c * HW:(c + 1) * HW])
                        last.then_inc(ln_step, 1)
                        dve.wait_ge(ln_step, T * 3 + 2)
                        dve.sem_inc(waited, 1)
                        nc.vector.bn_aggr(mv[:, :], stats[:, :, :].rearrange("p c s -> p (c s)")).then_inc(var_done, 1)
                        dve.wait_ge(std_done, T + 1)
                        nc.vector.reciprocal(rstd[:, :], std[:, :]).then_inc(ln_step, 1)
                        dve.wait_ge(ln_step, T * 3 + 3)
                        if not is_int(T, 0):
                            dve.wait_ge(turned, T)
                        nc.vector.tensor_scalar(xn[:, :], xs, mv[:, 0:1], rstd[:, :], ALU.subtract, ALU.mult)\
                          .then_inc(xn_ready, 1)
                    late = tile_of(slot, b, t, 5)
                    if late:
                        add(late, 1)
                    last_one = tile_of(slot, b, t, 4)
                    if last_one:
                        T, _, tt = last_one
                        dve.wait_ge(gmid_taken, T + 1)
                        nc.vector.tensor_tensor(gmid_t[ER:2 * ER, tt % 2, :], gmid_f[ER:2 * ER, :],
                                                gmid_t[ER:2 * ER, tt % 2, :].bitcast(F32), ALU.subtract)\
                          .then_inc(gmid_lo_done, 1)
                    mids = tile_of(slot, b, t, 3)
                    if mids:
                        T = mids[0]
                        at = [0]
                        if is_int(T, 0):
                            dve.wait_ge(lora_loaded, LORA_LOADS)

                        def step(ins):
                            at[0] += 1
                            ins.then_inc(r_step, 1)
                            dve.wait_ge(r_step, T * STEPS + at[0])

                        STEPS = 9
                        dve.wait_ge(mid_ready, T + 1)
                        step(nc.vector.tensor_copy(mid[:, :], g_ps[:, 0:ER + E]))
                        logit = mid[:, ER:ER + E]
                        rows = logit.unsqueeze(2).broadcast_to([P, E, E])
                        cols = logit.unsqueeze(1).broadcast_to([P, E, E])
                        nc.vector.tensor_tensor(above[:, :, :], cols, rows, ALU.is_gt)
                        nc.vector.tensor_tensor(tied[:, :, :], cols, rows, ALU.is_equal)
                        step(nc.vector.tensor_reduce(top[:, :], logit, AX_X, ALU.max))
                        nc.vector.tensor_scalar(low[:, :], logit, top[:, 0:1], None, ALU.subtract).then_inc(low_ready, 1)
                        step(nc.vector.tensor_tensor(tied[:, :, :], tied[:, :, :], earlier[:, :, :], ALU.mult))
                        step(nc.vector.tensor_tensor(above[:, :, :], above[:, :, :], tied[:, :, :], ALU.add))
                        step(nc.vector.tensor_reduce(rank[:, :], above[:, :, :], AX_X, ALU.add))
                    now = tile_of(slot, b, t, 4)
                    if now:
                        add(now, 0)
                    if mids:
                        dve.wait_ge(ex_done, T + 1)
                        step(nc.vector.scalar_tensor_tensor(wts[:, :], rank[:, :], 2.0, ex[:, :], ALU.is_lt, ALU.mult))
                        step(nc.vector.reduce_sum(total[:, :], wts[:, :], AX_X))
                        step(nc.vector.reciprocal(top[:, :], total[:, :]))
                        step(nc.vector.tensor_scalar(gate[:, :], wts[:, :], top[:, 0:1], None, ALU.mult))
                        assert at[0] == STEPS
                        if not is_int(T, 0):
                            dve.wait_ge(gmid_turned, T)
                        for n in range(2):
                            last = nc.vector.tensor_tensor(gmid[:, n, :].rearrange("p (e r) -> p e r", e=E),
                                                           mid[:, 0:ER].rearrange("p (e r) -> p e r", e=E),
                                                           gate[:, :].unsqueeze(2).broadcast_to([P, E, R]), ALU.mult)
                        last.then_inc(gmid_ready, 1)

                def add(now, half):
                    T, _, tt = now
                    cols = slice(half * HW, (half + 1) * HW)
                    dve.wait_ge(d_ready, T * 2 + (half + 1))
                    nc.vector.tensor_tensor(x1[:, tt % XR, cols], d_ps[:, :], x1[:, tt % XR, cols], ALU.add)\
                      .then_inc(y_ready, 1)

                slots(dve, do)
                add((NT - 1, NB - 1, TPB - 1), 1)

            @block.tensor
            def _(pe):
                def project_half(now, half):
                    T, _, tt = now
                    cols = slice(half * HW, (half + 1) * HW)
                    u = tt % 2
                    if half == 0:
                        pe.wait_ge(a_lo_done, T + 1)
                        if not (is_int(T, 0) or is_int(T, 1)):
                            pe.wait_ge(o_taken, T - 1)
                    for k in range(KT):
                        for n, (a, w) in enumerate(((a_hi, wo_hi), (a_hi, wo_lo), (a_lo, wo_hi))):
                            last = nc.tensor.matmul(o_ps[:, u, cols], a[:, u, k, :], w[:, k, cols],
                                                    start=(k == 0 and n == 0), stop=(k == KT - 1 and n == 2))
                    last.then_inc(o_ready, 1)

                def experts_half(now, half):
                    T, bb, tt = now
                    if half == 0:
                        if is_int(T, 0):
                            pe.wait_ge(up_step, 5)
                        if is_int(tt, TPB - 1) and isinstance(T, int):
                            pe.wait_ge(up_step, 3 * NB + 2)
                        pe.wait_ge(gmid_lo_done, T + 1)
                    if not (is_int(T, 0) and half == 0):
                        pe.wait_ge(y_ready, T * 2 + half)
                    pe.sem_inc(waited_pe, 1)
                    for n, table in enumerate((up_hi, up_lo)):
                        last = nc.tensor.matmul(d_ps[:, :], gmid_t[:, tt % 2, :],
                                                batch(table, bb)[:, half * HW:(half + 1) * HW],
                                                start=n == 0, stop=n == 1)
                    last.then_inc(d_ready, 1)

                def do(slot, b, t):
                    proj, turn, mids, add = (tile_of(slot, b, t, lag) for lag in (1, 2, 3, 4))
                    if proj:
                        project_half(proj, 0)
                        if is_int(proj[0], 0):
                            pe.wait_ge(mod_in, 32)
                            for v in range(2):
                                last = nc.tensor.transpose(t_ps[:, v * P:v * P + NB * KT], mod_rows[:, v, :],
                                                           ident[0:NB * KT, 0:NB * KT])
                            last.then_inc(mod_turned, 1)
                    if mids:
                        T, _, tt = mids
                        if is_int(T, 0):
                            pe.wait_ge(lora_loaded, LORA_LOADS)
                        pe.wait_ge(h_ready, T + 1)
                        if not is_int(T, 0):
                            pe.wait_ge(gmid_taken, T)
                        for k in range(KT):
                            last = nc.tensor.matmul(g_ps[:, 0:P], h_t[:, tt % 2, k, :], down[:, k, :],
                                                    start=k == 0, stop=k == KT - 1)
                        last.then_inc(mid_ready, 1)
                    if add:
                        experts_half(add, 0)
                    if proj:
                        project_half(proj, 1)
                    if turn:
                        T = turn[0]
                        if is_int(T, 0):
                            pe.wait_ge(mod_ready, 1)
                        pe.wait_ge(xn_ready, T + 1)
                        if not is_int(T, 0):
                            pe.wait_ge(h_ready, T)
                        for k in range(KT):
                            last = nc.tensor.transpose(t_ps[:, k * P:(k + 1) * P], xn[:, k * P:(k + 1) * P], ident[:, :])
                        last.then_inc(turned, 1)
                    if mids:
                        T = mids[0]
                        pe.wait_ge(mod_ready, 1)
                        pe.wait_ge(gmid_ready, T + 1)
                        nc.tensor.transpose(g_ps[:, MID_T], gmid[:, :, :].rearrange("p n r -> p (n r)"), ident[:, :])\
                          .then_inc(gmid_turned, 1)
                    if add:
                        experts_half(add, 1)

                slots(pe, do)


def kernel(L0_attn_x, L0_attn_wq_w, L0_attn_wq_b, L0_attn_wk_w, L0_attn_wk_b, L0_attn_wv_w, L0_attn_wv_b,
           L0_attn_wo_w, L0_attn_wo_b, L0_ffn_router_w, L0_ffn_A, L0_ffn_B, L0_c, L0_wmod):
    import numpy as np
    import concourse.bacc as bacc
    from concourse.bass_utils import run_bass_kernel_spmd

    def tiles(a):
        return np.ascontiguousarray(a.reshape(-1, P, a.shape[-1]).transpose(1, 0, 2))

    x = np.asarray(L0_attn_x)
    bsz, s, d = x.shape
    lora_a, router, lora_b = np.asarray(L0_ffn_A), np.asarray(L0_ffn_router_w), np.asarray(L0_ffn_B)
    e, r, _ = lora_a.shape
    down = np.zeros((d, P), np.float32)
    down[:, :e * r] = lora_a.reshape(e * r, d).T
    down[:, e * r:e * r + e] = router.T
    arrays = {
        "x": np.ascontiguousarray(x.reshape(bsz * s, d)),
        "w_q": np.asarray(L0_attn_wq_w), "w_k": np.asarray(L0_attn_wk_w), "w_v": np.asarray(L0_attn_wv_w),
        "w_o": np.asarray(L0_attn_wo_w),
        "b_q": np.ascontiguousarray(np.asarray(L0_attn_wq_b).reshape(-1, P).T),
        "b_k": np.ascontiguousarray(np.asarray(L0_attn_wk_b).reshape(-1, P).T),
        "b_v": np.asarray(L0_attn_wv_b),
        "b_o": np.asarray(L0_attn_wo_b).reshape(1, d),
        "lora_in": tiles(down),
        "lora_out": np.ascontiguousarray(lora_b.transpose(0, 2, 1).reshape(e * r, d)),
        "c_t": tiles(np.asarray(L0_c).T),
        "w_mod": np.asarray(L0_wmod),
        "ident_in": np.eye(P, dtype=np.float32),
        "earlier_in": np.ascontiguousarray(np.broadcast_to(np.tril(np.ones((e, e), np.float32), -1), (P, e, e))),
    }
    nc = bacc.Bacc("TRN2", target_bir_lowering=False, num_devices=1)
    args = {n: nc.dram_tensor(n, a.shape, mybir.dt.from_np(a.dtype), kind="ExternalInput").ap()
            for n, a in arrays.items()}
    out = nc.dram_tensor("out", (bsz * s, d), F32, kind="ExternalOutput").ap()
    adaln_block(nc, **args, out=out)
    r = run_bass_kernel_spmd(nc, [arrays], core_ids=[0])
    return r.results[0]["out"].reshape(bsz, s, d)
```
